# Optimizing a Trainium2 kernel written in Bass

```python
import numpy as np
import jax
import jax.numpy as jnp

def _softmax(x, axis=-1):
    return jax.nn.softmax(x, axis=axis)

def _gelu(x):
    return jax.nn.gelu(x, approximate=True)

def _silu(x):
    return jax.nn.silu(x)

def _sigmoid(x):
    return jax.nn.sigmoid(x)

def _layernorm(x, axis=-1, eps=1e-05):
    m = jnp.mean(x, axis=axis, keepdims=True)
    v = jnp.var(x, axis=axis, keepdims=True)
    return (x - m) / jnp.sqrt(v + eps)

def _scatter_add(tgt, idx, src, axis=0):
    return tgt.at[idx].add(src)

def _segment_sum(src, seg, n):
    return jax.ops.segment_sum(src, seg, n)
kernel_name = 'mk_decoder_postln_d2_seqx_r4_80f0f3'

def setup_inputs(seed: int=0):
    np.random.seed(seed)
    _w = jnp.asarray

    def _rec_inputs():
        import jax
        import jax.numpy as jnp
        _rk = jax.random.key(seed)
        x = -0.0002928 + 1 * jax.random.normal(jax.random.fold_in(_rk, 1), (8, 512, 256), jnp.float32)
        _lenS = 512 - jax.random.randint(jax.random.fold_in(_rk, 7), (8,), 0, max(1, 512 // 4) + 1, jnp.int32)
        _lenS2 = 1601 - jax.random.randint(jax.random.fold_in(_rk, 8), (8,), 0, max(1, 1601 // 4) + 1, jnp.int32)
        _ctx_1024P = jax.random.normal(jax.random.fold_in(_rk, 11), (8, 16, 256), jnp.float32)
        _ctx_1024c = jax.random.dirichlet(jax.random.fold_in(_rk, 511), 0.3 * jnp.ones((16,), jnp.float32), (8, 1601))
        _ctx_1024t = jnp.einsum('bsk,bkd->bsd', _ctx_1024c, _ctx_1024P)
        _ctx_1024t = _ctx_1024t * jax.lax.rsqrt(jnp.mean(jnp.square(_ctx_1024t)) + 1e-12) * 0.953939
        ctx_1024 = -1.39393e-06 + 0.999914 * (_ctx_1024t + 0.3 * jax.random.normal(jax.random.fold_in(_rk, 611), (8, 1601, 256), jnp.float32))
        return (x, ctx_1024)
    x, ctx_1024 = _rec_inputs()

    def _L0_attn_setup():
        import jax, jax.numpy as jnp
        import numpy as np
        N_HEADS = 16
        WINDOW = 64
        key = jax.random.key(seed)
        ks = jax.random.split(key, 6)
        B, S, D = (2, 512, 256)
        x = jax.random.normal(ks[0], (B, S, D), dtype=jnp.float32)
        scale = 1.0 / np.sqrt(D)
        Wq = jax.random.normal(ks[1], (D, D), dtype=jnp.float32) * scale
        Wk = jax.random.normal(ks[2], (D, D), dtype=jnp.float32) * scale
        Wv = jax.random.normal(ks[3], (D, D), dtype=jnp.float32) * scale
        Wo = jax.random.normal(ks[4], (D, D), dtype=jnp.float32) * scale
        slopes = jnp.asarray(2.0 ** (-8.0 * (np.arange(1, N_HEADS + 1) / N_HEADS)), dtype=jnp.float32)
        return {'x': x, 'Wq': Wq, 'Wk': Wk, 'Wv': Wv, 'Wo': Wo, 'slopes': slopes}
    _L0_attn_all = _L0_attn_setup()
    _L0_attn_in = {k: v for k, v in _L0_attn_all.items() if k in ('Wq', 'Wk', 'Wv', 'Wo', 'slopes')}
    del _L0_attn_all

    def _L0_xattn_setup():
        import jax, jax.numpy as jnp
        import numpy as np
        D_MODEL = 256
        NUM_HEADS = 16
        D_K = D_MODEL // NUM_HEADS
        key = jax.random.key(seed)
        ks = jax.random.split(key, 11)
        B, S = (2, 512)
        s = 1.0 / np.sqrt(D_MODEL)
        inp = {'q': jax.random.normal(ks[0], (B, S, D_MODEL), jnp.float32), 'k': jax.random.normal(ks[1], (B, S, D_MODEL), jnp.float32), 'v': jax.random.normal(ks[2], (B, S, D_MODEL), jnp.float32), 'Wq': jax.random.normal(ks[3], (D_MODEL, D_MODEL), jnp.float32) * s, 'bq': jax.random.normal(ks[4], (D_MODEL,), jnp.float32) * 0.01, 'Wk': jax.random.normal(ks[5], (D_MODEL, D_MODEL), jnp.float32) * s, 'bk': jax.random.normal(ks[6], (D_MODEL,), jnp.float32) * 0.01, 'Wv': jax.random.normal(ks[7], (D_MODEL, D_MODEL), jnp.float32) * s, 'bv': jax.random.normal(ks[8], (D_MODEL,), jnp.float32) * 0.01, 'Wo': jax.random.normal(ks[9], (D_MODEL, D_MODEL), jnp.float32) * s, 'bo': jax.random.normal(ks[10], (D_MODEL,), jnp.float32) * 0.01}
        return inp
    _L0_xattn_all = _L0_xattn_setup()
    _L0_xattn_in = {k: v for k, v in _L0_xattn_all.items() if k in ('Wq', 'bq', 'Wk', 'bk', 'Wv', 'bv', 'Wo', 'bo')}
    del _L0_xattn_all

    def _L0_ffn_setup():
        import jax, jax.numpy as jnp
        import numpy as np
        DIM = 256
        HID = 512
        OUT = 256
        NE = 8
        TOPK = 2

        def _xavier(key, shape):
            fan_in, fan_out = (shape[-2], shape[-1])
            lim = jnp.sqrt(6.0 / (fan_in + fan_out))
            return jax.random.uniform(key, shape, jnp.float32, -lim, lim)
        key = jax.random.key(seed)
        ks = jax.random.split(key, 8)
        X = jax.random.normal(ks[0], (4, 256, DIM), jnp.float32)
        W1 = _xavier(ks[1], (NE, DIM, HID))
        W3 = _xavier(ks[2], (NE, DIM, HID))
        W2 = _xavier(ks[3], (NE, HID, OUT))
        b1 = jnp.zeros((NE, HID), jnp.float32)
        b3 = jnp.zeros((NE, HID), jnp.float32)
        b2 = jnp.zeros((NE, OUT), jnp.float32)
        Wg = _xavier(ks[4], (DIM, NE))
        bg = jnp.zeros((NE,), jnp.float32)
        Wf = _xavier(ks[5], (OUT, OUT))
        bf = jnp.zeros((OUT,), jnp.float32)
        return {'X': X, 'W1': W1, 'b1': b1, 'W3': W3, 'b3': b3, 'W2': W2, 'b2': b2, 'Wg': Wg, 'bg': bg, 'Wf': Wf, 'bf': bf}
    _L0_ffn_all = _L0_ffn_setup()
    _L0_ffn_in = {k: v for k, v in _L0_ffn_all.items() if k in ('W1', 'b1', 'W3', 'b3', 'W2', 'b2', 'Wg', 'bg', 'Wf', 'bf')}
    del _L0_ffn_all

    def _L1_attn_setup():
        import jax, jax.numpy as jnp
        import numpy as np
        DIM = 256
        N_QUAT = DIM // 4
        LN_EPS = 1e-05
        NORM_EPS = 1e-12

        def quat_mul(q1, q2):
            r1, i1, j1, k1 = (q1[..., 0], q1[..., 1], q1[..., 2], q1[..., 3])
            r2, i2, j2, k2 = (q2[..., 0], q2[..., 1], q2[..., 2], q2[..., 3])
            r = r1 * r2 - i1 * i2 - j1 * j2 - k1 * k2
            i = r1 * i2 + i1 * r2 + j1 * k2 - k1 * j2
            j = r1 * j2 - i1 * k2 + j1 * r2 + k1 * i2
            k = r1 * k2 + i1 * j2 - j1 * i2 + k1 * r2
            return jnp.stack([r, i, j, k], axis=-1)

        def quat_conj(q):
            return q * jnp.array([1.0, -1.0, -1.0, -1.0], dtype=q.dtype)
        key = jax.random.key(seed)
        ks = jax.random.split(key, 7)
        B, L, D = (4, 1024, DIM)
        s = 1.0 / np.sqrt(D)
        return {'x': jax.random.normal(ks[0], (B, L, D), dtype=jnp.float32), 'Wk': jax.random.normal(ks[1], (D, D), dtype=jnp.float32) * s, 'bk': jnp.zeros((D,), dtype=jnp.float32), 'Wv': jax.random.normal(ks[2], (D, D), dtype=jnp.float32) * s, 'bv': jnp.zeros((D,), dtype=jnp.float32), 'ln_g': jnp.ones((D,), dtype=jnp.float32), 'ln_b': jnp.zeros((D,), dtype=jnp.float32), 'Wo': jax.random.normal(ks[3], (D, D), dtype=jnp.float32) * s, 'bo': jnp.zeros((D,), dtype=jnp.float32)}
    _L1_attn_all = _L1_attn_setup()
    _L1_attn_in = {k: v for k, v in _L1_attn_all.items() if k in ('Wk', 'bk', 'Wv', 'bv', 'ln_g', 'ln_b', 'Wo', 'bo')}
    del _L1_attn_all

    def _L1_xattn_setup():
        import jax, jax.numpy as jnp
        import numpy as np
        D_MODEL = 256
        B, S = (4, 512)
        key = jax.random.key(seed)
        ks = jax.random.split(key, 10)
        s = 1.0 / np.sqrt(D_MODEL)
        return {'k': jax.random.normal(ks[0], (B, S, D_MODEL), jnp.float32), 'v': jax.random.normal(ks[1], (B, S, D_MODEL), jnp.float32), 'q': jax.random.normal(ks[2], (B, S, D_MODEL), jnp.float32), 'Wk': jax.random.normal(ks[3], (D_MODEL, D_MODEL), jnp.float32) * s, 'Wv': jax.random.normal(ks[4], (D_MODEL, D_MODEL), jnp.float32) * s, 'bv': jnp.zeros((D_MODEL,), jnp.float32), 'Wq': jax.random.normal(ks[5], (D_MODEL, D_MODEL), jnp.float32) * s, 'bq': jnp.zeros((D_MODEL,), jnp.float32), 'Wo': jax.random.normal(ks[6], (D_MODEL, D_MODEL), jnp.float32) * s, 'bo': jnp.zeros((D_MODEL,), jnp.float32)}
    _L1_xattn_all = _L1_xattn_setup()
    _L1_xattn_in = {k: v for k, v in _L1_xattn_all.items() if k in ('Wk', 'Wv', 'bv', 'Wq', 'bq', 'Wo', 'bo')}
    del _L1_xattn_all

    def _L1_ffn_setup():
        import jax, jax.numpy as jnp
        import numpy as np
        QMAX = 127.0

        def _ste_round(v):
            return v + jax.lax.stop_gradient(jnp.round(v) - v)

        def _act_fake_quant(x, clip_factor):
            scale = jax.nn.sigmoid(clip_factor) * jnp.max(jnp.abs(x)) / QMAX
            return jnp.clip(_ste_round(x / scale), -QMAX - 1.0, QMAX) * scale

        def _weight_fake_quant(w):
            scale = jnp.max(jnp.abs(w), axis=1, keepdims=True) / QMAX
            return jnp.clip(_ste_round(w / scale), -QMAX - 1.0, QMAX) * scale
        key = jax.random.key(seed)
        k1, k2, k3, k4 = jax.random.split(key, 4)
        B, S, H, I = (8, 2048, 256, 704)
        return {'x': jax.random.normal(k1, (B, S, H), dtype=jnp.float32), 'clip_x': jnp.full((1,), 4.0, dtype=jnp.float32), 'clip_down': jnp.full((1,), 4.0, dtype=jnp.float32), 'w_gate': jax.random.normal(k2, (I, H), dtype=jnp.float32) * 0.02, 'w_up': jax.random.normal(k3, (I, H), dtype=jnp.float32) * 0.02, 'w_down': jax.random.normal(k4, (H, I), dtype=jnp.float32) * 0.02}
    _L1_ffn_all = _L1_ffn_setup()
    _L1_ffn_in = {k: v for k, v in _L1_ffn_all.items() if k in ('clip_x', 'clip_down', 'w_gate', 'w_up', 'w_down')}
    del _L1_ffn_all
    return {'x': x, 'ctx_1024': ctx_1024, 'L0_attn_Wq': _L0_attn_in['Wq'], 'L0_attn_Wk': _L0_attn_in['Wk'], 'L0_attn_Wv': _L0_attn_in['Wv'], 'L0_attn_Wo': _L0_attn_in['Wo'], 'L0_attn_slopes': _L0_attn_in['slopes'], 'L0_xattn_Wq': _L0_xattn_in['Wq'], 'L0_xattn_bq': _L0_xattn_in['bq'], 'L0_xattn_Wk': _L0_xattn_in['Wk'], 'L0_xattn_bk': _L0_xattn_in['bk'], 'L0_xattn_Wv': _L0_xattn_in['Wv'], 'L0_xattn_bv': _L0_xattn_in['bv'], 'L0_xattn_Wo': _L0_xattn_in['Wo'], 'L0_xattn_bo': _L0_xattn_in['bo'], 'L0_ffn_W1': _L0_ffn_in['W1'], 'L0_ffn_b1': _L0_ffn_in['b1'], 'L0_ffn_W3': _L0_ffn_in['W3'], 'L0_ffn_b3': _L0_ffn_in['b3'], 'L0_ffn_W2': _L0_ffn_in['W2'], 'L0_ffn_b2': _L0_ffn_in['b2'], 'L0_ffn_Wg': _L0_ffn_in['Wg'], 'L0_ffn_bg': _L0_ffn_in['bg'], 'L0_ffn_Wf': _L0_ffn_in['Wf'], 'L0_ffn_bf': _L0_ffn_in['bf'], 'L1_attn_Wk': _L1_attn_in['Wk'], 'L1_attn_bk': _L1_attn_in['bk'], 'L1_attn_Wv': _L1_attn_in['Wv'], 'L1_attn_bv': _L1_attn_in['bv'], 'L1_attn_ln_g': _L1_attn_in['ln_g'], 'L1_attn_ln_b': _L1_attn_in['ln_b'], 'L1_attn_Wo': _L1_attn_in['Wo'], 'L1_attn_bo': _L1_attn_in['bo'], 'L1_xattn_Wk': _L1_xattn_in['Wk'], 'L1_xattn_Wv': _L1_xattn_in['Wv'], 'L1_xattn_bv': _L1_xattn_in['bv'], 'L1_xattn_Wq': _L1_xattn_in['Wq'], 'L1_xattn_bq': _L1_xattn_in['bq'], 'L1_xattn_Wo': _L1_xattn_in['Wo'], 'L1_xattn_bo': _L1_xattn_in['bo'], 'L1_ffn_clip_x': _L1_ffn_in['clip_x'], 'L1_ffn_clip_down': _L1_ffn_in['clip_down'], 'L1_ffn_w_gate': _L1_ffn_in['w_gate'], 'L1_ffn_w_up': _L1_ffn_in['w_up'], 'L1_ffn_w_down': _L1_ffn_in['w_down']}

def reference(x, ctx_1024, L0_attn_Wq, L0_attn_Wk, L0_attn_Wv, L0_attn_Wo, L0_attn_slopes, L0_xattn_Wq, L0_xattn_bq, L0_xattn_Wk, L0_xattn_bk, L0_xattn_Wv, L0_xattn_bv, L0_xattn_Wo, L0_xattn_bo, L0_ffn_W1, L0_ffn_b1, L0_ffn_W3, L0_ffn_b3, L0_ffn_W2, L0_ffn_b2, L0_ffn_Wg, L0_ffn_bg, L0_ffn_Wf, L0_ffn_bf, L1_attn_Wk, L1_attn_bk, L1_attn_Wv, L1_attn_bv, L1_attn_ln_g, L1_attn_ln_b, L1_attn_Wo, L1_attn_bo, L1_xattn_Wk, L1_xattn_Wv, L1_xattn_bv, L1_xattn_Wq, L1_xattn_bq, L1_xattn_Wo, L1_xattn_bo, L1_ffn_clip_x, L1_ffn_clip_down, L1_ffn_w_gate, L1_ffn_w_up, L1_ffn_w_down):
    import jax
    import jax.numpy as jnp

    def _L0_attn_ref(x, Wq, Wk, Wv, Wo, slopes):
        import jax, jax.numpy as jnp
        import numpy as np
        N_HEADS = 16
        WINDOW = 64
        B, S, D = x.shape
        H = N_HEADS
        dk = D // H
        q = jnp.einsum('bsd,od->bso', x, Wq).reshape(B, S, H, dk)
        k = jnp.einsum('bsd,od->bso', x, Wk).reshape(B, S, H, dk)
        v = jnp.einsum('bsd,od->bso', x, Wv).reshape(B, S, H, dk)
        scores = jnp.einsum('bqhd,bkhd->bhqk', q, k) / jnp.sqrt(jnp.asarray(dk, x.dtype))
        pos = jnp.arange(S)
        rel = (pos[:, None] - pos[None, :]).astype(x.dtype)
        scores = scores + slopes[None, :, None, None] * rel[None, None]
        window_mask = jnp.abs(pos[:, None] - pos[None, :]) <= WINDOW // 2
        scores = jnp.where(window_mask[None, None], scores, -jnp.inf)
        attn = jax.nn.softmax(scores, axis=-1)
        out = jnp.einsum('bhqk,bkhd->bqhd', attn, v).reshape(B, S, D)
        return jnp.einsum('bsd,od->bso', out, Wo)

    def _L0_xattn_ref(q, k, v, Wq, bq, Wk, bk, Wv, bv, Wo, bo):
        import jax, jax.numpy as jnp
        import numpy as np
        D_MODEL = 256
        NUM_HEADS = 16
        D_K = D_MODEL // NUM_HEADS
        B, S, _ = q.shape

        def heads(x, W, b):
            y = x @ W.T + b
            return y.reshape(B, -1, NUM_HEADS, D_K).transpose(0, 2, 1, 3)
        qh = heads(q, Wq, bq)
        kh = heads(k, Wk, bk)
        vh = heads(v, Wv, bv)
        scores = jnp.einsum('bhqd,bhkd->bhqk', qh, kh) / jnp.sqrt(jnp.float32(D_K))
        attn = jax.nn.softmax(scores, axis=-1)
        out = jnp.einsum('bhqk,bhkd->bhqd', attn, vh)
        out = out.transpose(0, 2, 1, 3).reshape(B, S, D_MODEL)
        return out @ Wo.T + bo

    def _L0_ffn_ref(X, W1, b1, W3, b3, W2, b2, Wg, bg, Wf, bf):
        import jax, jax.numpy as jnp
        import numpy as np
        DIM = 256
        HID = 512
        OUT = 256
        NE = 8
        TOPK = 2

        def _xavier(key, shape):
            fan_in, fan_out = (shape[-2], shape[-1])
            lim = jnp.sqrt(6.0 / (fan_in + fan_out))
            return jax.random.uniform(key, shape, jnp.float32, -lim, lim)
        gating = jax.nn.softmax(X @ Wg + bg, axis=-1)
        top_k_indices = jnp.argsort(gating, axis=-1)[..., -TOPK:]
        h1 = jnp.einsum('bsd,edh->bseh', X, W1) + b1
        h3 = jnp.einsum('bsd,edh->bseh', X, W3) + b3
        h = jax.nn.silu(h1 * h3)
        expert_outputs = jnp.einsum('bseh,eho->bseo', h, W2) + b2
        topk_out = jnp.take_along_axis(expert_outputs, top_k_indices[..., None], axis=2)
        topk_w = jnp.take_along_axis(gating, top_k_indices, axis=-1)
        mixed = jnp.sum(topk_w[..., None] * topk_out, axis=2)
        return mixed @ Wf + bf

    def _L1_attn_ref(x, Wk, bk, Wv, bv, ln_g, ln_b, Wo, bo):
        import jax, jax.numpy as jnp
        import numpy as np
        DIM = 256
        N_QUAT = DIM // 4
        LN_EPS = 1e-05
        NORM_EPS = 1e-12

        def quat_mul(q1, q2):
            r1, i1, j1, k1 = (q1[..., 0], q1[..., 1], q1[..., 2], q1[..., 3])
            r2, i2, j2, k2 = (q2[..., 0], q2[..., 1], q2[..., 2], q2[..., 3])
            r = r1 * r2 - i1 * i2 - j1 * j2 - k1 * k2
            i = r1 * i2 + i1 * r2 + j1 * k2 - k1 * j2
            j = r1 * j2 - i1 * k2 + j1 * r2 + k1 * i2
            k = r1 * k2 + i1 * j2 - j1 * i2 + k1 * r2
            return jnp.stack([r, i, j, k], axis=-1)

        def quat_conj(q):
            return q * jnp.array([1.0, -1.0, -1.0, -1.0], dtype=q.dtype)
        B, L, D = x.shape
        keys = (x @ Wk.T + bk).reshape(B, L, N_QUAT, 4)
        knorm = jnp.linalg.norm(keys, axis=-1, keepdims=True)
        keys = keys / jnp.maximum(knorm, NORM_EPS)
        values = (x @ Wv.T + bv).reshape(B, L, N_QUAT, 4)
        bound = quat_mul(values, keys)
        memory = jnp.cumsum(bound, axis=1)
        retrieved = quat_mul(memory, quat_conj(keys)).reshape(B, L, D)
        positions = jnp.arange(1, L + 1, dtype=x.dtype)
        retrieved = retrieved / jnp.sqrt(positions)[None, :, None]
        mu = jnp.mean(retrieved, axis=-1, keepdims=True)
        var = jnp.var(retrieved, axis=-1, keepdims=True)
        normed = (retrieved - mu) / jnp.sqrt(var + LN_EPS) * ln_g + ln_b
        return x + (normed @ Wo.T + bo)

    def _L1_xattn_ref(k, v, q, Wk, Wv, bv, Wq, bq, Wo, bo):
        import jax, jax.numpy as jnp
        import numpy as np
        D_MODEL = 256
        B, S = (4, 512)
        kp = jnp.einsum('bsd,ed->bse', k, Wk)
        vp = jnp.einsum('bsd,ed->bse', v, Wv) + bv
        qp = jnp.einsum('bsd,ed->bse', q, Wq) + bq
        scale = 1.0 / jnp.sqrt(jnp.float32(kp.shape[-1]))
        scores = jnp.einsum('bqd,bkd->bqk', qp, kp) * scale
        probs = jax.nn.softmax(scores, axis=-1)
        ctx = jnp.einsum('bqk,bkd->bqd', probs, vp)
        return jnp.einsum('bqd,ed->bqe', ctx, Wo) + bo

    def _L1_ffn_ref(x, clip_x, clip_down, w_gate, w_up, w_down):
        import jax, jax.numpy as jnp
        import numpy as np
        QMAX = 127.0

        def _ste_round(v):
            return v + jax.lax.stop_gradient(jnp.round(v) - v)

        def _act_fake_quant(x, clip_factor):
            scale = jax.nn.sigmoid(clip_factor) * jnp.max(jnp.abs(x)) / QMAX
            return jnp.clip(_ste_round(x / scale), -QMAX - 1.0, QMAX) * scale

        def _weight_fake_quant(w):
            scale = jnp.max(jnp.abs(w), axis=1, keepdims=True) / QMAX
            return jnp.clip(_ste_round(w / scale), -QMAX - 1.0, QMAX) * scale
        xq = _act_fake_quant(x, clip_x[0])
        gate = jnp.einsum('bsh,ih->bsi', xq, _weight_fake_quant(w_gate))
        up = jnp.einsum('bsh,ih->bsi', xq, _weight_fake_quant(w_up))
        h = _act_fake_quant(jax.nn.silu(gate) * up, clip_down[0])
        return jnp.einsum('bsi,hi->bsh', h, _weight_fake_quant(w_down))
    x = _layernorm(x + _L0_attn_ref(x, L0_attn_Wq, L0_attn_Wk, L0_attn_Wv, L0_attn_Wo, L0_attn_slopes), axis=-1)
    x = _layernorm(x + _L0_xattn_ref(x, ctx_1024, ctx_1024, L0_xattn_Wq, L0_xattn_bq, L0_xattn_Wk, L0_xattn_bk, L0_xattn_Wv, L0_xattn_bv, L0_xattn_Wo, L0_xattn_bo), axis=-1)
    x = _layernorm(x + _L0_ffn_ref(x, L0_ffn_W1, L0_ffn_b1, L0_ffn_W3, L0_ffn_b3, L0_ffn_W2, L0_ffn_b2, L0_ffn_Wg, L0_ffn_bg, L0_ffn_Wf, L0_ffn_bf), axis=-1)
    x = _layernorm(x + _L1_attn_ref(x, L1_attn_Wk, L1_attn_bk, L1_attn_Wv, L1_attn_bv, L1_attn_ln_g, L1_attn_ln_b, L1_attn_Wo, L1_attn_bo), axis=-1)
    x = _layernorm(x + _L1_xattn_ref(ctx_1024, ctx_1024, x, L1_xattn_Wk, L1_xattn_Wv, L1_xattn_bv, L1_xattn_Wq, L1_xattn_bq, L1_xattn_Wo, L1_xattn_bo), axis=-1)
    x = _layernorm(x + _L1_ffn_ref(x, L1_ffn_clip_x, L1_ffn_clip_down, L1_ffn_w_gate, L1_ffn_w_up, L1_ffn_w_down), axis=-1)
    return x

_drawn_inputs = setup_inputs


def setup_inputs(seed=0):
    import zlib

    import numpy as np

    out = dict(_drawn_inputs(seed))
    spreads = {'L0_ffn_b1': (0.0, 0.278),
     'L0_ffn_b3': (0.0, 0.277),
     'L0_ffn_b2': (0.0, 0.1),
     'L0_ffn_bg': (0.0, 0.1),
     'L0_ffn_bf': (0.0, 0.1),
     'L1_attn_bk': (0.0, 0.1),
     'L1_attn_bv': (0.0, 0.1),
     'L1_attn_ln_g': (1.0, 0.2),
     'L1_attn_ln_b': (0.0, 0.1),
     'L1_attn_bo': (0.0, 0.1),
     'L1_xattn_bv': (0.0, 0.1),
     'L1_xattn_bq': (0.0, 0.471),
     'L1_xattn_bo': (0.0, 0.1)}
    factors = {'L0_xattn_bq': 8.0, 'L0_xattn_bk': 8.0, 'L0_xattn_bv': 3.382, 'L0_xattn_bo': 3.478}
    for name, (base, spread) in spreads.items():
        noise = np.random.default_rng([zlib.crc32(name.encode()), seed]).standard_normal(out[name].shape)
        drawn = base * np.exp(spread * noise) if base else spread * noise
        out[name] = jnp.asarray(drawn.astype(out[name].dtype))
    for name, factor in factors.items():
        out[name] = (out[name] * factor).astype(out[name].dtype)
    return out
```

```python
from contextlib import ExitStack

import concourse.bass as bass
import numpy as np
from concourse import mybir

F32 = mybir.dt.float32
BF16 = mybir.dt.bfloat16
ALU = mybir.AluOpType
ACT = mybir.ActivationFunctionType
AX = mybir.AxisListType

P = 128
B, S, D = 8, 512, 256
C = 1601
T = B * S
QT = S // P
KC = D // P
H, DK = 16, 16
HG, HPG = 4, 4
HALO = 32
WIN = P + 2 * HALO
PADT = T + 2 * HALO
BW = S + 2 * HALO
EPS = 1e-5
NEG = -1e30
KPART = (0, 0, 1, 1, 0, 2)
QPART = (0, 1, 0, 1, 2, 0)
SPLIT = len(KPART) * DK
POSR = 12


def after(eng, sem, value):
    if not isinstance(value, int) or value > 0:
        eng.wait_ge(sem, value)


def over_batches(eng, body):
    body(0, 0, 0)
    with eng.Fori(0, (B - 2) // 2) as i:
        body(i * 2 + 1, 1, i)
        body(i * 2 + 2, 0, i + 1)
    body(B - 1, 1, B // 2 - 1)


class Sems:

    def __init__(self, nc, ctx, phase):
        self.nc, self.phase, self.mine = nc, phase, []
        ctx.callback(self.clear)

    def __call__(self, name, n=None):
        if n is None:
            self.mine.append(self.nc.alloc_semaphore(f"{self.phase}_{name}"))
            return self.mine[-1]
        return [self(f"{name}{i}") for i in range(n)]

    def clear(self):
        self.nc.clear_and_free_semaphores(self.mine)
        self.nc.all_engine_barrier()


class Mem:
    def __init__(self, nc, ctx, phase):
        self.nc, self.ctx, self.phase = nc, ctx, phase

    def sb(self, name, shape, dt=F32):
        return self.ctx.enter_context(self.nc.sbuf_tensor(f"{self.phase}_{name}", shape, dt))

    def ps(self, name, shape, dt=F32):
        return self.ctx.enter_context(self.nc.psum_tensor(f"{self.phase}_{name}", shape, dt))


class Chain:

    def __init__(self, eng, sem, per_batch=0):
        self.eng, self.sem, self.per, self.b, self.n = eng, sem, per_batch, 0, 0

    def start(self, b):
        self.b, self.n = b, 0

    def link(self, ins):
        self.n += 1
        ins.then_inc(self.sem, 1)
        self.eng.wait_ge(self.sem, self.b * self.per + self.n)

    def end(self):
        assert self.n == self.per, (self.n, self.per)


def w_in(ap):
    return ap.rearrange("(c p) n -> p c n", p=P)


def load_all(nc, g, d):
    with ExitStack() as ctx:
        sem = Sems(nc, ctx, "ld")
        loaded = sem("loaded")
        block = ctx.enter_context(nc.Block())

        @block.sync
        def _(sp):
            sp.dma_start(g.x[:, :, :], d["x"].rearrange("b (t p) d -> p (b t) d", p=P)).then_inc(loaded, 16)
            sp.dma_start(g.ident[:, :], d["ident"]).then_inc(loaded, 16)
            sp.wait_ge(loaded, 32)

        @block.vector
        def _(dve):
            dve.memset(g.halfneg[:, :], -0.5)
            dve.wait_ge(loaded, 32)
            dve.tensor_copy(g.identb[:, :], g.ident[:, :])


def project_split(nc, phase, source, width, chunks, jobs):
    ahead = 4 // (KC * len(jobs))
    pieces = [(a, j, oc) for a in range(ahead) for j in range(len(jobs)) for oc in range(KC)]
    turns = chunks // ahead
    with ExitStack() as ctx:
        sem, mem = Sems(nc, ctx, phase), Mem(nc, ctx, phase)
        w_loaded, w_ready, projected, rest_ready = (sem(x) for x in ("w_loaded", "w_ready", "projected", "rest_ready"))
        part0_ready, part1_ready, parts_ready = (sem(x) for x in ("part0_ready", "part1_ready", "parts_ready"))
        stored = sem("stored", 4)
        srcT = mem.sb("source", [P, KC, chunks * width])
        src_loaded = sem("src_loaded", 4)
        wT = [mem.sb(f"w{j}", [P, KC, D]) for j in range(len(jobs))]
        bias = [mem.sb(f"b{j}", [P, KC]) for j in range(len(jobs))]
        rest = mem.sb("rest", [P, 4, width])
        parts = mem.sb("parts", [P, 4, 3, width], BF16)
        acc = [mem.ps(f"acc{k}", [P, 512]) for k in range(4)]
        block = ctx.enter_context(nc.Block())
        n_w = sum(1 + (j[1] is not None) for j in jobs)

        def turn_loop(eng, body):
            body(0)
            if turns > 1:
                with eng.Fori(1, turns) as i:
                    body(i)

        @block.sync
        def _(sp):
            for j, (w, b, _, _) in enumerate(jobs):
                sp.dma_start(wT[j][:, :, :], w_in(w)).then_inc(w_loaded, 16)
                if b is not None:
                    sp.dma_start(bias[j][:, :], b.rearrange("(c p) -> p c", p=P),
                                 allow_slow_non_contiguous=True).then_inc(w_loaded, 16)

            quarter = chunks * width // 4
            for k in range(4):
                sp.dma_start(srcT[:, :, k * quarter:(k + 1) * quarter],
                             w_in(source)[:, :, k * quarter:(k + 1) * quarter]).then_inc(src_loaded[k], 16)

            def body(i):
                for k, (a, j, oc) in enumerate(pieces):
                    sp.wait_ge(parts_ready, i * 4 + k + 1)
                    out = jobs[j][3].rearrange("s (c p) t -> p c s t", p=P)[:, oc, :, bass.ds((i * ahead + a) * width, width)]
                    sp.dma_start(out, parts[:, k, :, :]).then_inc(stored[k], 16)
            turn_loop(sp, body)
            for k in range(4):
                sp.wait_ge(stored[k], 16 * turns)

        @block.tensor
        def _(pe):
            pe.wait_ge(w_ready, 1)
            for k in range(4):
                pe.wait_ge(src_loaded[k], 16)

            def body(i):
                for k, (a, j, oc) in enumerate(pieces):
                    after(pe, rest_ready, i * 4 + k - 3)
                    for c in range(KC):
                        mm = pe.matmul(acc[k][:, 0:width], wT[j][:, c, oc * P:(oc + 1) * P],
                                       srcT[:, c, bass.ds((i * ahead + a) * width, width)],
                                       start=(c == 0), stop=(c == KC - 1))
                    mm.then_inc(projected, 1)
            turn_loop(pe, body)

        @block.scalar
        def _(act):
            act.wait_ge(w_ready, 1)

            def body(i):
                for pair in (0, 2):
                    for k in (pair, pair + 1):
                        a, j, oc = pieces[k]
                        act.wait_ge(projected, i * 4 + k + 1)
                        after(act, stored[k], i * 16)
                        act.activation(parts[:, k, 0, :], acc[k][:, 0:width], ACT.Identity,
                                       bias=bias[j][:, oc:oc + 1] if jobs[j][1] is not None else 0.0)\
                           .then_inc(part0_ready, 1)
                    for k in (pair, pair + 1):
                        act.wait_ge(rest_ready, i * 4 + k + 1)
                        act.activation(parts[:, k, 1, :], rest[:, k, :], ACT.Copy).then_inc(part1_ready, 1)
            turn_loop(act, body)

        @block.vector
        def _(dve):
            dve.wait_ge(w_loaded, 16 * n_w)
            scaled = sem("scaled")
            n = 0
            for j, (_, b, factor, _) in enumerate(jobs):
                if factor != 1.0:
                    dve.tensor_scalar(wT[j][:, :, :], wT[j][:, :, :], factor, None, ALU.mult).then_inc(scaled, 1)
                    n += 1
                    if b is not None:
                        dve.tensor_scalar(bias[j][:, :], bias[j][:, :], factor, None, ALU.mult).then_inc(scaled, 1)
                        n += 1
            after(dve, scaled, n)
            dve.sem_inc(w_ready, 1)

            def body(i):
                for pair in (0, 2):
                    for k in (pair, pair + 1):
                        a, j, oc = pieces[k]
                        dve.wait_ge(part0_ready, i * 4 + k + 1)
                        after(dve, parts_ready, i * 4 + k - 3)
                        dve.scalar_tensor_tensor(out=rest[:, k, :], in0=acc[k][:, 0:width],
                                                 scalar=bias[j][:, oc:oc + 1] if jobs[j][1] is not None else 0.0,
                                                 in1=parts[:, k, 0, :], op0=ALU.add, op1=ALU.subtract)\
                           .then_inc(rest_ready, 1)
                    for k in (pair, pair + 1):
                        dve.wait_ge(part1_ready, i * 4 + k + 1)
                        dve.tensor_tensor(parts[:, k, 2, :], rest[:, k, :], parts[:, k, 1, :], ALU.subtract)\
                           .then_inc(parts_ready, 1)
            turn_loop(dve, body)


class Tail:

    def __init__(self, nc, ctx, g, sem, mem, d, bo, xT_out, heads=None, terms=None, factor=1.0, row=None):
        self.g, self.d, self.bo_in, self.xT_out, self.heads = g, d, bo, xT_out, heads
        self.has_bo, self.factor, self.row = bo is not None, factor, row
        self.terms = terms or (lambda par, k: [(self.oT[:, par, h, k * P:(k + 1) * P], self.woP[:, h, :])
                                               for h in range(HG)])
        if heads:
            self.woP = mem.sb("woP", [P, HG, D])
            self.gather = mem.sb("gather", [P, HG, H])
            self.spread = mem.sb("spread", [H, HG, P])
            self.oT = mem.sb("oT", [P, 2, HG, S])
            self.inv = mem.sb("inv", [H, S])
        self.y = mem.sb("y", [P, QT, D])
        self.xn = mem.sb("xn", [P, QT, D])
        self.stats = mem.sb("stats", [P, QT, 6])
        self.mv = mem.sb("mv", [P, QT, 2])
        self.veps = mem.sb("veps", [P, QT])
        self.rstd = mem.sb("rstd", [P, QT])
        self.bo = mem.sb("bo", [P, D])
        self.misc = mem.ps("misc", [P, 512])
        if xT_out is not None:
            self.xt = mem.sb("xt", [P, KC, S])
        self.misc_done = sem("misc_done")
        self.freed = sem("freed")
        self.o_copied = sem("o_copied")
        self.stat = sem("stat")
        self.var_ready = sem("var_ready")
        self.rstd_ready = sem("rstd_ready")
        self.xn_ready = sem("xn_ready")
        self.x_kept = sem("x_kept")
        self.passed, self.pool_passed = sem("passed"), sem("pool_passed")
        self.c_loaded = sem("tail_loaded")
        self.xt_stored = sem("xt_stored")
        self.xt_free = sem("xt_free")

    def begin(self, pool):
        pool.sem_inc(self.freed, 1)
        pool.sem_inc(self.x_kept, 1)
        if self.xT_out is not None:
            pool.sem_inc(self.xt_free, 1)

    def wait_freed(self, eng, n):
        eng.wait_ge(self.freed, n + 1)

    def load(self, sp):
        if self.heads:
            sp.dma_start(self.woP[:, :, :], self.d[self.heads + "_WoP"].rearrange("(c p) n -> p c n", p=P)).then_inc(self.c_loaded, 16)
            sp.dma_start(self.gather[:, :, :], self.d["gather"]).then_inc(self.c_loaded, 16)
            sp.dma_start(self.spread[:, :, :], self.d["spread"]).then_inc(self.c_loaded, 16)
        if isinstance(self.bo_in, str):
            sp.dma_start(self.bo[:, :], self.d[self.bo_in].rearrange("(a n) -> a n", a=1).to_broadcast([P, D]))\
              .then_inc(self.c_loaded, 16)

    def wait_loaded(self, eng):
        after(eng, self.c_loaded, 48 * (self.heads is not None) + 16 * isinstance(self.bo_in, str))

    def pe(self, pe, step, b, par, n):
        what, k = step
        self.wait_freed(pe, n - 1)
        if what == "den":
            pe.wait_ge(self.o_copied, b * HG + HG)
            for h in range(HG):
                mm = pe.matmul(self.misc[0:H, 0:S], self.gather[:, h, :], self.oT[:, par, h, :],
                               start=(h == 0), stop=(h == HG - 1))
        elif what == "spread":
            mm = pe.matmul(self.misc[:, 0:S], self.spread[:, k, :], self.inv[:, :], start=True, stop=True)
        elif what == "out":
            terms = self.terms(par, k)
            for i, (lhsT, rhs) in enumerate(terms):
                mm = pe.matmul(self.misc[:, 0:D], lhsT, rhs, start=(i == 0), stop=(i == len(terms) - 1))
        else:
            pe.wait_ge(self.xn_ready, b * QT + k + 1)
            for c in range(KC):
                mm = pe.transpose(self.misc[:, c * P:(c + 1) * P], self.xn[:, k, c * P:(c + 1) * P],
                                  self.g.ident[:, :])
        mm.then_inc(self.misc_done, 1)

    def act(self, act, step, b, n):
        what, k = step
        if what == "turn":
            act.wait_ge(self.misc_done, n)
            if k == 0:
                act.wait_ge(self.xt_free, b + 1)
            act.activation(self.xt[:, :, k * P:(k + 1) * P],
                           self.misc[:, 0:D].rearrange("p (c t) -> p c t", c=KC), ACT.Copy).then_inc(self.freed, 1)

    def dve(self, dve, step, b, par, n):
        what, k = step
        if what == "turn":
            return
        dve.wait_ge(self.misc_done, n)
        if what == "den":
            dve.reciprocal(self.inv[:, :], self.misc[0:H, 0:S]).then_inc(self.freed, 1)
        elif what == "spread":
            dve.tensor_tensor(self.oT[:, par, k, :], self.oT[:, par, k, :], self.misc[:, 0:S], ALU.mult).then_inc(self.freed, 1)
        elif what == "out":
            links = 2 + self.has_bo + (self.row is not None)
            at = b * (QT * links) + k * links
            dve.wait_ge(self.x_kept, b + 1)
            x, y, i = self.g.x[:, b * QT + k, :], self.y[:, k, :], 0
            if self.row is not None:
                dve.tensor_tensor(y, self.misc[:, 0:D], self.row, ALU.mult).then_inc(self.freed, 1)
                self.wait_freed(dve, n)
                dve.tensor_tensor(y, y, x, ALU.add).then_inc(self.stat, 1)
                i += 1
                dve.wait_ge(self.stat, at + i)
            else:
                dve.scalar_tensor_tensor(out=y, in0=x, scalar=self.factor, in1=self.misc[:, 0:D],
                                         op0=ALU.mult, op1=ALU.add).then_inc(self.freed, 1)
                self.wait_freed(dve, n)
            if self.has_bo:
                dve.tensor_tensor(y, y, self.bo[:, :], ALU.add).then_inc(self.stat, 1)
                i += 1
                dve.wait_ge(self.stat, at + i)
            dve.bn_stats(self.stats[:, k, :], self.y[:, k, :]).then_inc(self.stat, 1)
            dve.wait_ge(self.stat, at + links - 1)
            dve.sem_inc(self.passed, 1)
            dve.bn_aggr(self.mv[:, k, :], self.stats[:, k, :]).then_inc(self.stat, 1)
            dve.wait_ge(self.stat, at + links)
            if k == QT - 1:
                dve.tensor_scalar(self.veps[:, :], self.mv[:, :, 1], EPS, None, ALU.add).then_inc(self.var_ready, 1)

    def dve_normalize(self, dve, b):
        dve.wait_ge(self.rstd_ready, b + 1)
        dve.wait_ge(self.x_kept, b + 1)
        for k in range(QT):
            dve.tensor_scalar(self.xn[:, k, :], self.y[:, k, :], self.mv[:, k, 0:1], self.rstd[:, k:k + 1],
                              ALU.subtract, ALU.mult).then_inc(self.xn_ready, 1)

    def pool(self, pool, b, n_turned):
        pool.wait_ge(self.var_ready, b + 1)
        pool.tensor_tensor(self.rstd[:, :], self.veps[:, :], self.g.halfneg[:, :], ALU.pow).then_inc(self.rstd_ready, 1)
        pool.wait_ge(self.xn_ready, b * QT + QT)
        pool.sem_inc(self.pool_passed, 1)
        pool.tensor_copy(self.g.x[:, bass.ds(b * QT, QT), :], self.xn[:, :, :]).then_inc(self.x_kept, 1)
        if self.xT_out is None:
            return
        self.wait_freed(pool, n_turned)
        pool.dma_start(w_in(self.xT_out)[:, :, bass.ds(b * S + HALO, S)], self.xt[:, :, :]).then_inc(self.xt_stored, 16)
        pool.wait_ge(self.xt_stored, b * 16 + 16)
        pool.sem_inc(self.xt_free, 1)

    def finish(self, eng):
        eng.wait_ge(self.x_kept, B + 1)
        if self.xT_out is not None:
            eng.wait_ge(self.xt_stored, B * 16)


PLAIN_STEPS = [("out", q) for q in range(QT)] + [("turn", q) for q in range(QT)]
TAIL_STEPS = [("den", 0)] + [("spread", h) for h in range(HG)] + [("out", q) for q in range(QT)] + \
             [("turn", q) for q in range(QT)]


SHIFTED = QT + 1
VT = 2 * DK
ROWS = SPLIT + POSR


def window_attention(nc, g, d, q_parts, k_parts, xT_out):
    UNITS = HG * QT
    at_unit = [[("den", 0)], [("spread", 0)], [("spread", 1)], [("spread", 2)], [("spread", 3)], [("out", 0)],
               [("out", 1)], [("out", 2)], [("out", 3)], [("v", 0)], [("v", 1)], [("v", 2)],
               [("v", 3), ("turn", 0)], [("v", 4), ("turn", 1)], [("turn", 2)], [("turn", 3)]]
    per_batch = sum(len(u) for u in at_unit)
    NORMALIZE_AT = 10

    def plan(b):
        first, last = isinstance(b, int) and b == 0, isinstance(b, int) and b == B - 1
        n = SHIFTED if first else 2 * SHIFTED + (b - 1) * per_batch
        out, k = [], 0
        for unit in at_unit:
            row = []
            for step in unit:
                if (step[0] == "v" and not last) or (step[0] != "v" and not first):
                    k += 1
                    row.append((step, n + k))
            out.append(row)
        return out

    after_last = 2 * SHIFTED + (B - 2) * per_batch + len(TAIL_STEPS)

    with ExitStack() as ctx:
        sem, mem = Sems(nc, ctx, "wa"), Mem(nc, ctx, "wa")
        t = Tail(nc, ctx, g, sem, mem, d, None, xT_out, heads="L0_attn")
        wvT = mem.sb("wvT", [P, KC, D])
        mask = mem.sb("mask", [P, 3, WIN], BF16)
        kq = mem.sb("kq", [P, HG, HPG, BW], BF16)
        qq = mem.sb("qq", [P, HG, HPG, S], BF16)
        xw = mem.sb("xw", [P, 2, KC, BW])
        v = mem.sb("v", [P, 2, SHIFTED, H, VT])
        probs = mem.sb("probs", [P, 2, HPG, WIN])
        pT1 = mem.sb("pT1", [P, 2, HPG * P])
        pT2 = mem.sb("pT2", [P // 2, 2, HPG * P])
        negmax = mem.sb("negmax", [P, 2, HPG])
        slope = mem.sb("slope", [P, 2, H])
        slope_part = mem.sb("slope_part", [P, 3, H], BF16)
        pick = mem.sb("pick", [P, 2, 4])
        pos_q = mem.sb("pos_q", [P, S])
        pos_k = mem.sb("pos_k", [P, BW])
        side = mem.sb("side", [P, 2, H])
        pS = [mem.ps(f"pS{k}", [P, 2, 512]) for k in range(2)]
        pTa, pTb = mem.ps("pTa", [P, 512]), mem.ps("pTb", [P, 512])
        pO = mem.ps("pO", [P, 512])
        const_loaded, const_ready = sem("const_loaded"), sem("const_ready")
        kq_loaded, xw_loaded = sem("kq_loaded", HG), sem("xw_loaded", 2)
        scored, max_ready, exped = sem("scored"), sem("max_ready"), sem("exped")
        turned, t1_copied, t2_copied, pv_done = sem("turned"), sem("t1_copied"), sem("t2_copied"), sem("pv_done")
        block = ctx.enter_context(nc.Block())
        rows = slice(SPLIT, SPLIT + POSR)

        @block.sync
        def _(sp):
            sp.dma_start(slope[rows, 0, :], d["slopes"]).then_inc(const_loaded, 16)
            sp.dma_start(pick[rows, :, :], d["pick"]).then_inc(const_loaded, 16)
            sp.dma_start(pos_q[rows, :], d["pos_q"]).then_inc(const_loaded, 16)
            sp.dma_start(pos_k[rows, :], d["pos_k"]).then_inc(const_loaded, 16)
            sp.dma_start(probs[:, 0, 0:3, :], d["mask"]).then_inc(const_loaded, 16)
            sp.dma_start(wvT[:, :, :], w_in(d["L0_attn_WvT"])).then_inc(t.c_loaded, 16)
            t.load(sp)
            sp.dma_start(xw[:, 0, :, :], w_in(d["xT"])[:, :, 0:BW]).then_inc(xw_loaded[0], 16)

            def body(b, par, used):
                for hg in range(HG):
                    after(sp, scored, (b - 1) * UNITS + (hg + 1) * QT)
                    heads = slice(hg * HPG * DK, (hg + 1) * HPG * DK)
                    for r in range(len(KPART)):
                        to = slice(r * DK, (r + 1) * DK)
                        sp.dma_start(kq[to, hg, :, :], k_parts[KPART[r], heads, bass.ds(b * S, BW)]
                                     .rearrange("(h e) t -> e h t", e=DK)).then_inc(kq_loaded[hg], 16)
                        sp.dma_start(qq[to, hg, :, :], q_parts[QPART[r], heads, bass.ds(b * S + HALO, S)]
                                     .rearrange("(h e) t -> e h t", e=DK)).then_inc(kq_loaded[hg], 16)
                    if hg == 0 and not (isinstance(b, int) and b == B - 1):
                        after(sp, t.misc_done, 0 if isinstance(b, int) else 2 * SHIFTED + (b - 1) * per_batch)
                        sp.dma_start(xw[:, 1 - par, :, :], w_in(d["xT"])[:, :, bass.ds(b * S + S, BW)])\
                          .then_inc(xw_loaded[1 - par], 16)
            over_batches(sp, body)
            for hg in range(HG):
                sp.wait_ge(kq_loaded[hg], B * 2 * len(KPART) * 16)

        def v_pe(pe, par, used, s, n):
            if s == 0:
                pe.wait_ge(xw_loaded[par], used * 16 + 16)
            t.wait_freed(pe, n - 1)
            m = P if s < QT else 2 * HALO
            for c in range(KC):
                mm = pe.matmul(t.misc[0:m, 0:D], xw[:, par, c, s * P:s * P + m], wvT[:, c, :],
                               start=(c == 0), stop=(c == KC - 1))
            mm.then_inc(t.misc_done, 1)

        def v_act(act, b, par, s, n):
            m = P if s < QT else 2 * HALO
            act.wait_ge(t.misc_done, n)
            after(act, pv_done, (b - 1) * UNITS)
            act.activation(v[0:m, par, s, :, 0:DK], t.misc[0:m, 0:D].rearrange("p (h e) -> p h e", h=H), ACT.Copy)\
               .then_inc(t.freed, 1)

        def scores(pe, b, k):
            hg, qt = k // QT, k % QT
            if qt == 0:
                pe.wait_ge(kq_loaded[hg], b * (2 * len(KPART) * 16) + 2 * len(KPART) * 16)
            after(pe, exped, b * UNITS + k - 1)
            for j in range(HPG):
                out = pS[k % 2][:, j // 2, j % 2 * WIN:(j % 2 + 1) * WIN]
                pe.matmul(out, qq[0:ROWS, hg, j, qt * P:(qt + 1) * P], kq[0:ROWS, hg, j, qt * P:qt * P + WIN],
                          start=True, stop=False)
                edge = 0 if qt == 0 else 2 if qt == QT - 1 else 1
                mm = pe.matmul(out, g.identb[:, :], mask[:, edge, :], start=False, stop=True)
            mm.then_inc(scored, 1)

        def turn(pe, b, k):
            pe.wait_ge(exped, b * UNITS + k + 1)
            after(pe, t1_copied, b * UNITS + k)
            after(pe, t2_copied, b * UNITS + k)
            for j in range(HPG):
                pe.transpose(pTa[:, j * P:(j + 1) * P], probs[:, k % 2, j, 0:P], g.ident[:, :])
            for j in range(HPG):
                mm = pe.transpose(pTb[0:P // 2, j * P:(j + 1) * P], probs[:, k % 2, j, P:WIN], g.ident[:, :])
            mm.then_inc(turned, 1)

        def times_v(pe, b, par, k):
            hg, qt = k // QT, k % QT
            pe.wait_ge(t1_copied, b * UNITS + k + 1)
            pe.wait_ge(t2_copied, b * UNITS + k + 1)
            if qt == 0:
                after(pe, t.o_copied, b * HG + hg)
            if k == 0:
                t.wait_freed(pe, SHIFTED if isinstance(b, int) and b == 0 else 2 * SHIFTED + (b - 1) * per_batch)
            for half, (src, m) in enumerate(((pT1, P), (pT2, P // 2))):
                for j in range(HPG):
                    mm = pe.matmul(pO[j * VT:(j + 1) * VT, qt * P:(qt + 1) * P],
                                   v[0:m, par, qt + half, hg * HPG + j, :], src[0:m, k % 2, j * P:(j + 1) * P],
                                   start=(half == 0), stop=(half == 1), skip_group_check=True)
            mm.then_inc(pv_done, 1)

        @block.tensor
        def _(pe):
            pe.wait_ge(const_ready, 1)
            t.wait_loaded(pe)
            for s in range(SHIFTED):
                v_pe(pe, 0, 0, s, s + 1)

            def body(b, par, used):
                for k, steps in enumerate(plan(b)):
                    scores(pe, b, k)
                    if k >= 1:
                        turn(pe, b, k - 1)
                    if k >= 2:
                        times_v(pe, b, par, k - 2)
                    for step, n in steps:
                        if step[0] == "v":
                            v_pe(pe, 1 - par, used + par, step[1], n)
                        else:
                            t.pe(pe, step, b - 1, 1 - par, n)
                turn(pe, b, UNITS - 1)
                times_v(pe, b, par, UNITS - 2)
                times_v(pe, b, par, UNITS - 1)
            over_batches(pe, body)
            for k, step in enumerate(TAIL_STEPS):
                t.pe(pe, step, B - 1, 1, after_last + k + 1)

        @block.scalar
        def _(act):
            for s in range(SHIFTED):
                v_act(act, 0, 0, s, s + 1)

            def exps(b, k):
                n = b * UNITS + k
                act.wait_ge(max_ready, n + 1)
                after(act, turned, n - 1)
                for j in range(HPG):
                    ins = act.activation(probs[:, k % 2, j, :], pS[k % 2][:, j // 2, j % 2 * WIN:(j % 2 + 1) * WIN],
                                         ACT.Exp, bias=negmax[:, k % 2, j:j + 1])
                ins.then_inc(exped, 1)

            def copy_t2(b, k):
                act.wait_ge(turned, b * UNITS + k + 1)
                after(act, pv_done, b * UNITS + k - 1)
                act.activation(pT2[:, k % 2, :], pTb[0:P // 2, :], ACT.Copy).then_inc(t2_copied, 1)

            def copy_o(b, par, hg):
                act.wait_ge(pv_done, b * UNITS + (hg + 1) * QT)
                act.activation(t.oT[:, par, hg, :], pO[:, :], ACT.Copy).then_inc(t.o_copied, 1)

            def body(b, par, used):
                for k, steps in enumerate(plan(b)):
                    exps(b, k)
                    if k >= 1:
                        copy_t2(b, k - 1)
                    if k >= 2 and (k - 2) % QT == QT - 1:
                        copy_o(b, par, (k - 2) // QT)
                    for step, n in steps:
                        if step[0] == "v":
                            v_act(act, b + 1, 1 - par, step[1], n)
                        else:
                            t.act(act, step, b - 1, n)
                copy_t2(b, UNITS - 1)
                copy_o(b, par, HG - 1)
            act.wait_ge(const_ready, 1)
            over_batches(act, body)
            for k, step in enumerate(TAIL_STEPS):
                t.act(act, step, B - 1, after_last + k + 1)

        @block.vector
        def _(dve):
            made = sem("made")
            ready = sem("ready")
            count = [0]

            def link(ins):
                count[0] += 1
                ins.then_inc(made, 1)
                dve.wait_ge(made, count[0])
            dve.wait_ge(const_loaded, 80)
            link(dve.tensor_copy(mask[:, :, :], probs[:, 0, 0:3, :]))
            link(dve.memset(v[:, :, :, :, DK:VT], 1.0))
            for i in range(3):
                link(dve.tensor_copy(slope_part[rows, i, :], slope[rows, i % 2, :]))
                if i < 2:
                    link(dve.tensor_tensor(slope[rows, (i + 1) % 2, :], slope[rows, i % 2, :],
                                           slope_part[rows, i, :], ALU.subtract))
            for s in range(2):
                link(dve.tensor_scalar(side[rows, s, :], slope_part[rows, 0, :], pick[rows, s, 1:2],
                                       pick[rows, s, 0:1], ALU.mult, ALU.add))
                for i in (1, 2):
                    link(dve.scalar_tensor_tensor(out=side[rows, s, :], in0=slope_part[rows, i, :],
                                                  scalar=pick[rows, s, i + 1:i + 2], in1=side[rows, s, :],
                                                  op0=ALU.mult, op1=ALU.add))
            for h in range(H):
                dve.tensor_scalar(qq[rows, h // HPG, h % HPG, :], pos_q[rows, :], side[rows, 0, h:h + 1], None,
                                  ALU.mult).then_inc(ready, 1)
                dve.tensor_scalar(kq[rows, h // HPG, h % HPG, :], pos_k[rows, :], side[rows, 1, h:h + 1], None,
                                  ALU.mult).then_inc(ready, 1)
            dve.wait_ge(ready, 2 * H)
            dve.sem_inc(const_ready, 1)

            def maxes(b, k):
                n = b * UNITS + k
                dve.wait_ge(scored, n + 1)
                after(dve, exped, n - 1)
                dve.tensor_reduce(negmax[:, k % 2, :].rearrange("p (a c) -> p a c", a=2),
                                  pS[k % 2][:, :, 0:2 * WIN].rearrange("p a (c w) -> p a c w", c=2),
                                  AX.X, ALU.max, negate=True).then_inc(max_ready, 1)

            def copy_t1(b, k):
                dve.wait_ge(turned, b * UNITS + k + 1)
                after(dve, pv_done, b * UNITS + k - 1)
                dve.tensor_copy(pT1[:, k % 2, :], pTa[:, :]).then_inc(t1_copied, 1)

            def body(b, par, used):
                for k, steps in enumerate(plan(b)):
                    maxes(b, k)
                    if k >= 1:
                        copy_t1(b, k - 1)
                    for step, n in steps:
                        if step[0] != "v":
                            t.dve(dve, step, b - 1, 1 - par, n)
                    if k == NORMALIZE_AT and not (isinstance(b, int) and b == 0):
                        t.dve_normalize(dve, b - 1)
                copy_t1(b, UNITS - 1)
            over_batches(dve, body)
            for k, step in enumerate(TAIL_STEPS):
                t.dve(dve, step, B - 1, 1, after_last + k + 1)
                if step == ("out", QT - 1):
                    t.dve_normalize(dve, B - 1)

        @block.gpsimd
        def _(pool):
            t.begin(pool)
            with pool.Fori(0, B - 1) as b:
                t.pool(pool, b, 2 * SHIFTED + b * per_batch + per_batch)
            t.pool(pool, B - 1, after_last + len(TAIL_STEPS))
            t.finish(pool)


VCH, VTOK = 4, 101
CCH = VCH * VTOK
CTX = 32 * CCH
KT = -(-C // P)
KLAST = C - (KT - 1) * P


def project_v(nc, d, v_out):
    with ExitStack() as ctx:
        sem, mem = Sems(nc, ctx, "pv"), Mem(nc, ctx, "pv")
        cT = mem.sb("cT", [P, 2, KC, CCH])
        wT, bv = mem.sb("wT", [P, KC, D]), mem.sb("bv", [P, D])
        vs = mem.sb("vs", [P, 2, VCH, D])
        acc = mem.ps("acc", [P, 2, 2, 2, D])
        w_loaded, loaded, stored = sem("w_loaded"), sem("loaded", 2), sem("stored", 2)
        product_ready, v_ready = sem("product_ready"), sem("v_ready")
        block = ctx.enter_context(nc.Block())
        TURNS = CTX // CCH // 2

        def turns(eng, body):
            body(0)
            with eng.Fori(1, TURNS) as i:
                body(i)

        @block.sync
        def _(sp):
            sp.dma_start(wT[:, :, :], w_in(d["L0_xattn_WvT"])).then_inc(w_loaded, 16)
            sp.dma_start(bv[:, :], d["L0_xattn_bv"].rearrange("(a n) -> a n", a=1).to_broadcast([P, D]))\
              .then_inc(w_loaded, 16)

            def body(i):
                for k in range(2):
                    after(sp, product_ready, i * 4 + 2 * k - 2)
                    sp.dma_start(cT[:, k, :, :], w_in(d["cT"])[:, :, bass.ds((i * 2 + k) * CCH, CCH)])\
                      .then_inc(loaded[k], 16)
            turns(sp, body)

        @block.gpsimd
        def _(pool):
            def body(i):
                for k in range(2):
                    pool.wait_ge(v_ready, i * 4 + 2 * k + 2)
                    pool.dma_start(v_out[bass.ds((i * 2 + k) * CCH, CCH), :].rearrange("(t p) n -> p t n", p=VTOK),
                                   vs[0:VTOK, k, :, :]).then_inc(stored[k], 16)
            turns(pool, body)
            for k in range(2):
                pool.wait_ge(stored[k], TURNS * 16)

        @block.tensor
        def _(pe):
            pe.wait_ge(w_loaded, 32)

            def body(i):
                for k in range(2):
                    pe.wait_ge(loaded[k], i * 16 + 16)
                    for h in range(2):
                        after(pe, v_ready, i * 4 + 2 * k + h - 3)
                        for q in range(2):
                            tile = 2 * h + q
                            for c in range(KC):
                                mm = pe.matmul(acc[0:VTOK, k, h, q, :], cT[:, k, c, tile * VTOK:(tile + 1) * VTOK],
                                               wT[:, c, :], start=(c == 0), stop=(c == KC - 1))
                        mm.then_inc(product_ready, 1)
            turns(pe, body)

        @block.vector
        def _(dve):
            dve.wait_ge(w_loaded, 32)

            def body(i):
                for k in range(2):
                    after(dve, stored[k], i * 16)
                    for h in range(2):
                        dve.wait_ge(product_ready, i * 4 + 2 * k + h + 1)
                        dve.tensor_tensor(vs[0:VTOK, k, 2 * h:2 * h + 2, :], acc[0:VTOK, k, h, :, :],
                                          bv[0:VTOK, :].rearrange("p (a n) -> p a n", a=1).to_broadcast([VTOK, 2, D]),
                                          ALU.add).then_inc(v_ready, 1)
            turns(dve, body)


def cross_attention(nc, g, d, q_parts, k_parts, v_in, xT_out):
    MAXR = 3
    ROWS_B = SPLIT + MAXR
    U = B * HG
    TILES = HPG * QT
    HALVES = 2 * TILES
    HALF = (0, (C + 1) // 2, C)
    STEPS_B = KT * HPG
    HALVES_AT = [3] * 10 + [2] + [0] * (KT - 11)
    ROWS_AT = KT - 1
    tail_at = {}
    for i, step in enumerate(TAIL_STEPS):
        at = (0, 1 + i) if i < 1 + HG + QT else (1, i - (HG + QT))
        tail_at[at] = step
    NORMALIZE_AT = (0, KT - 2)

    def plan(b):
        first, last = isinstance(b, int) and b == 0, isinstance(b, int) and b == B - 1
        n = 2 if first else 2 + 2 * HG + (b - 1) * (2 * HG + len(TAIL_STEPS))
        out, i = {}, 0
        for hg in range(HG):
            for kt in range(KT):
                row = []
                if (hg, kt) in tail_at and not first:
                    row.append(tail_at[hg, kt])
                if kt == ROWS_AT and not (last and hg == HG - 1):
                    row += [("rows", 0), ("rows", 1)]
                out[hg, kt] = []
                for step in row:
                    i += 1
                    out[hg, kt].append((step, n + i))
        return out

    after_last = 2 + 2 * U - 2 + (B - 1) * len(TAIL_STEPS)
    with ExitStack() as ctx:
        sem, mem = Sems(nc, ctx, "xa"), Mem(nc, ctx, "xa")
        t = Tail(nc, ctx, g, sem, mem, d, "L0_xattn_bo", xT_out, heads="L0_xattn")
        kx = mem.sb("kx", [P, HG, HPG, C], BF16)
        qx = mem.sb("qx", [P, HG, HPG, S], BF16)
        v_raw = mem.sb("v_raw", [P, 2, KT, HPG * DK])
        v = mem.sb("v", [P, HG, KT, HPG, VT])
        NP_ = 8
        probs = mem.sb("probs", [P, NP_, S])
        half_max = mem.sb("half_max", [P, QT, HPG, 2])
        negmax = mem.sb("negmax", [P, 2, QT * HPG])
        max_parts = mem.sb("max_parts", [P, QT, HPG, MAXR], BF16)
        pA = [mem.ps(f"pA{k}", [P, 1024]) for k in range(2)]
        pB = [mem.ps(f"pB{k}", [P, 512]) for k in range(2)]
        pO = mem.ps("pO", [P, 512])
        kq_loaded, v_loaded = sem("kq_loaded", HG), sem("v_loaded", 2)
        const_ready, v_placed = sem("const_ready"), sem("v_placed")
        half_scored, half_maxed, max_chain, parts_ready = sem("half_scored"), sem("half_maxed"), sem("max_chain"), sem("parts_ready")
        rows_set, scored, exped, pv_done = sem("rows_set"), sem("scored"), sem("exped"), sem("pv_done")
        block = ctx.enter_context(nc.Block())
        CHAIN = 6
        misc16 = t.misc[:, :].bitcast(BF16)

        def unit_of(b, hg):
            return b * HG + hg

        def later(b, hg, k):
            return (b + (hg + k) // HG, (hg + k) % HG)

        def exists(b, hg):
            return not (isinstance(b, int) and b >= B)

        def turned_count(b):
            p = plan(b)
            return [n for row in p.values() for step, n in row if step == ("turn", QT - 1)][0]

        @block.sync
        def _(sp):
            t.load(sp)

            def load(b, hg):
                u = unit_of(b, hg)
                after(sp, scored, (u - HG + 1) * STEPS_B)
                heads = slice(hg * HPG * DK, (hg + 1) * HPG * DK)
                for r in range(len(KPART)):
                    to = slice(r * DK, (r + 1) * DK)
                    sp.dma_start(kx[to, hg, :, :], k_parts[KPART[r], heads, bass.ds(b * C, C)]
                                 .rearrange("(h e) t -> e h t", e=DK)).then_inc(kq_loaded[hg], 16)
                    sp.dma_start(qx[to, hg, :, :], q_parts[QPART[r], heads, bass.ds(b * S, S)]
                                 .rearrange("(h e) t -> e h t", e=DK)).then_inc(kq_loaded[hg], 16)
                after(sp, v_placed, u - 1)
                full = (KT - 1) * P
                sp.dma_start(v_raw[:, hg % 2, 0:KT - 1, :], v_in[bass.ds(b * C, full), heads]
                             .rearrange("(t p) n -> p t n", p=P)).then_inc(v_loaded[hg % 2], 16)
                sp.dma_start(v_raw[0:KLAST, hg % 2, KT - 1, :], v_in[bass.ds(b * C + full, KLAST), heads])\
                  .then_inc(v_loaded[hg % 2], 16)
            load(0, 0)
            load(0, 1)

            def body(b, par, used):
                for hg in range(HG):
                    to = later(b, hg, 2)
                    if exists(*to):
                        load(*to)
            over_batches(sp, body)

        def place_v(pool, b, hg):
            u = unit_of(b, hg)
            after(pool, pv_done, (u - HG + 1) * KT)
            pool.wait_ge(v_loaded[hg % 2], (b * 2 + hg // 2) * 32 + 32)
            pool.sem_inc(t.pool_passed, 1)
            pool.tensor_copy(v[:, hg, 0:KT - 1, :, 0:DK],
                             v_raw[:, hg % 2, 0:KT - 1, :].rearrange("p t (h e) -> p t h e", e=DK)).then_inc(v_half, 1)
            pool.tensor_copy(v[0:KLAST, hg, KT - 1, :, 0:DK],
                             v_raw[0:KLAST, hg % 2, KT - 1, :].rearrange("p (h e) -> p h e", e=DK)).then_inc(v_half, 1)
            pool.wait_ge(v_half, u * 2 + 2)
            pool.sem_inc(v_placed, 1)
        v_half = sem("v_half")

        @block.gpsimd
        def _(pool):
            t.begin(pool)
            pool.wait_ge(const_ready, 1)
            place_v(pool, 0, 0)
            place_v(pool, 0, 1)

            def body(b, par, used):
                for hg in range(HG):
                    to = later(b, hg, 2)
                    if exists(*to):
                        place_v(pool, *to)
                    if hg == 1 and not (isinstance(b, int) and b == 0):
                        t.pool(pool, b - 1, turned_count(b))
            over_batches(pool, body)
            t.pool(pool, B - 1, after_last + len(TAIL_STEPS))
            t.finish(pool)

        def first_scores(pe, b, hg, half):
            u, tile, h = unit_of(b, hg), half // 2, half % 2
            j, qt = tile // QT, tile % QT
            if half == 0:
                pe.wait_ge(kq_loaded[hg], b * (2 * len(KPART) * 16) + 2 * len(KPART) * 16)
            after(pe, half_maxed, u * HALVES + half - 1)
            lo, hi = HALF[h], HALF[h + 1]
            for at in range(lo, hi, 512):
                w = min(512, hi - at)
                mm = pe.matmul(pA[h][:, at - lo:at - lo + w], qx[0:SPLIT, hg, j, qt * P:(qt + 1) * P],
                               kx[0:SPLIT, hg, j, at:at + w], start=True, stop=True)
            mm.then_inc(half_scored, 1)

        def second_scores(pe, b, hg, kt, j):
            n = unit_of(b, hg) * STEPS_B + kt * HPG + j
            if kt == 0 and j == 0:
                pe.wait_ge(rows_set, unit_of(b, hg) * 2 + 2)
            after(pe, exped, n - 1)
            m = P if kt < KT - 1 else KLAST
            pe.matmul(pB[j % 2][0:m, :], kx[0:ROWS_B, hg, j, kt * P:kt * P + m], qx[0:ROWS_B, hg, j, :],
                      start=True, stop=True).then_inc(scored, 1)

        def times_v(pe, b, hg, kt):
            u = unit_of(b, hg)
            if kt == 0:
                pe.wait_ge(v_placed, u + 1)
                after(pe, t.o_copied, u)
            m = P if kt < KT - 1 else KLAST
            for j in range(HPG):
                n = kt * HPG + j
                pe.wait_ge(exped, u * STEPS_B + n + 1)
                mm = pe.matmul(pO[j * VT:(j + 1) * VT, :], v[0:m, hg, kt, j, :], probs[0:m, n % NP_ if (KT * HPG) % NP_ == 0 else (n + (u_par(hg)) * 4) % NP_, :],
                               start=(kt == 0), stop=(kt == KT - 1), skip_group_check=True)
            mm.then_inc(pv_done, 1)

        def u_par(hg):
            return hg % 2

        def rows_pe(pe, b, hg, pair, n):
            t.wait_freed(pe, n - 1)
            pe.wait_ge(parts_ready, unit_of(b, hg) + 1)
            for jj in range(2):
                for qt in range(QT):
                    at = (jj * QT + qt) * P
                    mm = pe.transpose(misc16[SPLIT:SPLIT + MAXR, at:at + P], max_parts[:, qt, 2 * pair + jj, :],
                                      g.identb[:, :])
            mm.then_inc(t.misc_done, 1)

        def rows_act(act, b, hg, pair, n):
            act.wait_ge(t.misc_done, n)
            after(act, scored, (unit_of(b, hg) - HG + 1) * STEPS_B)
            act.activation(qx[SPLIT:SPLIT + MAXR, hg, 2 * pair:2 * pair + 2, :],
                           misc16[SPLIT:SPLIT + MAXR, :].rearrange("p (j t) -> p j t", j=2), ACT.Copy)\
               .then_inc(t.freed, 1)
            t.wait_freed(act, n)
            act.sem_inc(rows_set, 1)

        @block.tensor
        def _(pe):
            t.wait_loaded(pe)
            pe.wait_ge(const_ready, 1)
            for half in range(HALVES):
                first_scores(pe, 0, 0, half)
            for pair in range(2):
                rows_pe(pe, 0, 0, pair, pair + 1)

            def body(b, par, used):
                steps = plan(b)
                for hg in range(HG):
                    nb, nhg = later(b, hg, 1)
                    more = exists(nb, nhg)
                    half = 0
                    for kt in range(KT):
                        halves = HALVES_AT[kt] if more else 0
                        second_scores(pe, b, hg, kt, 0)
                        second_scores(pe, b, hg, kt, 1)
                        if halves:
                            first_scores(pe, nb, nhg, half)
                        if kt >= 1:
                            times_v(pe, b, hg, kt - 1)
                        elif hg >= 1:
                            times_v(pe, b, hg - 1, KT - 1)
                        for k in range(1, min(halves, 2)):
                            first_scores(pe, nb, nhg, half + k)
                        second_scores(pe, b, hg, kt, 2)
                        second_scores(pe, b, hg, kt, 3)
                        for k in range(2, halves):
                            first_scores(pe, nb, nhg, half + k)
                        half += halves
                        for step, n in steps[hg, kt]:
                            if step[0] == "rows":
                                rows_pe(pe, nb, nhg, step[1], n)
                            else:
                                t.pe(pe, step, b - 1, 1 - par, n)
                times_v(pe, b, HG - 1, KT - 1)
            over_batches(pe, body)
            for k, step in enumerate(TAIL_STEPS):
                t.pe(pe, step, B - 1, 1, after_last + k + 1)

        @block.scalar
        def _(act):
            def exps(b, hg, kt, j):
                n = unit_of(b, hg) * STEPS_B + kt * HPG + j
                m = P if kt < KT - 1 else KLAST
                act.wait_ge(scored, n + 1)
                if j == 0:
                    after(act, pv_done, unit_of(b, hg) * KT + kt - 1)
                at = (kt * HPG + j + u_par(hg) * 4) % NP_
                act.activation(probs[0:m, at, :], pB[j % 2][0:m, :], ACT.Exp).then_inc(exped, 1)

            def copy_o(b, par, hg):
                act.wait_ge(pv_done, (unit_of(b, hg) + 1) * KT)
                act.activation(t.oT[:, par, hg, :], pO[:, :], ACT.Copy).then_inc(t.o_copied, 1)

            for pair in range(2):
                rows_act(act, 0, 0, pair, pair + 1)

            def body(b, par, used):
                steps = plan(b)
                for hg in range(HG):
                    nb, nhg = later(b, hg, 1)
                    for kt in range(KT):
                        for j in range(HPG):
                            exps(b, hg, kt, j)
                            if kt == 0 and j == 1 and hg >= 1:
                                copy_o(b, par, hg - 1)
                        for step, n in steps[hg, kt]:
                            if step[0] == "rows":
                                rows_act(act, nb, nhg, step[1], n)
                            else:
                                t.act(act, step, b - 1, n)
                copy_o(b, par, HG - 1)
            over_batches(act, body)
            for k, step in enumerate(TAIL_STEPS):
                t.act(act, step, B - 1, after_last + k + 1)

        @block.vector
        def _(dve):
            made = sem("made")
            dve.memset(v[:, :, :, :, DK:VT], 1.0).then_inc(made, 1)
            dve.memset(kx[SPLIT:SPLIT + MAXR, :, :, :], 1.0).then_inc(made, 1)
            dve.wait_ge(made, 2)
            dve.sem_inc(const_ready, 1)
            t.wait_loaded(dve)

            def maxes(b, hg, half):
                u, tile, h = unit_of(b, hg), half // 2, half % 2
                j, qt = tile // QT, tile % QT
                dve.wait_ge(half_scored, u * HALVES + half + 1)
                if half == 0:
                    after(dve, max_chain, u * CHAIN)
                dve.tensor_reduce(half_max[:, qt, j, h:h + 1], pA[h][:, 0:HALF[h + 1] - HALF[h]], AX.X, ALU.max,
                                  negate=True).then_inc(half_maxed, 1)

            def split_max(b, hg):
                u = unit_of(b, hg)
                i = [0]

                def link(ins):
                    i[0] += 1
                    ins.then_inc(max_chain, 1)
                    dve.wait_ge(max_chain, u * CHAIN + i[0])
                dve.wait_ge(half_maxed, (u + 1) * HALVES)
                link(dve.tensor_reduce(negmax[:, 0, :], half_max[:, :, :, :].rearrange("p q j h -> p (q j) h"),
                                       AX.X, ALU.min))
                part = [max_parts[:, :, :, i].rearrange("p q j -> p (q j)") for i in range(MAXR)]
                after(dve, t.misc_done, rows_before(b, hg))
                link(dve.tensor_copy(part[0], negmax[:, 0, :]))
                link(dve.tensor_tensor(negmax[:, 1, :], negmax[:, 0, :], part[0], ALU.subtract))
                link(dve.tensor_copy(part[1], negmax[:, 1, :]))
                link(dve.tensor_tensor(negmax[:, 0, :], negmax[:, 1, :], part[1], ALU.subtract))
                link(dve.tensor_copy(part[2], negmax[:, 0, :]))
                dve.sem_inc(parts_ready, 1)

            def rows_before(b, hg):
                if isinstance(b, int) and b == 0 and hg == 0:
                    return 0
                if isinstance(b, int) and b == 0 and hg == 1:
                    return 2
                if hg >= 2:
                    rb, rhg = b, hg - 2
                else:
                    rb, rhg = b - 1, hg + 2
                return [n for step, n in plan(rb)[rhg, ROWS_AT] if step == ("rows", 1)][0]

            for half in range(HALVES):
                maxes(0, 0, half)
            split_max(0, 0)

            def body(b, par, used):
                steps = plan(b)
                for hg in range(HG):
                    nb, nhg = later(b, hg, 1)
                    more = exists(nb, nhg)
                    half = 0
                    for kt in range(KT):
                        if more:
                            for k in range(HALVES_AT[kt]):
                                maxes(nb, nhg, half)
                                half += 1
                                if half == HALVES:
                                    split_max(nb, nhg)
                        for step, n in steps[hg, kt]:
                            if step[0] != "rows":
                                t.dve(dve, step, b - 1, 1 - par, n)
                        if (hg, kt) == NORMALIZE_AT and not (isinstance(b, int) and b == 0):
                            t.dve_normalize(dve, b - 1)
            over_batches(dve, body)
            for k, step in enumerate(TAIL_STEPS):
                t.dve(dve, step, B - 1, 1, after_last + k + 1)
                if step == ("out", QT - 1):
                    t.dve_normalize(dve, B - 1)


NE, TOPK, HID = 8, 2, 512
HC = HID // P


def gates(nc, g, d, xT_in, gT):
    TT = B * QT
    with ExitStack() as ctx:
        sem, mem = Sems(nc, ctx, "ga"), Mem(nc, ctx, "ga")
        xT = mem.sb("xT", [P, KC, T])
        wg, bg = mem.sb("wg", [P, KC, NE]), mem.sb("bg", [NE, 1])
        lT = mem.sb("lT", [NE, T])
        logit, gate = mem.sb("logit", [P, TT, NE]), mem.sb("gate", [P, TT, NE])
        col, col2 = mem.sb("col", [P, TT]), mem.sb("col2", [P, TT])
        tri = mem.sb("tri", [P, NE, NE])
        more, atleast = mem.sb("more", [P, TT, NE, NE]), mem.sb("atleast", [P, TT, NE, NE])
        acc = mem.ps("acc", [P, 2, 512])
        turned = mem.ps("turned", [P, TT, NE])
        back = mem.ps("back", [P, 2, 512])
        w_loaded, loaded = sem("w_loaded"), sem("loaded", 4)
        product, copied, all_turned = sem("product"), sem("copied"), sem("all_turned")
        chain, shifted, exped, weights_ready, back_turned, back_copied, stored = (
            sem(n) for n in ("chain", "shifted", "exped", "weights_ready", "back_turned", "back_copied", "stored"))
        block = ctx.enter_context(nc.Block())

        @block.sync
        def _(sp):
            sp.dma_start(wg[:, :, :], w_in(d["L0_ffn_Wg"])).then_inc(w_loaded, 16)
            sp.dma_start(bg[:, :], d["L0_ffn_bg"].rearrange("(p a) -> p a", a=1)).then_inc(w_loaded, 16)
            sp.dma_start(tri[:, :, :], d["tri"]).then_inc(w_loaded, 16)
            for k in range(4):
                w = T // 4
                sp.dma_start(xT[:, :, k * w:(k + 1) * w], w_in(xT_in)[:, :, HALO + k * w:HALO + (k + 1) * w])\
                  .then_inc(loaded[k], 16)
            sp.wait_ge(back_copied, B)
            sp.dma_start(gT, lT[:, :]).then_inc(stored, 16)
            sp.wait_ge(stored, 16)

        @block.tensor
        def _(pe):
            pe.wait_ge(w_loaded, 48)
            for b in range(B):
                if b % 2 == 0:
                    pe.wait_ge(loaded[b // 2], 16)
                after(pe, copied, b - 1)
                for c in range(KC):
                    mm = pe.matmul(acc[0:NE, b % 2, :], wg[:, c, :], xT[:, c, b * S:(b + 1) * S],
                                   start=(c == 0), stop=(c == KC - 1))
                mm.then_inc(product, 1)
            for b in range(B):
                pe.wait_ge(copied, b + 1)
                for q in range(QT):
                    at = b * QT + q
                    mm = pe.transpose(turned[:, at, :], lT[:, at * P:(at + 1) * P], g.ident[0:NE, 0:NE])
            mm.then_inc(all_turned, 1)
            pe.wait_ge(weights_ready, 1)
            for b in range(B):
                after(pe, back_copied, b - 1)
                for q in range(QT):
                    mm = pe.transpose(back[0:NE, b % 2, q * P:(q + 1) * P], gate[:, b * QT + q, :], g.ident[:, :])
                mm.then_inc(back_turned, 1)

        @block.scalar
        def _(act):
            act.wait_ge(w_loaded, 48)
            for b in range(B):
                act.wait_ge(product, b + 1)
                act.activation(lT[:, b * S:(b + 1) * S], acc[0:NE, b % 2, :], ACT.Identity, bias=bg[:, :])\
                   .then_inc(copied, 1)
            act.wait_ge(shifted, 1)
            act.activation(gate[:, :, :], logit[:, :, :], ACT.Exp).then_inc(exped, 1)
            for b in range(B):
                act.wait_ge(back_turned, b + 1)
                act.activation(lT[:, b * S:(b + 1) * S], back[0:NE, b % 2, :], ACT.Copy).then_inc(back_copied, 1)

        @block.vector
        def _(dve):
            n = [0]

            def link(ins):
                n[0] += 1
                ins.then_inc(chain, 1)
                dve.wait_ge(chain, n[0])

            def spread(ap, axis, shape):
                return ap.rearrange("p t (a e) -> p t a e" if axis == 2 else "p t (e a) -> p t e a", a=1)\
                         .to_broadcast(shape)
            dve.wait_ge(all_turned, 1)
            link(dve.tensor_reduce(col[:, :], turned[:, :, :], AX.X, ALU.max))
            wide = [P, TT, NE]
            dve.tensor_tensor(logit[:, :, :], turned[:, :, :],
                              col[:, :].rearrange("p (t a) -> p t a", a=1).to_broadcast(wide), ALU.subtract)\
               .then_inc(shifted, 1)
            dve.wait_ge(exped, 1)
            link(dve.tensor_reduce(col2[:, :], gate[:, :, :], AX.X, ALU.add))
            link(dve.reciprocal(col[:, :], col2[:, :]))
            link(dve.tensor_tensor(gate[:, :, :], gate[:, :, :],
                                   col[:, :].rearrange("p (t a) -> p t a", a=1).to_broadcast(wide), ALU.mult))
            pairs = [P, TT, NE, NE]
            mine, other = spread(gate[:, :, :], 3, pairs), spread(gate[:, :, :], 2, pairs)
            link(dve.tensor_tensor(more[:, :, :, :], other, mine, ALU.is_gt))
            link(dve.tensor_tensor(atleast[:, :, :, :], other, mine, ALU.is_ge))
            link(dve.tensor_tensor(atleast[:, :, :, :], atleast[:, :, :, :], more[:, :, :, :], ALU.subtract))
            later = tri[:, :, :].rearrange("p (a e) f -> p a e f", a=1).to_broadcast(pairs)
            link(dve.tensor_tensor(atleast[:, :, :, :], atleast[:, :, :, :], later, ALU.mult))
            link(dve.tensor_tensor(atleast[:, :, :, :], atleast[:, :, :, :], more[:, :, :, :], ALU.add))
            link(dve.tensor_reduce(logit[:, :, :], atleast[:, :, :, :], AX.X, ALU.add))
            dve.scalar_tensor_tensor(out=gate[:, :, :], in0=logit[:, :, :], scalar=float(TOPK), in1=gate[:, :, :],
                                     op0=ALU.is_lt, op1=ALU.mult).then_inc(weights_ready, 1)


def experts(nc, g, d, xT_in, gT, xT_out):
    STEPS = NE * HC
    at_step = {}
    for q in range(QT):
        at_step[2 + 2 * q] = [("out", q)]
        at_step[16 + 2 * q] = [("turn", q)]
    NORMALIZE_AT = 12
    with ExitStack() as ctx:
        sem, mem = Sems(nc, ctx, "ex"), Mem(nc, ctx, "ex")
        mixT = mem.sb("mixT", [P, KC, S])
        wf = mem.sb("wf", [P, KC, D])
        t = Tail(nc, ctx, g, sem, mem, d, "L0_ffn_bf", xT_out,
                 terms=lambda par, k: [(mixT[:, c, k * P:(k + 1) * P], wf[:, c, :]) for c in range(KC)])
        w1, w3 = mem.sb("w1", [P, NE, KC, HID]), mem.sb("w3", [P, NE, KC, HID])
        w2 = mem.sb("w2", [P, NE, HC, D])
        b1, b3 = mem.sb("b1", [P, NE, HC]), mem.sb("b3", [P, NE, HC])
        b2 = mem.sb("b2", [NE, D])
        one_of = mem.sb("one_of", [NE, NE, P])
        xT = mem.sb("xT", [P, 2, KC, S])
        gate = mem.sb("gate", [NE, 2, S])
        h1 = mem.sb("h1", [P, 2, S])
        u = mem.sb("u", [P, 2, S])
        hid = mem.sb("hid", [P, 2, S])
        p1 = [mem.ps(f"p1_{k}", [P, 512]) for k in range(2)]
        p3 = [mem.ps(f"p3_{k}", [P, 512]) for k in range(2)]
        pg, pm = mem.ps("pg", [P, 512]), [mem.ps(f"pm{k}", [P, 512]) for k in range(KC)]
        w_loaded, x_loaded = sem("w_loaded", NE), sem("x_loaded", 2)
        s_loaded = sem("s_loaded")
        p1_done, p3_done, h1_ready, u_ready, silu_ready, hid_ready, mixed, gate_spread, batch_mixed, mix_copied = (
            sem(n) for n in ("p1_done", "p3_done", "h1_ready", "u_ready", "silu_ready", "hid_ready", "mixed",
                             "gate_spread", "batch_mixed", "mix_copied"))
        block = ctx.enter_context(nc.Block())

        def is_first(b):
            return isinstance(b, int) and b == 0

        def plan(b):
            n, k, out = (b - 1) * len(PLAIN_STEPS), 0, []
            for s in range(STEPS):
                row = []
                for step in ([] if is_first(b) else at_step.get(s, [])):
                    k += 1
                    row.append((step, n + k))
                out.append(row)
            return out
        after_last = (B - 1) * len(PLAIN_STEPS)

        @block.sync
        def _(sp):
            sp.dma_start(xT[:, 0, :, :], w_in(xT_in)[:, :, HALO:HALO + S]).then_inc(x_loaded[0], 16)
            sp.dma_start(gate[:, 0, :], gT[:, 0:S]).then_inc(x_loaded[0], 16)
            sp.dma_start(b1[:, :, :], d["L0_ffn_b1"].rearrange("e (c p) -> p e c", p=P), allow_slow_non_contiguous=True).then_inc(s_loaded, 16)
            sp.dma_start(b3[:, :, :], d["L0_ffn_b3"].rearrange("e (c p) -> p e c", p=P), allow_slow_non_contiguous=True).then_inc(s_loaded, 16)
            sp.dma_start(b2[:, :], d["L0_ffn_b2"]).then_inc(s_loaded, 16)
            sp.dma_start(one_of[:, :, :], d["one_of"]).then_inc(s_loaded, 16)
            sp.dma_start(wf[:, :, :], w_in(d["L0_ffn_Wf"])).then_inc(s_loaded, 16)
            t.load(sp)
            for e in range(NE):
                sp.dma_start(w1[:, e, :, :], w_in(d["L0_ffn_W1"][e])).then_inc(w_loaded[e], 16)
                sp.dma_start(w3[:, e, :, :], w_in(d["L0_ffn_W3"][e])).then_inc(w_loaded[e], 16)
                sp.dma_start(w2[:, e, :, :], w_in(d["L0_ffn_W2"][e])).then_inc(w_loaded[e], 16)

            def body(b, par, used):
                if isinstance(b, int) and b == B - 1:
                    return
                after(sp, batch_mixed, b)
                sp.dma_start(xT[:, 1 - par, :, :], w_in(xT_in)[:, :, bass.ds(b * S + (HALO + S), S)]).then_inc(x_loaded[1 - par], 16)
                sp.dma_start(gate[:, 1 - par, :], gT[:, bass.ds(b * S + S, S)]).then_inc(x_loaded[1 - par], 16)
            over_batches(sp, body)

        @block.tensor
        def _(pe):
            pe.wait_ge(s_loaded, 80)
            t.wait_loaded(pe)

            def mix(b, s):
                e, hc = s // HC, s % HC
                pe.wait_ge(hid_ready, b * STEPS + s + 1)
                if s == 0:
                    after(pe, mix_copied, b)
                for oc in range(KC):
                    mm = pe.matmul(pm[oc][:, :], w2[:, e, hc, oc * P:(oc + 1) * P], hid[:, s % 2, :],
                                   start=(s == 0), stop=False)
                mm.then_inc(mixed, 1)

            def body(b, par, used):
                pe.wait_ge(x_loaded[par], used * 32 + 32)
                for s, steps in enumerate(plan(b)):
                    e, hc = s // HC, s % HC
                    if is_first(b) and hc == 0:
                        pe.wait_ge(w_loaded[e], 48)
                    for w, p, free, done in ((w1, p1, h1_ready, p1_done), (w3, p3, u_ready, p3_done)):
                        after(pe, free, b * STEPS + s - 1)
                        for c in range(KC):
                            mm = pe.matmul(p[s % 2][:, :], w[:, e, c, hc * P:(hc + 1) * P], xT[:, par, c, :],
                                           start=(c == 0), stop=(c == KC - 1))
                        mm.then_inc(done, 1)
                    if s >= 1:
                        mix(b, s - 1)
                    if hc == 0:
                        if s == 0:
                            after(pe, hid_ready, b * STEPS)
                        pe.matmul(pg[:, :], one_of[:, e, :], gate[:, par, :], start=True, stop=True)\
                          .then_inc(gate_spread, 1)
                    for step, n in steps:
                        t.pe(pe, step, b - 1, 1 - par, n)
                mix(b, STEPS - 1)
                for oc in range(KC):
                    mm = pe.matmul(pm[oc][:, :], b2[:, oc * P:(oc + 1) * P], gate[:, par, :], start=False, stop=True)
                mm.then_inc(batch_mixed, 1)
            over_batches(pe, body)
            for k, step in enumerate(PLAIN_STEPS):
                if k == 0:
                    pe.wait_ge(mix_copied, B)
                t.pe(pe, step, B - 1, 1, after_last + k + 1)

        @block.scalar
        def _(act):
            act.wait_ge(s_loaded, 80)

            def body(b, par, used):
                for s, steps in enumerate(plan(b)):
                    e, hc = s // HC, s % HC
                    n = b * STEPS + s
                    act.wait_ge(p1_done, n + 1)
                    after(act, u_ready, n - 1)
                    act.activation(h1[:, s % 2, :], p1[s % 2][:, :], ACT.Identity, bias=b1[:, e, hc:hc + 1])\
                       .then_inc(h1_ready, 1)
                    act.wait_ge(u_ready, n + 1)
                    act.activation(u[:, s % 2, :], u[:, s % 2, :], ACT.Silu).then_inc(silu_ready, 1)
                    for step, k in steps:
                        t.act(act, step, b - 1, k)
                act.wait_ge(batch_mixed, b + 1)
                for oc in range(KC):
                    ins = act.activation(mixT[:, oc, :], pm[oc][:, :], ACT.Copy)
                ins.then_inc(mix_copied, 1)
            over_batches(act, body)
            for k, step in enumerate(PLAIN_STEPS):
                t.act(act, step, B - 1, after_last + k + 1)

        @block.vector
        def _(dve):
            dve.wait_ge(s_loaded, 80)
            t.wait_loaded(dve)

            def body(b, par, used):
                for s, steps in enumerate(plan(b)):
                    e, hc = s // HC, s % HC
                    n = b * STEPS + s
                    dve.wait_ge(p3_done, n + 1)
                    dve.wait_ge(h1_ready, n + 1)
                    after(dve, hid_ready, n - 1)
                    dve.scalar_tensor_tensor(out=u[:, s % 2, :], in0=p3[s % 2][:, :], scalar=b3[:, e, hc:hc + 1],
                                             in1=h1[:, s % 2, :], op0=ALU.add, op1=ALU.mult).then_inc(u_ready, 1)
                    if hc == 0:
                        dve.wait_ge(gate_spread, b * NE + e + 1)
                    dve.wait_ge(silu_ready, n + 1)
                    after(dve, mixed, n - 1)
                    dve.tensor_tensor(hid[:, s % 2, :], u[:, s % 2, :], pg[:, :], ALU.mult).then_inc(hid_ready, 1)
                    for step, k in steps:
                        t.dve(dve, step, b - 1, 1 - par, k)
                    if s == NORMALIZE_AT and not is_first(b):
                        t.dve_normalize(dve, b - 1)
            over_batches(dve, body)
            for k, step in enumerate(PLAIN_STEPS):
                t.dve(dve, step, B - 1, 1, after_last + k + 1)
                if step == ("out", QT - 1):
                    t.dve_normalize(dve, B - 1)

        @block.gpsimd
        def _(pool):
            t.begin(pool)
            with pool.Fori(0, B) as b:
                t.pool(pool, b, b * len(PLAIN_STEPS) + len(PLAIN_STEPS))
            t.finish(pool)


NQ = D // 4
BQ = QT * NQ


def quat_products(eng, M, a, k, comps, done):
    for c in comps:
        ins = eng.tensor_tensor(M[:, c, :, :], a, k[:, :, c:c + 1].to_broadcast([P, BQ, 4]), ALU.mult)
    ins.then_inc(done, 1)


def quat_combine(dve, chain, out, M, conj, last):
    plus, minus = (ALU.subtract, ALU.add) if conj else (ALU.add, ALU.subtract)
    dve.tensor_tensor(out[:, :, 1:3], M[:, 0, :, 1:3], M[:, 1, :, 0:4:3], plus)
    chain.link(dve.tensor_tensor(out[:, :, 0:4:3], M[:, 0, :, 0:4:3], M[:, 1, :, 1:3], minus))
    dve.tensor_tensor(out[:, :, 0:2], out[:, :, 0:2], M[:, 2, :, 2:4], minus)
    chain.link(dve.tensor_tensor(out[:, :, 2:4], out[:, :, 2:4], M[:, 2, :, 0:2], plus))
    for c, op in ((0, minus), (1, plus), (2, minus)):
        dve.tensor_tensor(out[:, :, c], out[:, :, c], M[:, 3, :, 3 - c], op)
    dve.tensor_tensor(out[:, :, 3], out[:, :, 3], M[:, 3, :, 0], plus).then_inc(last, 1)


def bind(nc, d, xT_in, khat, bound):
    with ExitStack() as ctx:
        sem, mem = Sems(nc, ctx, "qb"), Mem(nc, ctx, "qb")
        w, bias = mem.sb("w", [P, KC, 2, D]), mem.sb("bias", [P, 2, D])
        xT = mem.sb("xT", [P, 2, KC, S])
        kv = mem.sb("kv", [P, 2, QT, 2, D])
        sq, ss, nrm, inv = mem.sb("sq", [P, BQ, 4]), mem.sb("ss", [P, BQ]), mem.sb("nrm", [P, BQ]), mem.sb("inv", [P, BQ])
        M = mem.sb("M", [P, 4, BQ, 4])
        acc = mem.ps("acc", [P, QT, 2, D])
        w_loaded, x_loaded = sem("w_loaded"), sem("x_loaded", 2)
        kv_done, kv_ready, sq_ready, ss_ready, nrm_ready, inv_ready, kh_ready, pool_products, own, bound_ready = (
            sem(n) for n in ("kv_done", "kv_ready", "sq_ready", "ss_ready", "nrm_ready", "inv_ready", "kh_ready",
                             "pool_products", "own", "bound_ready"))
        block = ctx.enter_context(nc.Block())

        def of(tensor, b):
            return tensor[:, bass.ds(b * BQ, BQ), :]

        def keys(par):
            return kv[:, par, :, 0, :].rearrange("p t (n c) -> p t n c", c=4)

        def values(par):
            return kv[:, par, :, 1, :].rearrange("p t (n c) -> p t n c", c=4)

        @block.sync
        def _(sp):
            sp.dma_start(w[:, :, 0, :], w_in(d["L1_attn_WkT"])).then_inc(w_loaded, 16)
            sp.dma_start(w[:, :, 1, :], w_in(d["L1_attn_WvT"])).then_inc(w_loaded, 16)
            for k, n in enumerate(("bk", "bv")):
                sp.dma_start(bias[:, k, :], d["L1_attn_" + n].rearrange("(a n) -> a n", a=1).to_broadcast([P, D]))\
                  .then_inc(w_loaded, 16)

            def body(b, par, used):
                after(sp, kv_done, (b - 1) * QT + 1)
                sp.dma_start(xT[:, par, :, :], w_in(xT_in)[:, :, bass.ds(b * S + HALO, S)]).then_inc(x_loaded[par], 16)
            over_batches(sp, body)

        @block.tensor
        def _(pe):
            pe.wait_ge(w_loaded, 64)

            def body(b, par, used):
                pe.wait_ge(x_loaded[par], used * 16 + 16)
                for q in range(QT):
                    after(pe, kv_ready, (b - 1) * QT + q + 1)
                    for c in range(KC):
                        mm = pe.matmul(acc[:, q, :, :], xT[:, par, c, q * P:(q + 1) * P], w[:, c, :, :],
                                       start=(c == 0), stop=(c == KC - 1))
                    mm.then_inc(kv_done, 1)
            over_batches(pe, body)

        @block.scalar
        def _(act):
            def body(b, par, used):
                act.wait_ge(kv_ready, b * QT + QT)
                after(act, ss_ready, b)
                act.activation(sq[:, :, :].rearrange("p (t n) c -> p t n c", t=QT), keys(par), ACT.Square)\
                   .then_inc(sq_ready, 1)
                act.wait_ge(ss_ready, b + 1)
                after(act, inv_ready, b)
                act.activation(nrm[:, :], ss[:, :], ACT.Sqrt).then_inc(nrm_ready, 1)
            over_batches(act, body)

        @block.vector
        def _(dve):
            chain = Chain(dve, own, 3)
            dve.wait_ge(w_loaded, 64)

            def products(b, par):
                dve.wait_ge(kh_ready, b + 1)
                for c in (0, 1):
                    ins = dve.tensor_tensor(M[:, c, :, :].rearrange("p (t n) c -> p t n c", t=QT), values(par),
                                            of(khat, b)[:, :, c:c + 1].rearrange("p (t n) c -> p t n c", t=QT)
                                            .to_broadcast([P, QT, NQ, 4]), ALU.mult)
                chain.link(ins)
                dve.wait_ge(pool_products, b + 2)
                quat_combine(dve, chain, of(bound, b), M, False, bound_ready)
                dve.wait_ge(bound_ready, b + 1)

            def body(b, par, used):
                for q in range(QT):
                    dve.wait_ge(kv_done, b * QT + q + 1)
                    after(dve, pool_products, b)
                    dve.tensor_tensor(kv[:, par, q, :, :], acc[:, q, :, :], bias[:, :, :], ALU.add).then_inc(kv_ready, 1)
                dve.wait_ge(sq_ready, b + 1)
                after(dve, nrm_ready, b)
                dve.tensor_reduce(ss[:, :], sq[:, :, :], AX.X, ALU.add).then_inc(ss_ready, 1)
                if not (isinstance(b, int) and b == 0):
                    chain.start(b - 1)
                    products(b - 1, 1 - par)
                    chain.end()
                dve.wait_ge(nrm_ready, b + 1)
                after(dve, kh_ready, b)
                dve.tensor_scalar(inv[:, :], nrm[:, :], 1e-12, None, ALU.max).then_inc(maxed, 1)
                dve.wait_ge(maxed, b + 1)
                dve.reciprocal(inv[:, :], inv[:, :]).then_inc(inv_ready, 1)
            maxed = sem("maxed")
            over_batches(dve, body)
            chain.start(B - 1)
            products(B - 1, 1)

        @block.gpsimd
        def _(pool):
            pool.sem_inc(pool_products, 1)

            def body(b, par, used):
                pool.wait_ge(inv_ready, b + 1)
                pool.tensor_tensor(of(khat, b).rearrange("p (t n) c -> p t n c", t=QT), keys(par),
                                   inv[:, :].rearrange("p (t n a) -> p t n a", t=QT, a=1).to_broadcast([P, QT, NQ, 4]),
                                   ALU.mult).then_inc(kh_ready, 1)
                pool.wait_ge(kh_ready, b + 1)
                after(pool, bound_ready, b)
                for c in (2, 3):
                    ins = pool.tensor_tensor(M[:, c, :, :].rearrange("p (t n) c -> p t n c", t=QT), values(par),
                                             of(khat, b)[:, :, c:c + 1].rearrange("p (t n) c -> p t n c", t=QT)
                                             .to_broadcast([P, QT, NQ, 4]), ALU.mult)
                ins.then_inc(pool_products, 1)
            over_batches(pool, body)


def retrieve(nc, g, d, khat, bound, xT_out):
    with ExitStack() as ctx:
        sem, mem = Sems(nc, ctx, "qr"), Mem(nc, ctx, "qr")
        nT = mem.sb("nT", [P, KC, S])
        wo = mem.sb("wo", [P, KC, D])
        t = Tail(nc, ctx, g, sem, mem, d, True, xT_out, factor=2.0,
                 terms=lambda par, k: [(nT[:, c, k * P:(k + 1) * P], wo[:, c, :]) for c in range(KC)])
        ln_g, ln_b = mem.sb("ln_g", [P, KC]), mem.sb("ln_b", [P, KC])
        ln_b_cols, bo = mem.sb("ln_b_cols", [P, KC, P]), mem.sb("bo_row", [P, D])
        upper, ones, root = mem.sb("upper", [P, P]), mem.sb("ones", [P, P]), mem.sb("root", [P, QT])
        memory = mem.sb("memory", [P, 2, BQ, 4])
        M = mem.sb("M", [P, 4, BQ, 4])
        ret = mem.sb("ret", [P, BQ, 4])
        scaled, normed = mem.sb("scaled", [P, QT, D]), mem.sb("normed", [P, QT, D])
        st, mv = mem.sb("st", [P, QT, 6]), mem.sb("mv1", [P, QT, 2])
        veps, rstd = mem.sb("veps1", [P, QT]), mem.sb("rstd1", [P, QT])
        sums, pn = mem.ps("sums", [P, QT, D]), mem.ps("pn", [P, KC, S])
        c_loaded, row_ready, const_ready = sem("c_loaded"), sem("row_ready"), sem("const_ready")
        summed, mem_copied, pool_products, own, ret_ready, scaled_ready, var_ready, rstd_ready, normed_ready, turned, nT_ready = (
            sem(n) for n in ("summed", "mem_copied", "pool_products", "own", "ret_ready", "scaled_ready", "var1_ready",
                             "rstd1_ready", "normed_ready", "turned", "nT_ready"))
        block = ctx.enter_context(nc.Block())

        def of(tensor, b):
            return tensor[:, bass.ds(b * BQ, BQ), :]

        def is_first(b):
            return isinstance(b, int) and b == 0

        def number(b, i):
            return (b - 1) * len(PLAIN_STEPS) + i + 1

        @block.sync
        def _(sp):
            sp.dma_start(wo[:, :, :], w_in(d["L1_attn_WoT"])).then_inc(c_loaded, 16)
            sp.dma_start(ln_g[:, :], d["L1_attn_ln_g"].rearrange("(c p) -> p c", p=P), allow_slow_non_contiguous=True).then_inc(c_loaded, 16)
            sp.dma_start(ln_b[:, :], d["L1_attn_ln_b"].rearrange("(c p) -> p c", p=P), allow_slow_non_contiguous=True).then_inc(c_loaded, 16)
            sp.dma_start(bo[:, :], d["L1_attn_bo"].rearrange("(a n) -> a n", a=1).to_broadcast([P, D])).then_inc(c_loaded, 16)
            sp.dma_start(upper[:, :], d["upper"]).then_inc(c_loaded, 16)
            sp.dma_start(root[:, :], d["root"]).then_inc(c_loaded, 16)

        def running_sum(pe, b):
            after(pe, mem_copied, b)
            for q in range(QT):
                for k in range(q + 1):
                    mm = pe.matmul(sums[:, q, :], (upper if k == q else ones)[:, :],
                                   bound[:, bass.ds(b * BQ + k * NQ, NQ), :].rearrange("p n c -> p (n c)"),
                                   start=(k == 0), stop=(k == q))
            mm.then_inc(summed, 1)

        def more(b):
            return not (isinstance(b, int) and b == B - 1)

        @block.tensor
        def _(pe):
            pe.wait_ge(const_ready, 1)
            for c in range(KC):
                mm = pe.matmul(pn[:, 0, 0:D], ln_b_cols[:, c, :], wo[:, c, :], start=(c == 0), stop=(c == KC - 1))
            mm.then_inc(row_ready, 1)
            pe.wait_ge(const_ready, 2)
            running_sum(pe, 0)

            def body(b, par, used):
                if not is_first(b):
                    pe.wait_ge(nT_ready, b)
                    for i in range(QT):
                        t.pe(pe, PLAIN_STEPS[i], b - 1, 0, number(b, i))
                if more(b):
                    running_sum(pe, b + 1)
                if not is_first(b):
                    for i in range(QT, 2 * QT):
                        t.pe(pe, PLAIN_STEPS[i], b - 1, 0, number(b, i))
                pe.wait_ge(normed_ready, b * QT + QT)
                after(pe, nT_ready, b)
                for q in range(QT):
                    for c in range(KC):
                        mm = pe.transpose(pn[:, c, q * P:(q + 1) * P], normed[:, q, c * P:(c + 1) * P], g.ident[:, :])
                mm.then_inc(turned, 1)
            over_batches(pe, body)
            pe.wait_ge(nT_ready, B)
            for i, step in enumerate(PLAIN_STEPS):
                t.pe(pe, step, B - 1, 0, number(B, i))

        @block.scalar
        def _(act):
            def copy_memory(b, par):
                act.wait_ge(summed, b + 1)
                after(act, pool_products, b - 1)
                after(act, ret_ready, b - 1)
                act.activation(memory[:, par, :, :], sums[:, :, :].rearrange("p t (n c) -> p (t n) c", c=4), ACT.Copy)\
                   .then_inc(mem_copied, 1)
            act.wait_ge(c_loaded, 96)
            copy_memory(0, 0)

            def body(b, par, used):
                if more(b):
                    copy_memory(b + 1, 1 - par)
                if not is_first(b):
                    for i in range(QT, 2 * QT):
                        t.act(act, PLAIN_STEPS[i], b - 1, number(b, i))
                act.wait_ge(ret_ready, b + 1)
                after(act, normed_ready, b * QT)
                for q in range(QT):
                    act.activation(scaled[:, q, :], ret[:, q * NQ:(q + 1) * NQ, :].rearrange("p n c -> p (n c)"),
                                   ACT.Copy, scale=root[:, q:q + 1]).then_inc(scaled_ready, 1)
                act.wait_ge(turned, b + 1)
                act.activation(nT[:, :, :], pn[:, :, :], ACT.Copy).then_inc(nT_ready, 1)
            over_batches(act, body)
            for i in range(QT, 2 * QT):
                t.act(act, PLAIN_STEPS[i], B - 1, number(B, i))

        @block.vector
        def _(dve):
            made = sem("made")
            dve.wait_ge(c_loaded, 96)
            dve.memset(ones[:, :], 1.0).then_inc(made, 1)
            dve.wait_ge(made, 1)
            for c in range(KC):
                dve.tensor_scalar(ln_b_cols[:, c, :], ones[:, :], ln_b[:, c:c + 1], None, ALU.mult).then_inc(made, 1)
            dve.wait_ge(made, 1 + KC)
            dve.sem_inc(const_ready, 1)
            dve.wait_ge(row_ready, 1)
            dve.tensor_tensor(t.bo[:, :], pn[:, 0, 0:D], bo[:, :], ALU.add).then_inc(made, 1)
            for c in range(KC):
                dve.tensor_scalar(wo[:, c, :], wo[:, c, :], ln_g[:, c:c + 1], None, ALU.mult).then_inc(made, 1)
            dve.wait_ge(made, 2 + 2 * KC)
            dve.sem_inc(const_ready, 1)
            chain = Chain(dve, own, 3 + 2 * QT)

            def body(b, par, used):
                chain.start(b)
                dve.wait_ge(mem_copied, b + 1)
                for c in (0, 1):
                    ins = dve.tensor_tensor(M[:, c, :, :], memory[:, par, :, :],
                                            of(khat, b)[:, :, c:c + 1].to_broadcast([P, BQ, 4]), ALU.mult)
                chain.link(ins)
                if not is_first(b):
                    for i in range(QT):
                        t.dve(dve, PLAIN_STEPS[i], b - 1, 0, number(b, i))
                dve.wait_ge(pool_products, b + 1)
                after(dve, scaled_ready, b * QT)
                quat_combine(dve, chain, ret, M, True, ret_ready)
                if not is_first(b):
                    t.dve_normalize(dve, b - 1)
                for q in range(QT):
                    dve.wait_ge(scaled_ready, b * QT + q + 1)
                    chain.link(dve.bn_stats(st[:, q, :], scaled[:, q, :]))
                    dve.sem_inc(t.passed, 1)
                    chain.link(dve.bn_aggr(mv[:, q, :], st[:, q, :]))
                chain.end()
                dve.tensor_scalar(veps[:, :], mv[:, :, 1], EPS, None, ALU.add).then_inc(var_ready, 1)
                dve.wait_ge(rstd_ready, b + 1)
                after(dve, turned, b)
                for q in range(QT):
                    dve.tensor_scalar(normed[:, q, :], scaled[:, q, :], mv[:, q, 0:1], rstd[:, q:q + 1],
                                      ALU.subtract, ALU.mult).then_inc(normed_ready, 1)
                dve.wait_ge(normed_ready, b * QT + QT)
            over_batches(dve, body)
            for i, step in enumerate(PLAIN_STEPS[:QT]):
                t.dve(dve, step, B - 1, 0, number(B, i))
            t.dve_normalize(dve, B - 1)

        @block.gpsimd
        def _(pool):
            t.begin(pool)
            def body(b, par, used):
                pool.wait_ge(mem_copied, b + 1)
                after(pool, ret_ready, b)
                for c in (2, 3):
                    ins = pool.tensor_tensor(M[:, c, :, :], memory[:, par, :, :],
                                             of(khat, b)[:, :, c:c + 1].to_broadcast([P, BQ, 4]), ALU.mult)
                ins.then_inc(pool_products, 1)
                if not is_first(b):
                    t.pool(pool, b - 1, number(b, 2 * QT - 1))
                pool.wait_ge(var_ready, b + 1)
                after(pool, normed_ready, b * QT)
                pool.tensor_tensor(rstd[:, :], veps[:, :], g.halfneg[:, :], ALU.pow).then_inc(rstd_ready, 1)
            over_batches(pool, body)
            t.pool(pool, B - 1, number(B, 2 * QT - 1))
            t.finish(pool)


def context_attention(nc, g, d, xT_in, xT_out):
    GROUPS = [range(k, min(k + 4, KT)) for k in range(0, KT, 4)]
    slots = [[("ct", -1, 2), ("q", 1, 0), ("q", 1, 1), ("k", 1, 0)],
             [("ct", -1, 3), ("v", -1, 0), ("v", -1, 1), ("k", 1, 1)],
             [("ct", 0, 0)] + [("out", -1, q) for q in range(QT)],
             [("ct", 0, 1)] + [("turn", -1, q) for q in range(QT)]]
    EPILOGUE = [("ct", -1, 2), ("ct", -1, 3), ("v", -1, 0), ("v", -1, 1)] + \
               [("out", -1, q) for q in range(QT)] + [("turn", -1, q) for q in range(QT)]
    per_batch = sum(len(s) for s in slots)
    AHEAD = 2 * KC
    in_first = sum(rel >= 0 for s in slots for _, rel, _ in s)

    def is_first(b):
        return isinstance(b, int) and b == 0

    def plan(b):
        first, last = is_first(b), isinstance(b, int) and b == B - 1
        n = AHEAD if first else AHEAD + in_first + (b - 1) * per_batch
        out, i = [], 0
        for slot in slots:
            row = []
            for step in slot:
                if not (first and step[1] < 0) and not (last and step[1] > 0):
                    i += 1
                    row.append((step, n + i))
            out.append(row)
        return out

    after_last = AHEAD + in_first + (B - 2) * per_batch + per_batch - AHEAD
    with ExitStack() as ctx:
        sem, mem = Sems(nc, ctx, "cx"), Mem(nc, ctx, "cx")
        vT, wo = mem.sb("vT", [P, KC, S]), mem.sb("wo", [P, KC, D])
        t = Tail(nc, ctx, g, sem, mem, d, "L1_xattn_bo", xT_out,
                 terms=lambda par, k: [(vT[:, c, k * P:(k + 1) * P], wo[:, c, :]) for c in range(KC)])
        wq, wk, wv = (mem.sb(n, [P, KC, D]) for n in ("wq", "wk", "wv"))
        bq, bv = mem.sb("bq", [P, KC]), mem.sb("bv", [P, KC])
        xT, cT = mem.sb("xT", [P, 2, KC, S]), mem.sb("cT", [P, 2, KC, C])
        cn = mem.sb("cn", [P, 2, KT, D])
        q1, qk = mem.sb("q1", [P, KC, S]), mem.sb("qk", [P, 2, KC, S])
        probs, pT = mem.sb("probs", [P, 2, C]), mem.sb("pT", [P, KT, P])
        negmax, den, inv = mem.sb("negmax", [P, 2]), mem.sb("den", [P, 2]), mem.sb("inv", [P, 2])
        mixed, mixT = mem.sb("mixed", [P, 2, D]), mem.sb("mixT", [P, 2, KC, S])
        pS = mem.ps("pS", [P, 2048])
        pt = [mem.ps(f"pt{k}", [P, 512]) for k in range(2)]
        pO = mem.ps("pO", [P, 512])
        c_loaded, w_ready = sem("wc_loaded"), sem("w_ready")
        x_loaded, k_loaded = sem("x_loaded", 2), sem("k_loaded", 2)
        scored, max_ready, exped, inv_ready, turned, copied_even, copied_odd, summed, mixed_ready = (
            sem(n) for n in ("scored", "max_ready", "exped", "inv_ready", "turned", "copied_even", "copied_odd",
                             "summed", "mixed_ready"))
        block = ctx.enter_context(nc.Block())
        NG = len(GROUPS)

        @block.sync
        def _(sp):
            for w, n in ((wq, "WqT"), (wk, "Wk"), (wv, "WvT"), (wo, "WoT")):
                sp.dma_start(w[:, :, :], w_in(d["L1_xattn_" + n])).then_inc(c_loaded, 16)
            for v, n in ((bq, "bq"), (bv, "bv")):
                sp.dma_start(v[:, :], d["L1_xattn_" + n].rearrange("(c p) -> p c", p=P), allow_slow_non_contiguous=True).then_inc(c_loaded, 16)
            t.load(sp)

            def load_x(b, par):
                sp.dma_start(xT[:, par, :, :], w_in(xT_in)[:, :, bass.ds(b * S + HALO, S)]).then_inc(x_loaded[par], 16)

            def load(b, par):
                sp.dma_start(cT[:, par, :, :], w_in(d["cT"])[:, :, bass.ds(b * C, C)]).then_inc(k_loaded[par], 16)
                full = (KT - 1) * P
                rows = d["ctx"]
                sp.dma_start(cn[:, par, 0:KT - 1, :], rows[bass.ds(b * C, full), :].rearrange("(t p) n -> p t n", p=P))\
                  .then_inc(k_loaded[par], 16)
                sp.dma_start(cn[0:KLAST, par, KT - 1, :], rows[bass.ds(b * C + full, KLAST), :]).then_inc(k_loaded[par], 16)
            load_x(0, 0)
            load(0, 0)

            def body(b, par, used):
                if not (isinstance(b, int) and b == B - 1):
                    after(sp, summed, (b - 1) * QT + 1)
                    load_x(b + 1, 1 - par)
                    after(sp, summed, b * QT)
                    load(b + 1, 1 - par)
            over_batches(sp, body)

        def misc_pe(pe, step, b, par, n):
            what, rel, k = step
            if what in ("out", "turn"):
                return t.pe(pe, (what, k), b + rel, 0, n)
            t.wait_freed(pe, n - 1)
            own = par if rel == 0 else 1 - par
            if what == "q":
                if k == 0:
                    pe.wait_ge(x_loaded[own], x_count(b, par) * 16)
                for c in range(KC):
                    mm = pe.matmul(t.misc[:, :], wq[:, c, k * P:(k + 1) * P], xT[:, own, c, :], start=(c == 0), stop=(c == KC - 1))
            elif what == "k":
                for c in range(KC):
                    mm = pe.matmul(t.misc[:, :], wk[:, c, k * P:(k + 1) * P], q1[:, c, :], start=(c == 0), stop=(c == KC - 1))
            elif what == "v":
                for c in range(KC):
                    mm = pe.matmul(t.misc[:, :], wv[:, c, k * P:(k + 1) * P], mixT[:, own, c, :], start=(c == 0), stop=(c == KC - 1))
            else:
                pe.wait_ge(mixed_ready, (b + rel) * QT + k + 1)
                for c in range(KC):
                    mm = pe.transpose(t.misc[:, c * P:(c + 1) * P], mixed[:, k % 2, c * P:(c + 1) * P], g.ident[:, :])
            mm.then_inc(t.misc_done, 1)

        used_of = {}

        def x_count(b, par):
            return used_of["used"] + 1 + par

        def misc_act(act, step, b, par, n):
            what, rel, k = step
            if what in ("out", "turn"):
                return t.act(act, (what, k), b + rel, n)
            own = par if rel == 0 else 1 - par
            act.wait_ge(t.misc_done, n)
            if what == "q":
                ins = act.activation(q1[:, k, :], t.misc[:, :], ACT.Identity, bias=bq[:, k:k + 1])
            elif what == "k":
                ins = act.activation(qk[:, own, k, :], t.misc[:, :], ACT.Copy)
            elif what == "v":
                ins = act.activation(vT[:, k, :], t.misc[:, :], ACT.Identity, bias=bv[:, k:k + 1])
            else:
                ins = act.activation(mixT[:, own, :, k * P:(k + 1) * P], t.misc[:, 0:D].rearrange("p (c t) -> p c t", c=KC), ACT.Copy)
            ins.then_inc(t.freed, 1)

        def scores(pe, b, par, q):
            after(pe, exped, b * QT + q)
            if q == 0:
                pe.wait_ge(k_loaded[par], used_of["used"] * 48 + 48)
                if is_first(b):
                    t.wait_freed(pe, AHEAD)
            for at in range(0, C, 512):
                w = min(512, C - at)
                for c in range(KC):
                    mm = pe.matmul(pS[:, at:at + w], qk[:, par, c, q * P:(q + 1) * P], cT[:, par, c, at:at + w],
                                   start=(c == 0), stop=(c == KC - 1))
            mm.then_inc(scored, 1)

        def turn(pe, b, q, gi):
            unit = b * QT + q
            if gi == 0:
                pe.wait_ge(exped, unit + 1)
            after(pe, copied_odd if gi % 2 else copied_even, unit * 2 + gi // 2)
            for i, kt in enumerate(GROUPS[gi]):
                w = P if kt < KT - 1 else KLAST
                mm = pe.transpose(pt[gi % 2][0:w, i * P:(i + 1) * P], probs[:, q % 2, kt * P:kt * P + w], g.ident[:, :])
            mm.then_inc(turned, 1)

        def sum_up(pe, b, par, q):
            unit = b * QT + q
            after(pe, mixed_ready, unit)
            for gi, tiles in enumerate(GROUPS):
                pe.wait_ge(copied_odd if gi % 2 else copied_even, unit * 2 + gi // 2 + 1)
                for kt in tiles:
                    m = P if kt < KT - 1 else KLAST
                    mm = pe.matmul(pO[:, 0:D], pT[0:m, kt, :], cn[0:m, par, kt, :], start=(kt == 0), stop=(kt == KT - 1))
            mm.then_inc(summed, 1)

        def before(b, par, q):
            return (b, par, q - 1) if q else (b - 1, 1 - par, QT - 1)

        @block.tensor
        def _(pe):
            pe.wait_ge(w_ready, 1)
            used_of["used"] = 0
            used_of["first"] = True
            pe.wait_ge(x_loaded[0], 16)
            n = 0
            for what, w, src in (("q", wq, xT[:, 0, :, :]), ("k", wk, q1[:, :, :])):
                for k in range(KC):
                    n += 1
                    t.wait_freed(pe, n - 1)
                    for c in range(KC):
                        mm = pe.matmul(t.misc[:, :], w[:, c, k * P:(k + 1) * P], src[:, c, :], start=(c == 0), stop=(c == KC - 1))
                    mm.then_inc(t.misc_done, 1)

            def finish_unit(b, par, q, steps, run):
                todo = list(steps)

                def one():
                    if todo:
                        step, n = todo.pop(0)
                        misc_pe(pe, step, run[0], run[1], n)
                one()
                turn(pe, b, q, 0)
                turn(pe, b, q, 1)
                one()
                turn(pe, b, q, 2)
                turn(pe, b, q, 3)
                one()
                sum_up(pe, b, par, q)
                while todo:
                    one()

            def body(b, par, used):
                used_of["used"] = used
                for q, steps in enumerate(plan(b)):
                    scores(pe, b, par, q)
                    if is_first(b) and q == 0:
                        for step, n in steps:
                            misc_pe(pe, step, b, par, n)
                    else:
                        finish_unit(*before(b, par, q), steps, (b, par))
            over_batches(pe, body)
            finish_unit(B - 1, 1, QT - 1, [], None)
            for k, step in enumerate(EPILOGUE):
                misc_pe(pe, step, B, 0, after_last + k + 1)

        @block.scalar
        def _(act):
            act.wait_ge(w_ready, 1)
            for k in range(KC):
                misc_act(act, ("q", 0, k), 0, 0, k + 1)
            for k in range(KC):
                misc_act(act, ("k", 0, k), 0, 0, KC + k + 1)

            def copy(b, q, gi):
                unit = b * QT + q
                act.wait_ge(turned, unit * NG + gi + 1)
                tiles = GROUPS[gi]
                act.activation(pT[:, tiles[0]:tiles[-1] + 1, :], pt[gi % 2][:, 0:len(tiles) * P]
                               .rearrange("p (t n) -> p t n", n=P), ACT.Copy).then_inc(copied_even, 1)

            def exp(b, q):
                unit = b * QT + q
                act.wait_ge(max_ready, unit + 1)
                after(act, turned, (unit - 1) * NG)
                act.activation(probs[:, q % 2, :], pS[:, 0:C], ACT.Exp, bias=negmax[:, q % 2:q % 2 + 1],
                               accum_out=den[:, q % 2:q % 2 + 1]).then_inc(exped, 1)

            def mix(b, q):
                unit = b * QT + q
                act.wait_ge(summed, unit + 1)
                act.wait_ge(inv_ready, unit + 1)
                act.activation(mixed[:, q % 2, :], pO[:, 0:D], ACT.Copy, scale=inv[:, q % 2:q % 2 + 1])\
                   .then_inc(mixed_ready, 1)

            def finish_unit(b, q, steps, run, scores_of=None):
                todo = list(steps)

                def one():
                    if todo:
                        step, n = todo.pop(0)
                        misc_act(act, step, run[0], run[1], n)
                one()
                copy(b, q, 0)
                one()
                copy(b, q, 2)
                if scores_of:
                    exp(*scores_of)
                one()
                mix(b, q)
                while todo:
                    one()

            def body(b, par, used):
                for q, steps in enumerate(plan(b)):
                    if is_first(b) and q == 0:
                        exp(b, q)
                        for step, n in steps:
                            misc_act(act, step, b, par, n)
                    else:
                        pb, _, pq = before(b, par, q)
                        finish_unit(pb, pq, steps, (b, par), (b, q))
            over_batches(act, body)
            finish_unit(B - 1, QT - 1, [], None)
            for k, step in enumerate(EPILOGUE):
                misc_act(act, step, B, 0, after_last + k + 1)

        @block.vector
        def _(dve):
            dve.wait_ge(c_loaded, 96)
            t.wait_loaded(dve)
            made = sem("made")
            dve.tensor_scalar(wq[:, :, :], wq[:, :, :], D ** -0.5, None, ALU.mult).then_inc(made, 1)
            dve.tensor_scalar(bq[:, :], bq[:, :], D ** -0.5, None, ALU.mult).then_inc(made, 1)
            dve.wait_ge(made, 2)
            dve.sem_inc(w_ready, 1)

            def maximum(b, q):
                unit = b * QT + q
                dve.wait_ge(scored, unit + 1)
                after(dve, exped, unit - 1)
                dve.tensor_reduce(negmax[:, q % 2:q % 2 + 1], pS[:, 0:C], AX.X, ALU.max, negate=True).then_inc(max_ready, 1)

            def inverse(b, q):
                unit = b * QT + q
                dve.wait_ge(exped, unit + 1)
                after(dve, mixed_ready, unit - 1)
                dve.reciprocal(inv[:, q % 2:q % 2 + 1], den[:, q % 2:q % 2 + 1]).then_inc(inv_ready, 1)

            def copy(b, q, gi):
                unit = b * QT + q
                dve.wait_ge(turned, unit * NG + gi + 1)
                tiles = GROUPS[gi]
                m = KLAST if tiles[-1] == KT - 1 else P
                assert m == P or len(tiles) == 1
                dve.tensor_copy(pT[0:m, tiles[0]:tiles[-1] + 1, :], pt[gi % 2][0:m, 0:len(tiles) * P]
                                .rearrange("p (t n) -> p t n", n=P)).then_inc(copied_odd, 1)

            def misc_dve(step, b, n):
                what, rel, k = step
                if what in ("out", "turn"):
                    t.dve(dve, (what, k), b + rel, 0, n)

            def finish_unit(b, q, steps, run, scores_of=None, normalize=None):
                inverse(b, q)
                if scores_of:
                    maximum(*scores_of)
                if normalize is not None:
                    t.dve_normalize(dve, normalize)
                todo = list(steps)

                def one():
                    if todo:
                        step, n = todo.pop(0)
                        misc_dve(step, run, n)
                one()
                copy(b, q, 1)
                one()
                copy(b, q, 3)
                while todo:
                    one()

            def body(b, par, used):
                for q, steps in enumerate(plan(b)):
                    if is_first(b) and q == 0:
                        maximum(b, q)
                        for step, n in steps:
                            misc_dve(step, b, n)
                    else:
                        pb, _, pq = before(b, par, q)
                        finish_unit(pb, pq, steps, b, (b, q), b - 1 if q == QT - 1 and not is_first(b) else None)
            over_batches(dve, body)
            finish_unit(B - 1, QT - 1, [], None)
            for k, step in enumerate(EPILOGUE):
                misc_dve(step, B, after_last + k + 1)
                if step == ("out", -1, QT - 1):
                    t.dve_normalize(dve, B - 1)

        @block.gpsimd
        def _(pool):
            t.begin(pool)
            with pool.Fori(0, B - 1) as b:
                t.pool(pool, b, AHEAD + in_first + b * per_batch + per_batch)
            t.pool(pool, B - 1, after_last + len(EPILOGUE))
            t.finish(pool)


INNER = 704
IT = -(-INNER // P)
ILAST = INNER - (IT - 1) * P
QMAX = 127.0
ROUND = 1.5 * 2.0 ** 23


def quantize(dve, link, out, src, tmp, inv):
    link(dve.tensor_scalar(tmp, src, inv, -QMAX - 1, ALU.mult, ALU.max))
    link(dve.tensor_scalar(tmp, tmp, QMAX, ROUND, ALU.min, ALU.add))
    return dve.tensor_scalar(out, tmp, ROUND, None, ALU.subtract)


def quantized_ffn(nc, g, d, xT_in):
    with ExitStack() as outer:
        keep = Mem(nc, outer, "fk")
        wgu = keep.sb("wgu", [P, KC, 2, INNER], BF16)
        wd = keep.sb("wd", [P, IT, D], BF16)
        col = keep.sb("col", [P, 2, IT])
        down_row = keep.sb("down_row", [P, D])
        hid = keep.sb("hid", [P, IT, T])
        peak = keep.sb("peak", [P, IT, B])
        inv_x, inv_h = keep.sb("inv_x", [P, 1]), keep.sb("inv_h", [P, 1])
        sig = keep.sb("sig", [P, 2])

        with ExitStack() as ctx:
            sem, mem = Sems(nc, ctx, "fw"), Mem(nc, ctx, "fw")
            raw = mem.sb("raw", [P, 2, IT, D])
            raw_d = mem.sb("raw_d", [P, KC, INNER])
            tmp, tmp_d = mem.sb("tmp", [P, 2, IT, D]), mem.sb("tmp_d", [P, KC, INNER])
            qw, qd = mem.sb("qw", [P, 2, IT, D], BF16), mem.sb("qd", [P, KC, INNER], BF16)
            scale, inv = mem.sb("scale", [P, 2 * IT + KC]), mem.sb("inv", [P, 2 * IT + KC])
            diag, ones = mem.sb("diag", [P, KC, P]), mem.sb("ones", [P, P])
            clip, xmax = mem.sb("clip", [P, 2]), mem.sb("xmax", [P, 1])
            xall, sx = mem.sb("xall", [P, 1]), mem.sb("sx", [P, 1])
            bank = [mem.ps(f"bank{k}", [P, 1024], BF16) for k in range(2)]
            row = mem.ps("row", [P, 512])
            loaded, chain, x_peak, x_all = sem("loaded"), sem("chain"), sem("x_peak"), sem("x_all")
            quantized, diag_ready, turned, emptied, row_done, sig_ready = (
                sem(n) for n in ("quantized", "diag_ready", "turned", "emptied", "row_done", "sig_ready"))
            block = ctx.enter_context(nc.Block())
            squares = [(qw[:, s, it, c * P:(c + 1) * P], P, wgu[:, c, s, it * P:it * P + P], P)
                       if it < IT - 1 else
                       (qw[0:ILAST, s, it, c * P:(c + 1) * P], ILAST, wgu[:, c, s, it * P:it * P + ILAST], P)
                       for s in range(2) for it in range(IT) for c in range(KC)]
            squares += [(qd[:, c, it * P:min((it + 1) * P, INNER)], P, wd[0:min(P, INNER - it * P), it, c * P:(c + 1) * P],
                         min(P, INNER - it * P)) for it in range(IT) for c in range(KC)]

            @block.sync
            def _(sp):
                full = (IT - 1) * P
                for s, n in enumerate(("gate", "up")):
                    w = d["L1_ffn_w_" + n]
                    sp.dma_start(raw[:, s, 0:IT - 1, :], w[0:full, :].rearrange("(t p) n -> p t n", p=P)).then_inc(loaded, 16)
                    sp.dma_start(raw[0:ILAST, s, IT - 1, :], w[full:INNER, :]).then_inc(loaded, 16)
                sp.dma_start(raw_d[:, :, :], d["L1_ffn_w_down"].rearrange("(c p) n -> p c n", p=P)).then_inc(loaded, 16)
                for k, n in enumerate(("clip_x", "clip_down")):
                    sp.dma_start(clip[:, k:k + 1], d["L1_ffn_" + n].rearrange("(a n) -> a n", a=1).to_broadcast([P, 1]),
                                 allow_slow_non_contiguous=True).then_inc(loaded, 16)

            @block.gpsimd
            def _(pool):
                pool.wait_ge(x_peak, 1)
                pool.partition_all_reduce(xall[:, :], xmax[:, :], P, bass.bass_isa.ReduceOp.max).then_inc(x_all, 1)

            @block.scalar
            def _(act):
                act.wait_ge(loaded, 112)
                act.activation(sig[:, :], clip[:, :], ACT.Sigmoid).then_inc(sig_ready, 1)

            @block.vector
            def _(dve):
                n = [0]

                def link(ins):
                    n[0] += 1
                    ins.then_inc(chain, 1)
                    dve.wait_ge(chain, n[0])
                dve.tensor_reduce(xmax[:, :], g.x[:, :, :].rearrange("p t n -> p (t n)"), AX.X, ALU.max,
                                  apply_absolute_value=True).then_inc(x_peak, 1)
                link(dve.memset(raw[ILAST:P, :, IT - 1, :], 0.0))
                link(dve.memset(ones[:, :], 1.0))
                dve.wait_ge(loaded, 112)
                link(dve.tensor_reduce(scale[:, 0:2 * IT].rearrange("p (s t) -> p s t", s=2), raw[:, :, :, :], AX.X,
                                       ALU.max, apply_absolute_value=True))
                link(dve.tensor_reduce(scale[:, 2 * IT:], raw_d[:, :, :], AX.X, ALU.max, apply_absolute_value=True))
                link(dve.memset(scale[ILAST:P, IT - 1:2 * IT:IT], 1.0))
                link(dve.tensor_scalar(scale[:, :], scale[:, :], 1 / QMAX, None, ALU.mult))
                link(dve.reciprocal(inv[:, :], scale[:, :]))
                for s in range(2):
                    for it in range(IT):
                        k = s * IT + it
                        link(quantize(dve, link, qw[:, s, it, :], raw[:, s, it, :], tmp[:, s, it, :], inv[:, k:k + 1]))
                for c in range(KC):
                    k = 2 * IT + c
                    link(quantize(dve, link, qd[:, c, :], raw_d[:, c, :], tmp_d[:, c, :], inv[:, k:k + 1]))
                    link(dve.tensor_scalar(diag[:, c, :], g.ident[:, :], scale[:, k:k + 1], None, ALU.mult))
                dve.sem_inc(quantized, 1)
                for i, (_, _, to, m) in enumerate(squares):
                    if i % 8 == 0:
                        dve.wait_ge(turned, min(i + 8, len(squares)))
                    w = to.shape[-1]
                    ins = dve.tensor_copy(to, bank[i // 8 % 2][0:m, i % 8 * P:i % 8 * P + w])
                    ins.then_inc(emptied, 1)
                dve.wait_ge(row_done, 1)
                link(dve.tensor_copy(down_row[:, :], row[:, 0:D]))
                dve.wait_ge(x_all, 1)
                dve.wait_ge(sig_ready, 1)
                link(dve.scalar_tensor_tensor(out=sx[:, :], in0=xall[:, :], scalar=sig[:, 0:1], in1=ones[:, 0:1],
                                              op0=ALU.mult, op1=ALU.mult))
                link(dve.tensor_scalar(sx[:, :], sx[:, :], 1 / QMAX, None, ALU.mult))
                link(dve.reciprocal(inv_x[:, :], sx[:, :]))
                link(dve.tensor_scalar(col[:, :, :], scale[:, 0:2 * IT].rearrange("p (s t) -> p s t", s=2), sx[:, 0:1],
                                       None, ALU.mult))

            @block.tensor
            def _(pe):
                pe.wait_ge(quantized, 1)
                for i, (src, m, to, _) in enumerate(squares):
                    if i >= 16:
                        pe.wait_ge(emptied, (i // 8 - 1) * 8)
                    w = src.shape[-1]
                    pe.transpose(bank[i // 8 % 2][0:w, i % 8 * P:i % 8 * P + m], src, g.identb[0:m, 0:m]).then_inc(turned, 1)
                for c in range(KC):
                    mm = pe.matmul(row[:, c * P:(c + 1) * P], ones[:, :], diag[:, c, :], start=True, stop=True)
                mm.then_inc(row_done, 1)

        with ExitStack() as ctx:
            sem, mem = Sems(nc, ctx, "fu"), Mem(nc, ctx, "fu")
            xT, xs, xq = mem.sb("xT", [P, 2, KC, S]), mem.sb("xs", [P, KC, S]), mem.sb("xq", [P, 2, KC, S], BF16)
            sg = mem.sb("sg", [P, 2, S])
            pg = [mem.ps(f"pg{k}", [P, 512]) for k in range(2)]
            pu = [mem.ps(f"pu{k}", [P, 512]) for k in range(2)]
            x_loaded, own = sem("x_loaded", 2), sem("own")
            xq_ready, gate_done, up_done, silu_ready, hid_ready, peaked = (
                sem(n) for n in ("xq_ready", "gate_done", "up_done", "silu_ready", "hid_ready", "peaked"))
            block = ctx.enter_context(nc.Block())

            @block.sync
            def _(sp):
                def body(b, par, used):
                    after(sp, xq_ready, b)
                    sp.dma_start(xT[:, par, :, :], w_in(xT_in)[:, :, bass.ds(b * S + HALO, S)]).then_inc(x_loaded[par], 16)
                over_batches(sp, body)

            @block.tensor
            def _(pe):
                def body(b, par, used):
                    pe.wait_ge(xq_ready, b + 1)
                    for it in range(IT):
                        n = b * IT + it
                        m = P if it < IT - 1 else ILAST
                        for s, bank, free, done in ((0, pg, silu_ready, gate_done), (1, pu, hid_ready, up_done)):
                            after(pe, free, n - 1)
                            for c in range(KC):
                                mm = pe.matmul(bank[it % 2][0:m, :], wgu[:, c, s, it * P:it * P + m], xq[:, par, c, :],
                                               start=(c == 0), stop=(c == KC - 1))
                            mm.then_inc(done, 1)
                over_batches(pe, body)

            @block.scalar
            def _(act):
                def body(b, par, used):
                    for it in range(IT):
                        n = b * IT + it
                        m = P if it < IT - 1 else ILAST
                        act.wait_ge(gate_done, n + 1)
                        after(act, hid_ready, n - 1)
                        act.activation(sg[0:m, it % 2, :], pg[it % 2][0:m, :], ACT.Silu, scale=col[0:m, 0, it:it + 1])\
                           .then_inc(silu_ready, 1)
                over_batches(act, body)

            @block.vector
            def _(dve):
                dve.memset(peak[:, :, :], 0.0).then_inc(peaked, 1)
                chain = Chain(dve, own, 2)

                def quantize_x(b, par, used):
                    chain.start(b)
                    dve.wait_ge(x_loaded[par], used * 16 + 16)
                    after(dve, up_done, (b - 1) * IT)
                    after(dve, xq_ready, b)
                    quantize(dve, chain.link, xq[:, par, :, :], xT[:, par, :, :], xs[:, :, :], inv_x[:, 0:1])\
                        .then_inc(xq_ready, 1)
                    chain.end()
                quantize_x(0, 0, 0)
                dve.wait_ge(peaked, 1)

                def body(b, par, used):
                    for it in range(IT):
                        n = b * IT + it
                        m = P if it < IT - 1 else ILAST
                        dve.wait_ge(up_done, n + 1)
                        dve.wait_ge(silu_ready, n + 1)
                        to = hid[0:m, it, bass.ds(b * S, S)]
                        dve.scalar_tensor_tensor(out=to, in0=pu[it % 2][0:m, :], scalar=col[0:m, 1, it:it + 1],
                                                 in1=sg[0:m, it % 2, :], op0=ALU.mult, op1=ALU.mult).then_inc(hid_ready, 1)
                        if it == 2 and not (isinstance(b, int) and b == B - 1):
                            quantize_x(b + 1, 1 - par, used + par)
                        dve.wait_ge(hid_ready, n + 1)
                        dve.tensor_reduce(peak[0:m, it, bass.ds(b, 1)], to, AX.X, ALU.max,
                                          apply_absolute_value=True).then_inc(peaked, 1)
                over_batches(dve, body)

        with ExitStack() as ctx:
            sem, mem = Sems(nc, ctx, "fd"), Mem(nc, ctx, "fd")
            hq, hs = mem.sb("hq", [P, 2, IT, S], BF16), mem.sb("hs", [P, 2, S])

            def out_terms(par, k):
                return [(hq[0:P if it < IT - 1 else ILAST, par, it, k * P:(k + 1) * P],
                         wd[0:P if it < IT - 1 else ILAST, it, :]) for it in range(IT)]
            t = Tail(nc, ctx, g, sem, mem, d, None, None, terms=out_terms, row=down_row[:, :])
            hmax, hall, sh = mem.sb("hmax", [P, 1]), mem.sb("hall", [P, 1]), mem.sb("sh", [P, 1])
            h_peak, h_all, own, hq_ready, first = sem("h_peak"), sem("h_all"), sem("own"), sem("hq_ready"), sem("first")
            block = ctx.enter_context(nc.Block())

            def is_first(b):
                return isinstance(b, int) and b == 0

            @block.tensor
            def _(pe):
                def body(b, par, used):
                    if not is_first(b):
                        pe.wait_ge(hq_ready, b * IT)
                        for q in range(QT):
                            t.pe(pe, ("out", q), b - 1, 1 - par, (b - 1) * QT + q + 1)
                over_batches(pe, body)
                pe.wait_ge(hq_ready, B * IT)
                for q in range(QT):
                    t.pe(pe, ("out", q), B - 1, 1, (B - 1) * QT + q + 1)

            @block.gpsimd
            def _(pool):
                t.begin(pool)
                pool.wait_ge(h_peak, 1)
                pool.partition_all_reduce(hall[:, :], hmax[:, :], P, bass.bass_isa.ReduceOp.max).then_inc(h_all, 1)
                with pool.Fori(0, B) as b:
                    t.pool(pool, b, 0)
                t.finish(pool)

            @block.vector
            def _(dve):
                n = [0]

                def link(ins):
                    n[0] += 1
                    ins.then_inc(first, 1)
                    dve.wait_ge(first, n[0])
                dve.tensor_reduce(hmax[:, :], peak[:, :, :].rearrange("p a b -> p (a b)"), AX.X, ALU.max).then_inc(h_peak, 1)
                dve.wait_ge(h_all, 1)
                link(dve.tensor_tensor(sh[:, :], hall[:, :], sig[:, 1:2], ALU.mult))
                link(dve.tensor_scalar(sh[:, :], sh[:, :], 1 / QMAX, None, ALU.mult))
                link(dve.reciprocal(inv_h[:, :], sh[:, :]))
                link(dve.tensor_scalar(down_row[:, :], down_row[:, :], sh[:, 0:1], None, ALU.mult))
                chain = Chain(dve, own, 2 * IT)

                def body(b, par, used):
                    chain.start(b)
                    t.wait_freed(dve, max(b - 1, 0) * QT if isinstance(b, int) else (b - 1) * QT)
                    for it in range(IT):
                        m = P if it < IT - 1 else ILAST
                        after(dve, hq_ready, b * IT + it - 1)
                        quantize(dve, chain.link, hq[0:m, par, it, :], hid[0:m, it, bass.ds(b * S, S)],
                                 hs[0:m, it % 2, :], inv_h[0:m, 0:1]).then_inc(hq_ready, 1)
                    chain.end()
                    if not is_first(b):
                        for q in range(QT):
                            t.dve(dve, ("out", q), b - 1, 0, (b - 1) * QT + q + 1)
                        t.dve_normalize(dve, b - 1)
                over_batches(dve, body)
                for q in range(QT):
                    t.dve(dve, ("out", q), B - 1, 0, (B - 1) * QT + q + 1)
                t.dve_normalize(dve, B - 1)


def decoder(nc, d, out):
    with ExitStack() as ctx:
        g = Bag()
        g.x = ctx.enter_context(nc.sbuf_tensor("x_tokens", [P, B * QT, D], F32))
        g.ident = ctx.enter_context(nc.sbuf_tensor("ident", [P, P], F32))
        g.identb = ctx.enter_context(nc.sbuf_tensor("identb", [P, P], BF16))
        g.halfneg = ctx.enter_context(nc.sbuf_tensor("minus_half", [P, QT], F32))
        def scratch(name, shape, dt=F32):
            return nc.dram_tensor(name, shape, dt, kind="Internal").ap()
        q_parts, k_parts = (scratch(n, [3, D, PADT], BF16) for n in ("q_parts", "k_parts"))
        qx_parts, kx_parts = scratch("qx_parts", [3, D, T], BF16), scratch("kx_parts", [3, D, CTX], BF16)
        vx = scratch("vx", [CTX, D])
        gT = scratch("gT", [NE, T])
        xT = [scratch(f"xT{k}", [D, PADT]) for k in range(5)]
        load_all(nc, g, d)
        project_split(nc, "p0", d["xT"], PADT // 10, 10,
                      [(d["L0_attn_WqT"], None, DK ** -0.5, q_parts), (d["L0_attn_WkT"], None, 1.0, k_parts)])
        window_attention(nc, g, d, q_parts, k_parts, xT[0])
        project_split(nc, "p1", xT[0][:, HALO:HALO + T], S, T // S,
                      [(d["L0_xattn_WqT"], d["L0_xattn_bq"], DK ** -0.5, qx_parts)])
        project_split(nc, "p2", d["cT"], CCH, CTX // CCH, [(d["L0_xattn_WkT"], d["L0_xattn_bk"], 1.0, kx_parts)])
        project_v(nc, d, vx)
        cross_attention(nc, g, d, qx_parts, kx_parts, vx, xT[1])
        gates(nc, g, d, xT[1], gT)
        experts(nc, g, d, xT[1], gT, xT[2])
        with ExitStack() as held:
            khat = held.enter_context(nc.sbuf_tensor("khat", [P, B * BQ, 4], F32))
            bound = held.enter_context(nc.sbuf_tensor("bound", [P, B * BQ, 4], F32))
            bind(nc, d, xT[2], khat, bound)
            retrieve(nc, g, d, khat, bound, xT[3])
        context_attention(nc, g, d, xT[3], xT[4])
        quantized_ffn(nc, g, d, xT[4])
        store_x(nc, g, out)


def store_x(nc, g, out):
    with ExitStack() as ctx:
        stored = Sems(nc, ctx, "st")("stored")
        block = ctx.enter_context(nc.Block())

        @block.sync
        def _(sp):
            sp.dma_start(out.rearrange("b (t p) d -> p (b t) d", p=P), g.x[:, :, :]).then_inc(stored, 16)
            sp.wait_ge(stored, 16)


class Bag:
    pass


def layout(inputs):
    f = np.float32
    a = {k: np.ascontiguousarray(v) for k, v in inputs.items()}
    o = {"x": a["x"]}
    xT = np.zeros((D, PADT), f)
    xT[:, HALO:HALO + T] = a["x"].reshape(T, D).T
    o["xT"] = xT
    cT = np.zeros((D, CTX), f)
    cT[:, :B * C] = a["ctx_1024"].reshape(B * C, D).T
    o["cT"] = cT
    for n in ("L0_xattn_bq", "L0_xattn_bk", "L0_xattn_bv", "L0_xattn_bo"):
        o[n] = a[n]
    for n in ("L0_attn_Wq", "L0_attn_Wk", "L0_attn_Wv", "L0_xattn_Wq", "L0_xattn_Wk", "L0_xattn_Wv"):
        o[n + "T"] = np.ascontiguousarray(a[n].T)
    for n in ("L0_attn", "L0_xattn"):
        w = np.zeros((H, 2 * DK, D), f)
        w[:, :DK] = a[n + "_Wo"].T.reshape(H, DK, D)
        o[n + "_WoP"] = w.reshape(2 * D, D)
    o["ident"] = np.eye(P, dtype=f)
    gather, spread = np.zeros((P, HG, H), f), np.zeros((H, HG, P), f)
    for h in range(H):
        gather[32 * (h % HPG) + DK, h // HPG, h] = 1
        spread[h, h // HPG, 32 * (h % HPG):32 * (h % HPG) + 32] = 1
    o["gather"], o["spread"] = gather, spread
    r, j = np.arange(P)[:, None], np.arange(WIN)[None]
    mask = np.zeros((P, 3, WIN), f)
    for e in range(3):
        seen = (j >= r) & (j <= r + 2 * HALO)
        if e == 0:
            seen &= j >= HALO
        if e == 2:
            seen &= j < P + HALO
        mask[:, e] = np.where(seen, 0, NEG)
    o["mask"] = mask
    q, k = np.arange(S) + HALO, np.arange(BW)
    o["pos_q"] = np.stack([q // P * P] * 3 + [q % P] * 3 + [q * 0 + 1] * 6).astype(f)
    o["pos_k"] = np.stack([k * 0 + 1] * 6 + [-(k // P * P)] * 3 + [-(k % P)] * 3).astype(f)
    pick = np.zeros((POSR, 2, 4), f)
    for i in range(POSR):
        pick[i, 0 if i >= 6 else 1, 1 + i % 3] = 1
        pick[i, 1 if i >= 6 else 0, 0] = 1
    o["pick"] = pick
    o["slopes"] = np.repeat(a["L0_attn_slopes"][None], POSR, 0)
    for n in ("W1", "W2", "W3", "b1", "b2", "b3", "Wg", "bg", "Wf", "bf"):
        o["L0_ffn_" + n] = a["L0_ffn_" + n]
    e = np.arange(NE)
    o["tri"] = np.repeat((e[None, None, :] > e[None, :, None]).astype(f), P, 0)
    o["one_of"] = np.repeat(np.eye(NE, dtype=f)[:, :, None], P, 2)
    for n in ("bk", "bv", "ln_g", "ln_b", "bo"):
        o["L1_attn_" + n] = a["L1_attn_" + n]
    for n in ("bq", "bv", "bo", "Wk"):
        o["L1_xattn_" + n] = a["L1_xattn_" + n]
    for n in ("L1_attn_Wk", "L1_attn_Wv", "L1_attn_Wo", "L1_xattn_Wq", "L1_xattn_Wv", "L1_xattn_Wo"):
        o[n + "T"] = np.ascontiguousarray(a[n].T)
    for n in ("clip_x", "clip_down", "w_gate", "w_up", "w_down"):
        o["L1_ffn_" + n] = a["L1_ffn_" + n]
    o["ctx"] = a["ctx_1024"].reshape(B * C, D)
    i = np.arange(P)
    o["upper"] = (i[:, None] <= i[None, :]).astype(f)
    o["root"] = (1 / np.sqrt(np.arange(1, S + 1, dtype=f))).reshape(QT, P).T.copy()
    return o


def kernel(**inputs):
    import concourse.bacc as bacc
    from concourse.bass_utils import run_bass_kernel_spmd

    nc = bacc.Bacc("TRN2", target_bir_lowering=False, num_devices=1)
    arrays = {"in_" + name: np.ascontiguousarray(a) for name, a in layout(inputs).items()}
    d = {name[3:]: nc.dram_tensor(name, a.shape, mybir.dt.from_np(a.dtype), kind="ExternalInput").ap()
         for name, a in arrays.items()}
    out = nc.dram_tensor("out", (B, S, D), F32, kind="ExternalOutput").ap()
    decoder(nc, d, out)
    return run_bass_kernel_spmd(nc, [arrays], core_ids=[0]).results[0]["out"]
```

```python
from contextlib import ExitStack

import concourse.bass as bass
import numpy as np
from concourse import mybir

F32 = mybir.dt.float32
BF16 = mybir.dt.bfloat16
ALU = mybir.AluOpType
ACT = mybir.ActivationFunctionType
AX = mybir.AxisListType

P = 128
B, S, D = 8, 512, 256
C = 1601
T = B * S
QT = S // P
KC = D // P
H, DK = 16, 16
HG, HPG = 4, 4
HALO = 32
WIN = P + 2 * HALO
PADT = T + 2 * HALO
BW = S + 2 * HALO
EPS = 1e-5
NEG = -1e30
KPART = (0, 0, 1, 1, 0, 2)
QPART = (0, 1, 0, 1, 2, 0)
SPLIT = len(KPART) * DK
MAXR = 3
POSR = MAXR + 12


def after(eng, sem, value):
    if not isinstance(value, int) or value > 0:
        eng.wait_ge(sem, value)


def over_batches(eng, body):
    body(0, 0, 0)
    with eng.Fori(0, (B - 2) // 2) as i:
        body(i * 2 + 1, 1, i)
        body(i * 2 + 2, 0, i + 1)
    body(B - 1, 1, B // 2 - 1)


class Sems:

    def __init__(self, nc, ctx, phase):
        self.nc, self.phase, self.mine = nc, phase, []
        ctx.callback(self.clear)

    def __call__(self, name, n=None):
        if n is None:
            self.mine.append(self.nc.alloc_semaphore(f"{self.phase}_{name}"))
            return self.mine[-1]
        return [self(f"{name}{i}") for i in range(n)]

    def clear(self):
        self.nc.clear_and_free_semaphores(self.mine)
        self.nc.all_engine_barrier()


class Mem:
    def __init__(self, nc, ctx, phase):
        self.nc, self.ctx, self.phase = nc, ctx, phase

    def sb(self, name, shape, dt=F32):
        return self.ctx.enter_context(self.nc.sbuf_tensor(f"{self.phase}_{name}", shape, dt))

    def ps(self, name, shape, dt=F32):
        return self.ctx.enter_context(self.nc.psum_tensor(f"{self.phase}_{name}", shape, dt))


class Chain:

    def __init__(self, eng, sem, per_batch=0):
        self.eng, self.sem, self.per, self.b, self.n = eng, sem, per_batch, 0, 0

    def start(self, b):
        self.b, self.n = b, 0

    def link(self, ins):
        self.n += 1
        ins.then_inc(self.sem, 1)
        self.eng.wait_ge(self.sem, self.b * self.per + self.n)

    def end(self):
        assert self.n == self.per, (self.n, self.per)


def w_in(ap):
    return ap.rearrange("(c p) n -> p c n", p=P)


def load_all(nc, g, d):
    with ExitStack() as ctx:
        sem = Sems(nc, ctx, "ld")
        loaded = sem("loaded")
        block = ctx.enter_context(nc.Block())

        @block.sync
        def _(sp):
            sp.dma_start(g.ident[:, :], d["ident"]).then_inc(loaded, 16)
            sp.wait_ge(loaded, 16)

        @block.vector
        def _(dve):
            dve.memset(g.halfneg[:, :], -0.5)
            dve.wait_ge(loaded, 16)
            dve.tensor_copy(g.identb[:, :], g.ident[:, :])


def project_split(nc, phase, source, width, chunks, jobs):
    ahead = 4 // (KC * len(jobs))
    pieces = [(a, j, oc) for a in range(ahead) for j in range(len(jobs)) for oc in range(KC)]
    turns = chunks // ahead
    with ExitStack() as ctx:
        sem, mem = Sems(nc, ctx, phase), Mem(nc, ctx, phase)
        w_loaded, w_ready, projected, rest_ready = (sem(x) for x in ("w_loaded", "w_ready", "projected", "rest_ready"))
        part0_ready, part1_ready, parts_ready = (sem(x) for x in ("part0_ready", "part1_ready", "parts_ready"))
        stored = sem("stored", 4)
        srcT = mem.sb("source", [P, KC, chunks * width])
        src_loaded = sem("src_loaded", 4)
        wT = [mem.sb(f"w{j}", [P, KC, D]) for j in range(len(jobs))]
        bias = [mem.sb(f"b{j}", [P, KC]) for j in range(len(jobs))]
        rest = mem.sb("rest", [P, 4, width])
        parts = mem.sb("parts", [P, 4, 3, width], BF16)
        acc = [mem.ps(f"acc{k}", [P, 512]) for k in range(4)]
        block = ctx.enter_context(nc.Block())
        n_w = sum(1 + (j[1] is not None) for j in jobs)

        def turn_loop(eng, body):
            body(0)
            if turns > 1:
                with eng.Fori(1, turns) as i:
                    body(i)

        @block.sync
        def _(sp):
            for j, (w, b, _, _) in enumerate(jobs):
                sp.dma_start(wT[j][:, :, :], w_in(w)).then_inc(w_loaded, 16)
                if b is not None:
                    sp.dma_start(bias[j][:, :], b.rearrange("(c p) -> p c", p=P),
                                 allow_slow_non_contiguous=True).then_inc(w_loaded, 16)

            quarter = chunks * width // 4
            for k in range(4):
                sp.dma_start(srcT[:, :, k * quarter:(k + 1) * quarter],
                             w_in(source)[:, :, k * quarter:(k + 1) * quarter]).then_inc(src_loaded[k], 16)

            def body(i):
                for k, (a, j, oc) in enumerate(pieces):
                    sp.wait_ge(parts_ready, i * 4 + k + 1)
                    out = jobs[j][3].rearrange("s (c p) t -> p c s t", p=P)[:, oc, :, bass.ds((i * ahead + a) * width, width)]
                    sp.dma_start(out, parts[:, k, :, :]).then_inc(stored[k], 16)
            turn_loop(sp, body)
            for k in range(4):
                sp.wait_ge(stored[k], 16 * turns)

        @block.tensor
        def _(pe):
            pe.wait_ge(w_ready, 1)

            def body(i):
                for k, (a, j, oc) in enumerate(pieces):
                    after(pe, rest_ready, i * 4 + k - 3)
                    for c in range(KC):
                        mm = pe.matmul(acc[k][:, 0:width], wT[j][:, c, oc * P:(oc + 1) * P],
                                       srcT[:, c, bass.ds((i * ahead + a) * width, width)],
                                       start=(c == 0), stop=(c == KC - 1))
                    mm.then_inc(projected, 1)
            done = 0
            for k in range(4):
                pe.wait_ge(src_loaded[k], 16)
                until = (k + 1) * chunks // (4 * ahead)
                if done == 0:
                    body(0)
                    done = 1
                if until - done > 1:
                    with pe.Fori(done, until) as i:
                        body(i)
                elif until > done:
                    body(done)
                done = max(done, until)

        @block.scalar
        def _(act):
            act.wait_ge(w_ready, 1)

            def body(i):
                for pair in (0, 2):
                    for k in (pair, pair + 1):
                        a, j, oc = pieces[k]
                        act.wait_ge(projected, i * 4 + k + 1)
                        after(act, stored[k], i * 16)
                        act.activation(parts[:, k, 0, :], acc[k][:, 0:width], ACT.Identity,
                                       bias=bias[j][:, oc:oc + 1] if jobs[j][1] is not None else 0.0)\
                           .then_inc(part0_ready, 1)
                    for k in (pair, pair + 1):
                        act.wait_ge(rest_ready, i * 4 + k + 1)
                        act.activation(parts[:, k, 1, :], rest[:, k, :], ACT.Copy).then_inc(part1_ready, 1)
            turn_loop(act, body)

        @block.vector
        def _(dve):
            dve.wait_ge(w_loaded, 16 * n_w)
            scaled = sem("scaled")
            n = 0
            for j, (_, b, factor, _) in enumerate(jobs):
                if factor != 1.0:
                    dve.tensor_scalar(wT[j][:, :, :], wT[j][:, :, :], factor, None, ALU.mult).then_inc(scaled, 1)
                    n += 1
                    if b is not None:
                        dve.tensor_scalar(bias[j][:, :], bias[j][:, :], factor, None, ALU.mult).then_inc(scaled, 1)
                        n += 1
            after(dve, scaled, n)
            dve.sem_inc(w_ready, 1)

            def body(i):
                for pair in (0, 2):
                    for k in (pair, pair + 1):
                        a, j, oc = pieces[k]
                        dve.wait_ge(part0_ready, i * 4 + k + 1)
                        after(dve, parts_ready, i * 4 + k - 3)
                        dve.scalar_tensor_tensor(out=rest[:, k, :], in0=acc[k][:, 0:width],
                                                 scalar=bias[j][:, oc:oc + 1] if jobs[j][1] is not None else 0.0,
                                                 in1=parts[:, k, 0, :], op0=ALU.add, op1=ALU.subtract)\
                           .then_inc(rest_ready, 1)
                    for k in (pair, pair + 1):
                        dve.wait_ge(part1_ready, i * 4 + k + 1)
                        dve.tensor_tensor(parts[:, k, 2, :], rest[:, k, :], parts[:, k, 1, :], ALU.subtract)\
                           .then_inc(parts_ready, 1)
            turn_loop(dve, body)


class Tail:

    def __init__(self, nc, ctx, g, sem, mem, d, bo, xT_out, heads=None, terms=None, factor=1.0, row=None,
                 final=None):
        self.g, self.d, self.bo_in, self.xT_out, self.heads = g, d, bo, xT_out, heads
        self.final = final
        self.has_bo, self.factor, self.row = bo is not None, factor, row
        self.terms = terms or (lambda par, k: [(self.oT[:, par, h, k * P:(k + 1) * P], self.woP[:, h, :])
                                               for h in range(HG)])
        if heads:
            self.woP = mem.sb("woP", [P, HG, D])
            self.oT = mem.sb("oT", [P, 2, HG, S])
            self.den = mem.sb("den", [QT * H, P])
            self.inv = mem.sb("inv", [QT * H, P])
            self.spread = mem.sb("spread", [P, HG * S])
            self.inv_dram = nc.dram_tensor(f"{mem.phase}_inv_dram", [HPG, HG * S], F32, kind="Internal").ap()
            self.den_moved = sem("den_moved")
            self.inv_ready = sem("inv_ready")
            self.inv_stored = sem("inv_stored")
            self.inv_spread = sem("inv_spread")
            self.o_scaled = sem("o_scaled")
        self.y = mem.sb("y", [P, QT, D])
        self.xn = mem.sb("xn", [P, QT, D])
        self.stats = mem.sb("stats", [P, QT, 6])
        self.mv = mem.sb("mv", [P, QT, 2])
        self.veps = mem.sb("veps", [P, QT])
        self.rstd = mem.sb("rstd", [P, QT])
        self.bo = mem.sb("bo", [P, D])
        self.misc = mem.ps("misc", [P, 512])
        if xT_out is not None:
            self.xt = mem.sb("xt", [P, KC, S])
        self.misc_done = sem("misc_done")
        self.freed = sem("freed")
        self.o_copied = sem("o_copied")
        self.stat = sem("stat")
        self.var_ready = sem("var_ready")
        self.rstd_ready = sem("rstd_ready")
        self.xn_ready = sem("xn_ready")
        self.x_kept = sem("x_kept")
        self.stored_by = sem("stored_by")
        self.passed, self.pool_passed = sem("passed"), sem("pool_passed")
        self.c_loaded = sem("tail_loaded")
        self.xt_stored = sem("xt_stored")
        self.xt_free = sem("xt_free")

    def begin(self, pool):
        pool.sem_inc(self.freed, 1)
        pool.sem_inc(self.x_kept, 1)
        if self.xT_out is not None:
            pool.sem_inc(self.xt_free, 1)

    def wait_freed(self, eng, n):
        eng.wait_ge(self.freed, n + 1)

    def load(self, sp):
        if self.heads:
            sp.dma_start(self.woP[:, :, :], self.d[self.heads + "_WoP"].rearrange("(c p) n -> p c n", p=P)).then_inc(self.c_loaded, 16)
        if isinstance(self.bo_in, str):
            sp.dma_start(self.bo[:, :], self.d[self.bo_in].rearrange("(a n) -> a n", a=1).to_broadcast([P, D]))\
              .then_inc(self.c_loaded, 16)

    def wait_loaded(self, eng):
        after(eng, self.c_loaded, 16 * (self.heads is not None) + 16 * isinstance(self.bo_in, str))

    def pe(self, pe, step, b, par, n):
        what, k = step
        self.wait_freed(pe, n - 1)
        if what == "out":
            if self.heads and k == 0:
                pe.wait_ge(self.o_scaled, b + 1)
            terms = self.terms(par, k)
            for i, (lhsT, rhs) in enumerate(terms):
                mm = pe.matmul(self.misc[:, 0:D], lhsT, rhs, start=(i == 0), stop=(i == len(terms) - 1))
        else:
            pe.wait_ge(self.xn_ready, b * QT + k + 1)
            for c in range(KC):
                mm = pe.transpose(self.misc[:, c * P:(c + 1) * P], self.xn[:, k, c * P:(c + 1) * P],
                                  self.g.ident[:, :])
        mm.then_inc(self.misc_done, 1)

    def act(self, act, step, b, n):
        what, k = step
        if what == "turn":
            act.wait_ge(self.misc_done, n)
            if k == 0:
                act.wait_ge(self.xt_free, b + 1)
            act.activation(self.xt[:, :, k * P:(k + 1) * P],
                           self.misc[:, 0:D].rearrange("p (c t) -> p c t", c=KC), ACT.Copy).then_inc(self.freed, 1)

    def dve(self, dve, step, b, par, n):
        what, k = step
        if what == "turn":
            return
        dve.wait_ge(self.misc_done, n)
        if what == "out":
            links = 2 + self.has_bo + (self.row is not None)
            at = b * (QT * links) + k * links
            dve.wait_ge(self.x_kept, b + 1)
            x, y, i = self.g.x[:, b * QT + k, :], self.y[:, k, :], 0
            if self.row is not None:
                dve.tensor_tensor(y, self.misc[:, 0:D], self.row, ALU.mult).then_inc(self.freed, 1)
                self.wait_freed(dve, n)
                dve.tensor_tensor(y, y, x, ALU.add).then_inc(self.stat, 1)
                i += 1
                dve.wait_ge(self.stat, at + i)
            else:
                dve.scalar_tensor_tensor(out=y, in0=x, scalar=self.factor, in1=self.misc[:, 0:D],
                                         op0=ALU.mult, op1=ALU.add).then_inc(self.freed, 1)
                self.wait_freed(dve, n)
            if self.has_bo:
                dve.tensor_tensor(y, y, self.bo[:, :], ALU.add).then_inc(self.stat, 1)
                i += 1
                dve.wait_ge(self.stat, at + i)
            dve.bn_stats(self.stats[:, k, :], self.y[:, k, :]).then_inc(self.stat, 1)
            dve.wait_ge(self.stat, at + links - 1)
            dve.sem_inc(self.passed, 1)
            dve.bn_aggr(self.mv[:, k, :], self.stats[:, k, :]).then_inc(self.stat, 1)
            dve.wait_ge(self.stat, at + links)
            if k == QT - 1:
                dve.tensor_scalar(self.veps[:, :], self.mv[:, :, 1], EPS, None, ALU.add).then_inc(self.var_ready, 1)

    def dve_invert(self, dve, b):
        dve.wait_ge(self.den_moved, b * (16 * HPG) + 16 * HPG)
        dve.reciprocal(self.inv[:, :], self.den[:, :]).then_inc(self.inv_ready, 1)

    def pool_scale(self, pool, b, par):
        pool.wait_ge(self.o_copied, b * HG + HG)
        pool.sem_inc(self.pool_passed, 1)
        for j in range(HPG):
            pool.dma_start(self.den[j * 16:(j + 1) * 16, :],
                           self.oT[j * VT + DK:j * VT + DK + 1, par, :, :].rearrange("p h (q t) -> p (h q) t", q=QT))\
                .then_inc(self.den_moved, 16)
        pool.wait_ge(self.inv_ready, b + 1)
        pool.sem_inc(self.pool_passed, 1)
        pool.dma_start(self.inv_dram.rearrange("j (r t) -> (j r) t", t=P), self.inv[:, :]).then_inc(self.inv_stored, 16)
        pool.wait_ge(self.inv_stored, b * 16 + 16)
        pool.sem_inc(self.pool_passed, 1)
        for j in range(HPG):
            pool.dma_start(self.spread[j * VT:(j + 1) * VT, :], self.inv_dram[j:j + 1, :].to_broadcast([VT, HG * S]))\
                .then_inc(self.inv_spread, 16)
        pool.wait_ge(self.inv_spread, b * (16 * HPG) + 16 * HPG)
        o = self.oT[:, par, :, :].rearrange("p h t -> p (h t)")
        pool.tensor_tensor(o, o, self.spread[:, :], ALU.mult).then_inc(self.o_scaled, 1)

    def dve_normalize(self, dve, b):
        dve.wait_ge(self.rstd_ready, b + 1)
        dve.wait_ge(self.x_kept, b + 1)
        for k in range(QT):
            dve.tensor_scalar(self.xn[:, k, :], self.y[:, k, :], self.mv[:, k, 0:1], self.rstd[:, k:k + 1],
                              ALU.subtract, ALU.mult).then_inc(self.xn_ready, 1)

    def pool(self, pool, b, n_turned):
        self.pool_keep(pool, b)
        self.pool_store(pool, b, n_turned)

    def pool_keep(self, pool, b):
        pool.wait_ge(self.var_ready, b + 1)
        pool.tensor_tensor(self.rstd[:, :], self.veps[:, :], self.g.halfneg[:, :], ALU.pow).then_inc(self.rstd_ready, 1)
        pool.wait_ge(self.xn_ready, b * QT + QT)
        pool.sem_inc(self.pool_passed, 1)
        if self.final is not None:
            pool.dma_start(self.final[bass.ds(b, 1), :, :].rearrange("b (t p) d -> p (b t) d", p=P), self.xn[:, :, :])\
                .then_inc(self.xt_stored, 16)
            pool.wait_ge(self.xt_stored, b * 16 + 16)
            pool.sem_inc(self.x_kept, 1)
            return
        pool.tensor_copy(self.g.x[:, bass.ds(b * QT, QT), :], self.xn[:, :, :]).then_inc(self.x_kept, 1)

    def pool_store(self, pool, b, n_turned):
        if self.xT_out is None:
            return
        self.wait_freed(pool, n_turned)
        pool.sem_inc(self.stored_by, 1)
        pool.dma_start(w_in(self.xT_out)[:, :, bass.ds(b * S + HALO, S)], self.xt[:, :, :]).then_inc(self.xt_stored, 16)
        pool.wait_ge(self.xt_stored, b * 16 + 16)
        pool.sem_inc(self.xt_free, 1)

    def finish(self, eng):
        eng.wait_ge(self.x_kept, B + 1)
        if self.xT_out is not None or self.final is not None:
            eng.wait_ge(self.xt_stored, B * 16)


PLAIN_STEPS = [("out", q) for q in range(QT)] + [("turn", q) for q in range(QT)]
TAIL_STEPS = PLAIN_STEPS


SHIFTED = QT + 1
VT = 2 * DK
ROWS = SPLIT + POSR


def window_attention(nc, g, d, q_parts, k_parts, xT_out):
    ITEMS = HG * QT
    SCORED = 2
    at_item = {0: [("v", 0)], 3: [("v", 1)], 4: [("v", 2)], 7: [("v", 3)], 8: [("v", 4)],
               9: [("out", 0)], 10: [("out", 1)], 11: [("out", 2)], 12: [("out", 3)],
               14: [("turn", 0), ("turn", 1)], 15: [("turn", 2), ("turn", 3)]}
    ROWS_AT = (1, 2)
    INVERT_AT = 3
    NORMALIZE_AT = 13
    AHEAD = SHIFTED + 2
    in_first = SHIFTED + 2 * HG
    per_batch = in_first + len(TAIL_STEPS)

    def plan(b):
        first, last = isinstance(b, int) and b == 0, isinstance(b, int) and b == B - 1
        n = AHEAD if first else AHEAD + in_first + (b - 1) * per_batch
        out, i = [], 0
        for k in range(ITEMS):
            row = [step for step in at_item.get(k, []) if (not last if step[0] == "v" else not first)]
            if k % QT in ROWS_AT and not (last and k // QT == HG - 1):
                row.append(("rows", ROWS_AT.index(k % QT)))
            numbered = []
            for step in row:
                i += 1
                numbered.append((step, n + i))
            out.append(numbered)
        return out

    def number_of(b, step, items=range(ITEMS)):
        return [n for k in items for s, n in plan(b)[k] if s == step][0]

    def later(b, hg, k):
        return b + (hg + k) // HG, (hg + k) % HG

    def exists(b):
        return not (isinstance(b, int) and b >= B)

    after_last = AHEAD + in_first + (B - 2) * per_batch + 2 * (HG - 1) + len(TAIL_STEPS)
    with ExitStack() as ctx:
        sem, mem = Sems(nc, ctx, "wa"), Mem(nc, ctx, "wa")
        t = Tail(nc, ctx, g, sem, mem, d, None, xT_out, heads="L0_attn")
        wvT = mem.sb("wvT", [P, KC, D])
        mask = mem.sb("mask", [P, 3, WIN], BF16)
        kq = mem.sb("kq", [P, HG, HPG, BW], BF16)
        qq = mem.sb("qq", [P, HG, HPG, S], BF16)
        xw = mem.sb("xw", [P, 2, KC, BW])
        v = mem.sb("v", [P, 2, SHIFTED, H, VT])
        probs = mem.sb("probs", [P, 2, 2, HPG * P])
        negmax = mem.sb("negmax", [P, 2, QT * HPG])
        max_parts = mem.sb("max_parts", [P, QT, HPG, MAXR], BF16)
        zeros = mem.sb("zeros", [MAXR, HPG, S], BF16)
        slope = mem.sb("slope", [P, 2, H])
        slope_part = mem.sb("slope_part", [P, 3, H], BF16)
        pick = mem.sb("pick", [P, 2, 4])
        pos_q = mem.sb("pos_q", [P, S])
        pos_k = mem.sb("pos_k", [P, BW])
        side = mem.sb("side", [P, 2, H])
        pA = [mem.ps(f"pA{k}", [P, 2, 512]) for k in range(2)]
        pB = [mem.ps(f"pB{k}", [P, 512]) for k in range(2)]
        misc16 = t.misc[:, :].bitcast(BF16)
        pO = mem.ps("pO", [P, 512])
        const_loaded, const_ready = sem("const_loaded"), sem("const_ready")
        wv_loaded, x_loaded = sem("wv_loaded"), sem("x_loaded")
        kq_loaded, xw_loaded = sem("kq_loaded", HG), sem("xw_loaded", 2)
        first_scored, maxed, max_chain, parts_ready, rows_set, scored, exped, pv_done = (
            sem(n) for n in ("first_scored", "maxed", "max_chain", "parts_ready", "rows_set", "scored", "exped", "pv_done"))
        block = ctx.enter_context(nc.Block())
        rows = slice(SPLIT, SPLIT + POSR)
        mask_raw = probs[:, :, :, :].rearrange("p a b n -> p (a b n)")[:, 0:3 * WIN].rearrange("p (e w) -> p e w", e=3)
        KQ = 16 * 2 * len(KPART)

        @block.sync
        def _(sp):
            sp.dma_start(slope[rows, 0, :], d["slopes"]).then_inc(const_loaded, 16)
            sp.dma_start(pick[rows, :, :], d["pick"]).then_inc(const_loaded, 16)
            sp.dma_start(pos_q[rows, :], d["pos_q"]).then_inc(const_loaded, 16)
            sp.dma_start(pos_k[rows, :], d["pos_k"]).then_inc(const_loaded, 16)
            sp.dma_start(mask_raw, d["mask"]).then_inc(const_loaded, 16)
            sp.dma_start(wvT[:, :, :], w_in(d["L0_attn_WvT"])).then_inc(wv_loaded, 16)
            sp.dma_start(xw[:, 0, :, :], w_in(d["xT"])[:, :, 0:BW]).then_inc(xw_loaded[0], 16)
            t.load(sp)

            def body(b, par, used):
                for hg in range(HG):
                    after(sp, scored, (b - 1) * (ITEMS * SCORED) + (hg + 1) * (QT * SCORED))
                    if not (isinstance(b, int) and b == 0):
                        sp.dma_start(qq[SPLIT:SPLIT + MAXR, hg, :, :], zeros[:, :, :]).then_inc(kq_loaded[hg], 16)
                    heads = slice(hg * HPG * DK, (hg + 1) * HPG * DK)
                    for r in range(len(KPART)):
                        to = slice(r * DK, (r + 1) * DK)
                        sp.dma_start(kq[to, hg, :, :], k_parts[KPART[r], heads, bass.ds(b * S, BW)]
                                     .rearrange("(h e) t -> e h t", e=DK)).then_inc(kq_loaded[hg], 16)
                        sp.dma_start(qq[to, hg, :, :], q_parts[QPART[r], heads, bass.ds(b * S + HALO, S)]
                                     .rearrange("(h e) t -> e h t", e=DK)).then_inc(kq_loaded[hg], 16)
                    if hg == 0 and not (isinstance(b, int) and b == B - 1):
                        sp.dma_start(xw[:, 1 - par, :, :], w_in(d["xT"])[:, :, bass.ds(b * S + S, BW)])\
                          .then_inc(xw_loaded[1 - par], 16)
                if isinstance(b, int) and b == 0:
                    sp.dma_start(g.x[:, :, :], d["x"].rearrange("b (t p) d -> p (b t) d", p=P)).then_inc(x_loaded, 16)
            over_batches(sp, body)
            for hg in range(HG):
                sp.wait_ge(kq_loaded[hg], B * KQ + (B - 1) * 16)

        def v_pe(pe, par, used, s, n):
            if s == 0:
                pe.wait_ge(xw_loaded[par], used * 16 + 16)
            t.wait_freed(pe, n - 1)
            m = P if s < QT else 2 * HALO
            for c in range(KC):
                mm = pe.matmul(t.misc[0:m, 0:D], xw[:, par, c, s * P:s * P + m], wvT[:, c, :],
                               start=(c == 0), stop=(c == KC - 1))
            mm.then_inc(t.misc_done, 1)

        def v_act(act, b, par, s, n):
            m = P if s < QT else 2 * HALO
            act.wait_ge(t.misc_done, n)
            after(act, pv_done, (b - 1) * ITEMS)
            act.activation(v[0:m, par, s, :, 0:DK], t.misc[0:m, 0:D].rearrange("p (h e) -> p h e", h=H), ACT.Copy)\
               .then_inc(t.freed, 1)

        def first_scores(pe, b, hg, qt):
            n = b * ITEMS + hg * QT + qt
            if qt == 0:
                pe.wait_ge(kq_loaded[hg], b * (KQ + 16) + KQ)
            after(pe, maxed, n - 1)
            for j in range(HPG):
                out = pA[qt % 2][:, j // 2, j % 2 * WIN:(j % 2 + 1) * WIN]
                pe.matmul(out, qq[0:ROWS, hg, j, qt * P:(qt + 1) * P], kq[0:ROWS, hg, j, qt * P:qt * P + WIN],
                          start=True, stop=False)
                mm = pe.matmul(out, g.identb[:, :], mask[:, edge_of(qt), :], start=False, stop=True)
            mm.then_inc(first_scored, 1)

        def edge_of(qt):
            return 0 if qt == 0 else 2 if qt == QT - 1 else 1

        def second_scores(pe, b, k):
            hg, qt = k // QT, k % QT
            if qt == 0:
                pe.wait_ge(rows_set, b * (2 * HG) + 2 * hg + 2)
            for i, (lo, hi) in enumerate(((0, P), (P, WIN))):
                after(pe, exped, b * (ITEMS * SCORED) + k * SCORED + i - 1)
                for j in range(HPG):
                    out = pB[i][0:hi - lo, j * P:(j + 1) * P]
                    pe.matmul(out, kq[0:ROWS, hg, j, qt * P + lo:qt * P + hi], qq[0:ROWS, hg, j, qt * P:(qt + 1) * P],
                              start=True, stop=False)
                    mm = pe.matmul(out, mask[:, edge_of(qt), lo:hi], g.identb[:, :], start=False, stop=True)
                mm.then_inc(scored, 1)

        def times_v(pe, b, par, k):
            hg, qt = k // QT, k % QT
            pe.wait_ge(exped, b * (ITEMS * SCORED) + k * SCORED + SCORED)
            if qt == 0:
                after(pe, t.o_copied, b * HG + hg)
            if isinstance(b, int) and b == 0 and k == 0:
                t.wait_freed(pe, SHIFTED)
            for i, m in enumerate((P, P // 2)):
                for j in range(HPG):
                    mm = pe.matmul(pO[j * VT:(j + 1) * VT, qt * P:(qt + 1) * P],
                                   v[0:m, par, qt + i, hg * HPG + j, :], probs[0:m, k % 2, i, j * P:(j + 1) * P],
                                   start=(i == 0), stop=(i == 1), skip_group_check=True)
            mm.then_inc(pv_done, 1)

        def rows_pe(pe, b, hg, pair, n):
            t.wait_freed(pe, n - 1)
            pe.wait_ge(parts_ready, b * HG + hg + 1)
            for jj in range(2):
                for qt in range(QT):
                    at = (jj * QT + qt) * P
                    mm = pe.transpose(misc16[SPLIT:SPLIT + MAXR, at:at + P], max_parts[:, qt, 2 * pair + jj, :],
                                      g.identb[:, :])
            mm.then_inc(t.misc_done, 1)

        def rows_act(act, hg, pair, n):
            act.wait_ge(t.misc_done, n)
            act.activation(qq[SPLIT:SPLIT + MAXR, hg, 2 * pair:2 * pair + 2, :],
                           misc16[SPLIT:SPLIT + MAXR, :].rearrange("p (j t) -> p j t", j=2), ACT.Copy)\
               .then_inc(t.freed, 1)
            t.wait_freed(act, n)
            act.sem_inc(rows_set, 1)

        @block.tensor
        def _(pe):
            pe.wait_ge(wv_loaded, 16)
            for s in range(SHIFTED):
                v_pe(pe, 0, 0, s, s + 1)
            pe.wait_ge(const_ready, 1)
            t.wait_loaded(pe)
            for hg in range(2):
                for qt in range(QT):
                    first_scores(pe, 0, hg, qt)
                for pair in range(2 if hg == 0 else 0):
                    rows_pe(pe, 0, 0, pair, SHIFTED + pair + 1)

            def body(b, par, used):
                for k, steps in enumerate(plan(b)):
                    ahead, next_unit = later(b, k // QT, 2), later(b, k // QT, 1)
                    second_scores(pe, b, k)
                    if k >= 1:
                        times_v(pe, b, par, k - 1)
                    if exists(ahead[0]):
                        first_scores(pe, *ahead, k % QT)
                    for step, n in steps:
                        if step[0] == "v":
                            v_pe(pe, 1 - par, used + par, step[1], n)
                        elif step[0] == "rows":
                            rows_pe(pe, *next_unit, step[1], n)
                        else:
                            t.pe(pe, step, b - 1, 1 - par, n)
                times_v(pe, b, par, ITEMS - 1)
            over_batches(pe, body)
            for k, step in enumerate(TAIL_STEPS):
                t.pe(pe, step, B - 1, 1, after_last + k + 1)

        @block.scalar
        def _(act):
            for s in range(SHIFTED):
                v_act(act, 0, 0, s, s + 1)

            for pair in range(2):
                rows_act(act, 0, pair, SHIFTED + pair + 1)

            def exps(b, k):
                for i, m in enumerate((P, P // 2)):
                    act.wait_ge(scored, b * (ITEMS * SCORED) + k * SCORED + i + 1)
                    if i == 0:
                        after(act, pv_done, b * ITEMS + k - 1)
                    act.activation(probs[0:m, k % 2, i, :], pB[i][0:m, :], ACT.Exp).then_inc(exped, 1)

            def copy_o(b, par, hg):
                act.wait_ge(pv_done, b * ITEMS + (hg + 1) * QT)
                act.activation(t.oT[:, par, hg, :], pO[:, :], ACT.Copy).then_inc(t.o_copied, 1)

            def body(b, par, used):
                for k, steps in enumerate(plan(b)):
                    exps(b, k)
                    if k >= 1 and k % QT == 0:
                        copy_o(b, par, k // QT - 1)
                    for step, n in steps:
                        if step[0] == "v":
                            v_act(act, b + 1, 1 - par, step[1], n)
                        elif step[0] == "rows":
                            rows_act(act, later(b, k // QT, 1)[1], step[1], n)
                        else:
                            t.act(act, step, b - 1, n)
                copy_o(b, par, HG - 1)
            over_batches(act, body)
            for k, step in enumerate(TAIL_STEPS):
                t.act(act, step, B - 1, after_last + k + 1)

        @block.vector
        def _(dve):
            made = sem("made")
            ready = sem("ready")
            count = [0]

            def link(ins):
                count[0] += 1
                ins.then_inc(made, 1)
                dve.wait_ge(made, count[0])
            dve.wait_ge(const_loaded, 80)
            link(dve.tensor_copy(mask[:, :, :], mask_raw))
            link(dve.memset(zeros[:, :, :], 0.0))
            link(dve.memset(v[:, :, :, :, DK:VT], 1.0))
            for i in range(3):
                link(dve.tensor_copy(slope_part[rows, i, :], slope[rows, i % 2, :]))
                if i < 2:
                    link(dve.tensor_tensor(slope[rows, (i + 1) % 2, :], slope[rows, i % 2, :],
                                           slope_part[rows, i, :], ALU.subtract))
            for s in range(2):
                link(dve.tensor_scalar(side[rows, s, :], slope_part[rows, 0, :], pick[rows, s, 1:2],
                                       pick[rows, s, 0:1], ALU.mult, ALU.add))
                for i in (1, 2):
                    link(dve.scalar_tensor_tensor(out=side[rows, s, :], in0=slope_part[rows, i, :],
                                                  scalar=pick[rows, s, i + 1:i + 2], in1=side[rows, s, :],
                                                  op0=ALU.mult, op1=ALU.add))
            for h in range(H):
                dve.tensor_scalar(qq[rows, h // HPG, h % HPG, :], pos_q[rows, :], side[rows, 0, h:h + 1], None,
                                  ALU.mult).then_inc(ready, 1)
                dve.tensor_scalar(kq[rows, h // HPG, h % HPG, :], pos_k[rows, :], side[rows, 1, h:h + 1], None,
                                  ALU.mult).then_inc(ready, 1)
            dve.wait_ge(ready, 2 * H)
            dve.sem_inc(const_ready, 1)

            def maxes(b, hg, qt):
                n = b * ITEMS + hg * QT + qt
                dve.wait_ge(first_scored, n + 1)
                if qt == 0:
                    after(dve, max_chain, (b * HG + hg) * CHAIN)
                dve.tensor_reduce(negmax[:, 0, qt * HPG:(qt + 1) * HPG].rearrange("p (a c) -> p a c", a=2),
                                  pA[qt % 2][:, :, 0:2 * WIN].rearrange("p a (c w) -> p a c w", c=2),
                                  AX.X, ALU.max, negate=True).then_inc(maxed, 1)

            def split_max(b, hg):
                u = b * HG + hg
                i = [0]

                def link(ins):
                    i[0] += 1
                    ins.then_inc(max_chain, 1)
                    dve.wait_ge(max_chain, u * CHAIN + i[0])
                dve.wait_ge(maxed, (u + 1) * QT)
                part = [max_parts[:, :, :, i].rearrange("p q j -> p (q j)") for i in range(MAXR)]
                after(dve, t.misc_done, rows_before(b, hg))
                link(dve.tensor_copy(part[0], negmax[:, 0, :]))
                link(dve.tensor_tensor(negmax[:, 1, :], negmax[:, 0, :], part[0], ALU.subtract))
                link(dve.tensor_copy(part[1], negmax[:, 1, :]))
                link(dve.tensor_tensor(negmax[:, 0, :], negmax[:, 1, :], part[1], ALU.subtract))
                link(dve.tensor_copy(part[2], negmax[:, 0, :]))
                dve.sem_inc(parts_ready, 1)
            CHAIN = 5

            def rows_before(b, hg):
                if isinstance(b, int) and b == 0 and hg < 2:
                    return hg * AHEAD
                rb, rhg = (b, hg - 2) if hg >= 2 else (b - 1, hg + 2)
                return number_of(rb, ("rows", 1), [rhg * QT + ROWS_AT[1]])

            for qt in range(QT):
                maxes(0, 0, qt)
            split_max(0, 0)
            for qt in range(QT):
                maxes(0, 1, qt)
            dve.wait_ge(x_loaded, 16)

            def body(b, par, used):
                for k, steps in enumerate(plan(b)):
                    next_unit, ahead = later(b, k // QT, 1), later(b, k // QT, 2)
                    if k % QT == 0 and exists(next_unit[0]):
                        split_max(*next_unit)
                    if exists(ahead[0]):
                        maxes(*ahead, k % QT)
                    for step, n in steps:
                        if step[0] in ("out", "turn"):
                            t.dve(dve, step, b - 1, 1 - par, n)
                    if k == INVERT_AT and not (isinstance(b, int) and b == 0):
                        t.dve_invert(dve, b - 1)
                    if k == NORMALIZE_AT and not (isinstance(b, int) and b == 0):
                        t.dve_normalize(dve, b - 1)
            over_batches(dve, body)
            t.dve_invert(dve, B - 1)
            for k, step in enumerate(TAIL_STEPS):
                t.dve(dve, step, B - 1, 1, after_last + k + 1)
                if step == ("out", QT - 1):
                    t.dve_normalize(dve, B - 1)

        @block.gpsimd
        def _(pool):
            t.begin(pool)
            def body(b, par, used):
                if not (isinstance(b, int) and b == 0):
                    t.pool_scale(pool, b - 1, 1 - par)
                    t.pool(pool, b - 1, number_of(b, ("turn", QT - 1)))
            over_batches(pool, body)
            t.pool_scale(pool, B - 1, 1)
            t.pool(pool, B - 1, after_last + len(TAIL_STEPS))
            t.finish(pool)


VCH, VTOK = 4, 101
CCH = VCH * VTOK
CTX = 32 * CCH
KT = -(-C // P)
KLAST = C - (KT - 1) * P


def project_v(nc, d, v_out):
    with ExitStack() as ctx:
        sem, mem = Sems(nc, ctx, "pv"), Mem(nc, ctx, "pv")
        cT = mem.sb("cT", [P, 2, KC, CCH])
        wT, bv = mem.sb("wT", [P, KC, D]), mem.sb("bv", [P, D])
        vs = mem.sb("vs", [P, 2, VCH, D])
        acc = mem.ps("acc", [P, 2, 2, 2, D])
        w_loaded, loaded, stored = sem("w_loaded"), sem("loaded", 2), sem("stored", 2)
        product_ready, v_ready = sem("product_ready"), sem("v_ready")
        block = ctx.enter_context(nc.Block())
        TURNS = CTX // CCH // 2

        def turns(eng, body):
            body(0)
            with eng.Fori(1, TURNS) as i:
                body(i)

        @block.sync
        def _(sp):
            sp.dma_start(wT[:, :, :], w_in(d["L0_xattn_WvT"])).then_inc(w_loaded, 16)
            sp.dma_start(bv[:, :], d["L0_xattn_bv"].rearrange("(a n) -> a n", a=1).to_broadcast([P, D]))\
              .then_inc(w_loaded, 16)

            def body(i):
                for k in range(2):
                    after(sp, product_ready, i * 4 + 2 * k - 2)
                    sp.dma_start(cT[:, k, :, :], w_in(d["cT"])[:, :, bass.ds((i * 2 + k) * CCH, CCH)])\
                      .then_inc(loaded[k], 16)
            turns(sp, body)

        @block.gpsimd
        def _(pool):
            def body(i):
                for k in range(2):
                    pool.wait_ge(v_ready, i * 4 + 2 * k + 2)
                    pool.dma_start(v_out[bass.ds((i * 2 + k) * CCH, CCH), :].rearrange("(t p) n -> p t n", p=VTOK),
                                   vs[0:VTOK, k, :, :]).then_inc(stored[k], 16)
            turns(pool, body)
            for k in range(2):
                pool.wait_ge(stored[k], TURNS * 16)

        @block.tensor
        def _(pe):
            pe.wait_ge(w_loaded, 32)

            def body(i):
                for k in range(2):
                    pe.wait_ge(loaded[k], i * 16 + 16)
                    for h in range(2):
                        after(pe, v_ready, i * 4 + 2 * k + h - 3)
                        for q in range(2):
                            tile = 2 * h + q
                            for c in range(KC):
                                mm = pe.matmul(acc[0:VTOK, k, h, q, :], cT[:, k, c, tile * VTOK:(tile + 1) * VTOK],
                                               wT[:, c, :], start=(c == 0), stop=(c == KC - 1))
                        mm.then_inc(product_ready, 1)
            turns(pe, body)

        @block.vector
        def _(dve):
            dve.wait_ge(w_loaded, 32)

            def body(i):
                for k in range(2):
                    after(dve, stored[k], i * 16)
                    for h in range(2):
                        dve.wait_ge(product_ready, i * 4 + 2 * k + h + 1)
                        dve.tensor_tensor(vs[0:VTOK, k, 2 * h:2 * h + 2, :], acc[0:VTOK, k, h, :, :],
                                          bv[0:VTOK, :].rearrange("p (a n) -> p a n", a=1).to_broadcast([VTOK, 2, D]),
                                          ALU.add).then_inc(v_ready, 1)
            turns(dve, body)


def cross_attention(nc, g, d, q_parts, k_parts, v_in, xT_out):
    ROWS_B = SPLIT + MAXR
    U = B * HG
    TILES = HPG * QT
    HALVES = 2 * TILES
    HALF = (0, (C + 1) // 2, C)
    STEPS_B = KT * HPG
    HALVES_NEXT = [3, 3, 3, 3, 2, 2, 2] + [0] * (KT - 7)
    HALVES_AFTER = [0] * 7 + [1, 2, 3, 3, 3, 2]
    AHEAD = sum(HALVES_AFTER)
    assert sum(HALVES_NEXT) + AHEAD == HALVES
    F, N = "first", "second"
    ORDER_3 = ((F, 0), "v", (N, 0), (F, 1), (N, 1), (F, 2), (N, 2), (N, 3))
    ORDER_2 = ((N, 0), (F, 0), (N, 1), "v", (N, 2), (F, 1), (N, 3))
    ORDER_1 = ((N, 0), (N, 1), "v", (N, 2), (F, 0), (N, 3))
    ROWS_AT = (9, 10)
    tail_at = {(1, 1 + i + (i >= QT)): step for i, step in enumerate(TAIL_STEPS)}
    INVERT_AT, NORMALIZE_AT = (0, 3), (1, 1 + QT)

    def plan(b):
        first, last = isinstance(b, int) and b == 0, isinstance(b, int) and b == B - 1
        n = 2 if first else 2 + 2 * HG + (b - 1) * (2 * HG + len(TAIL_STEPS))
        out, i = {}, 0
        for hg in range(HG):
            for kt in range(KT):
                row = []
                if (hg, kt) in tail_at and not first:
                    row.append(tail_at[hg, kt])
                if kt in ROWS_AT and not (last and hg == HG - 1):
                    row.append(("rows", ROWS_AT.index(kt)))
                out[hg, kt] = []
                for step in row:
                    i += 1
                    out[hg, kt].append((step, n + i))
        return out

    after_last = 2 + 2 * U - 2 + (B - 1) * len(TAIL_STEPS)
    with ExitStack() as ctx:
        sem, mem = Sems(nc, ctx, "xa"), Mem(nc, ctx, "xa")
        t = Tail(nc, ctx, g, sem, mem, d, "L0_xattn_bo", xT_out, heads="L0_xattn")
        kx = mem.sb("kx", [P, HG, HPG, C], BF16)
        qx = mem.sb("qx", [P, HG, HPG, S], BF16)
        v_raw = mem.sb("v_raw", [P, 2, KT, HPG * DK])
        v = mem.sb("v", [P, HG, KT, HPG, VT])
        NP_ = 2 * HPG
        probs = mem.sb("probs", [P, NP_, S])
        half_max = mem.sb("half_max", [P, QT, HPG, 2])
        negmax = mem.sb("negmax", [P, 2, QT * HPG])
        max_parts = mem.sb("max_parts", [P, QT, HPG, MAXR], BF16)
        pA = [mem.ps(f"pA{k}", [P, 1024]) for k in range(2)]
        pB = [mem.ps(f"pB{k}", [P, 512]) for k in range(2)]
        pO = mem.ps("pO", [P, 512])
        kq_loaded, v_loaded = sem("kq_loaded", HG), sem("v_loaded", 2)
        const_ready, v_placed = sem("const_ready"), sem("v_placed")
        half_scored, half_maxed, max_chain, parts_ready = sem("half_scored"), sem("half_maxed"), sem("max_chain"), sem("parts_ready")
        rows_set, scored, exped, pv_done = sem("rows_set"), sem("scored"), sem("exped"), sem("pv_done")
        block = ctx.enter_context(nc.Block())
        CHAIN = 6
        misc16 = t.misc[:, :].bitcast(BF16)

        def unit_of(b, hg):
            return b * HG + hg

        def later(b, hg, k):
            return (b + (hg + k) // HG, (hg + k) % HG)

        def exists(b, hg):
            return not (isinstance(b, int) and b >= B)

        def halves_at(b, hg, kt):
            out = []
            for k, counts, before in ((1, HALVES_NEXT, AHEAD), (2, HALVES_AFTER, 0)):
                to = later(b, hg, k)
                if exists(*to):
                    n = before + sum(counts[:kt])
                    out += [(*to, half) for half in range(n, n + counts[kt])]
            return out

        def turned_count(b):
            p = plan(b)
            return [n for row in p.values() for step, n in row if step == ("turn", QT - 1)][0]

        @block.sync
        def _(sp):

            def load(b, hg):
                u = unit_of(b, hg)
                after(sp, scored, (u - HG + 1) * STEPS_B)
                heads = slice(hg * HPG * DK, (hg + 1) * HPG * DK)
                for r in range(len(KPART)):
                    to = slice(r * DK, (r + 1) * DK)
                    sp.dma_start(kx[to, hg, :, :], k_parts[KPART[r], heads, bass.ds(b * C, C)]
                                 .rearrange("(h e) t -> e h t", e=DK)).then_inc(kq_loaded[hg], 16)
                    sp.dma_start(qx[to, hg, :, :], q_parts[QPART[r], heads, bass.ds(b * S, S)]
                                 .rearrange("(h e) t -> e h t", e=DK)).then_inc(kq_loaded[hg], 16)
                after(sp, v_placed, u - 1)
                full = (KT - 1) * P
                sp.dma_start(v_raw[:, hg % 2, 0:KT - 1, :], v_in[bass.ds(b * C, full), heads]
                             .rearrange("(t p) n -> p t n", p=P)).then_inc(v_loaded[hg % 2], 16)
                sp.dma_start(v_raw[0:KLAST, hg % 2, KT - 1, :], v_in[bass.ds(b * C + full, KLAST), heads])\
                  .then_inc(v_loaded[hg % 2], 16)
            load(0, 0)
            load(0, 1)
            t.load(sp)

            def body(b, par, used):
                for hg in range(HG):
                    to = later(b, hg, 2)
                    if exists(*to):
                        load(*to)
            over_batches(sp, body)

        def place_v(pool, b, hg):
            u = unit_of(b, hg)
            after(pool, pv_done, (u - HG + 1) * KT)
            pool.wait_ge(v_loaded[hg % 2], (b * 2 + hg // 2) * 32 + 32)
            pool.sem_inc(t.pool_passed, 1)
            pool.tensor_copy(v[:, hg, 0:KT - 1, :, 0:DK],
                             v_raw[:, hg % 2, 0:KT - 1, :].rearrange("p t (h e) -> p t h e", e=DK)).then_inc(v_half, 1)
            pool.tensor_copy(v[0:KLAST, hg, KT - 1, :, 0:DK],
                             v_raw[0:KLAST, hg % 2, KT - 1, :].rearrange("p (h e) -> p h e", e=DK)).then_inc(v_half, 1)
            pool.wait_ge(v_half, u * 2 + 2)
            pool.sem_inc(v_placed, 1)
        v_half, ones_set = sem("v_half"), sem("ones_set")

        @block.gpsimd
        def _(pool):
            t.begin(pool)
            pool.memset(kx[SPLIT:SPLIT + MAXR, :, :, :], 1.0).then_inc(const_ready, 1)
            pool.wait_ge(const_ready, 1)
            pool.memset(v[:, :, :, :, DK:VT], 1.0).then_inc(ones_set, 1)
            pool.wait_ge(ones_set, 1)
            place_v(pool, 0, 0)
            place_v(pool, 0, 1)

            def body(b, par, used):
                for hg in range(HG):
                    to = later(b, hg, 2)
                    if exists(*to):
                        place_v(pool, *to)
                    if hg == 0 and not (isinstance(b, int) and b == 0):
                        t.pool_scale(pool, b - 1, 1 - par)
                    if hg == 1 and not (isinstance(b, int) and b == 0):
                        t.pool(pool, b - 1, turned_count(b))
            over_batches(pool, body)
            t.pool_scale(pool, B - 1, 1)
            t.pool(pool, B - 1, after_last + len(TAIL_STEPS))
            t.finish(pool)

        def first_scores(pe, b, hg, half):
            u, tile, h = unit_of(b, hg), half // 2, half % 2
            j, qt = tile // QT, tile % QT
            if half == 0:
                pe.wait_ge(kq_loaded[hg], b * (2 * len(KPART) * 16) + 2 * len(KPART) * 16)
            after(pe, half_maxed, u * HALVES + half - 1)
            lo, hi = HALF[h], HALF[h + 1]
            for at in range(lo, hi, 512):
                w = min(512, hi - at)
                mm = pe.matmul(pA[h][:, at - lo:at - lo + w], qx[0:SPLIT, hg, j, qt * P:(qt + 1) * P],
                               kx[0:SPLIT, hg, j, at:at + w], start=True, stop=True)
            mm.then_inc(half_scored, 1)

        def second_scores(pe, b, hg, kt, j):
            n = unit_of(b, hg) * STEPS_B + kt * HPG + j
            if kt == 0 and j == 0:
                pe.wait_ge(rows_set, unit_of(b, hg) * 2 + 2)
            after(pe, exped, n - 1)
            m = P if kt < KT - 1 else KLAST
            pe.matmul(pB[j % 2][0:m, :], kx[0:ROWS_B, hg, j, kt * P:kt * P + m], qx[0:ROWS_B, hg, j, :],
                      start=True, stop=True).then_inc(scored, 1)

        def times_v(pe, b, hg, kt):
            u = unit_of(b, hg)
            if kt == 0:
                pe.wait_ge(v_placed, u + 1)
                after(pe, t.o_copied, u)
            m = P if kt < KT - 1 else KLAST
            for j in range(HPG):
                n = kt * HPG + j
                pe.wait_ge(exped, u * STEPS_B + n + 1)
                mm = pe.matmul(pO[j * VT:(j + 1) * VT, :], v[0:m, hg, kt, j, :], probs[0:m, (n + u_par(hg) * HPG) % NP_, :],
                               start=(kt == 0), stop=(kt == KT - 1), skip_group_check=True)
            mm.then_inc(pv_done, 1)

        def u_par(hg):
            return hg % 2

        def rows_pe(pe, b, hg, pair, n):
            t.wait_freed(pe, n - 1)
            pe.wait_ge(parts_ready, unit_of(b, hg) + 1)
            for jj in range(2):
                for qt in range(QT):
                    at = (jj * QT + qt) * P
                    mm = pe.transpose(misc16[SPLIT:SPLIT + MAXR, at:at + P], max_parts[:, qt, 2 * pair + jj, :],
                                      g.identb[:, :])
            mm.then_inc(t.misc_done, 1)

        def rows_act(act, b, hg, pair, n):
            act.wait_ge(t.misc_done, n)
            after(act, scored, (unit_of(b, hg) - HG + 1) * STEPS_B)
            act.activation(qx[SPLIT:SPLIT + MAXR, hg, 2 * pair:2 * pair + 2, :],
                           misc16[SPLIT:SPLIT + MAXR, :].rearrange("p (j t) -> p j t", j=2), ACT.Copy)\
               .then_inc(t.freed, 1)
            t.wait_freed(act, n)
            act.sem_inc(rows_set, 1)

        @block.tensor
        def _(pe):
            for half in range(HALVES):
                first_scores(pe, 0, 0, half)
            for pair in range(2):
                rows_pe(pe, 0, 0, pair, pair + 1)
            for half in range(AHEAD):
                first_scores(pe, 0, 1, half)
            pe.wait_ge(const_ready, 1)
            t.wait_loaded(pe)

            def body(b, par, used):
                steps = plan(b)
                for hg in range(HG):
                    nb, nhg = later(b, hg, 1)
                    for kt in range(KT):
                        halves = halves_at(b, hg, kt)
                        for what in (ORDER_1, ORDER_1, ORDER_2, ORDER_3)[len(halves)]:
                            if what == "v" and kt >= 1:
                                times_v(pe, b, hg, kt - 1)
                            elif what == "v" and hg >= 1:
                                times_v(pe, b, hg - 1, KT - 1)
                            elif what[0] == "second":
                                second_scores(pe, b, hg, kt, what[1])
                            elif what[0] == "first" and what[1] < len(halves):
                                first_scores(pe, *halves[what[1]])
                        for step, n in steps[hg, kt]:
                            if step[0] == "rows":
                                rows_pe(pe, nb, nhg, step[1], n)
                            else:
                                t.pe(pe, step, b - 1, 1 - par, n)
                times_v(pe, b, HG - 1, KT - 1)
            over_batches(pe, body)
            for k, step in enumerate(TAIL_STEPS):
                t.pe(pe, step, B - 1, 1, after_last + k + 1)

        @block.scalar
        def _(act):
            def exps(b, hg, kt, j):
                n = unit_of(b, hg) * STEPS_B + kt * HPG + j
                m = P if kt < KT - 1 else KLAST
                act.wait_ge(scored, n + 1)
                if j == 0:
                    after(act, pv_done, unit_of(b, hg) * KT + kt - 1)
                at = (kt * HPG + j + u_par(hg) * HPG) % NP_
                act.activation(probs[0:m, at, :], pB[j % 2][0:m, :], ACT.Exp).then_inc(exped, 1)

            def copy_o(b, par, hg):
                act.wait_ge(pv_done, (unit_of(b, hg) + 1) * KT)
                act.activation(t.oT[:, par, hg, :], pO[:, :], ACT.Copy).then_inc(t.o_copied, 1)

            for pair in range(2):
                rows_act(act, 0, 0, pair, pair + 1)

            def body(b, par, used):
                steps = plan(b)
                for hg in range(HG):
                    nb, nhg = later(b, hg, 1)
                    for kt in range(KT):
                        for j in range(HPG):
                            exps(b, hg, kt, j)
                            if kt == 0 and j == 1 and hg >= 1:
                                copy_o(b, par, hg - 1)
                        for step, n in steps[hg, kt]:
                            if step[0] == "rows":
                                rows_act(act, nb, nhg, step[1], n)
                            else:
                                t.act(act, step, b - 1, n)
                copy_o(b, par, HG - 1)
            over_batches(act, body)
            for k, step in enumerate(TAIL_STEPS):
                t.act(act, step, B - 1, after_last + k + 1)

        @block.vector
        def _(dve):
            t.wait_loaded(dve)

            def maxes(b, hg, half):
                u, tile, h = unit_of(b, hg), half // 2, half % 2
                j, qt = tile // QT, tile % QT
                dve.wait_ge(half_scored, u * HALVES + half + 1)
                if half == 0:
                    after(dve, max_chain, u * CHAIN)
                dve.tensor_reduce(half_max[:, qt, j, h:h + 1], pA[h][:, 0:HALF[h + 1] - HALF[h]], AX.X, ALU.max,
                                  negate=True).then_inc(half_maxed, 1)

            def split_max(b, hg):
                u = unit_of(b, hg)
                i = [0]

                def link(ins):
                    i[0] += 1
                    ins.then_inc(max_chain, 1)
                    dve.wait_ge(max_chain, u * CHAIN + i[0])
                dve.wait_ge(half_maxed, (u + 1) * HALVES)
                link(dve.tensor_reduce(negmax[:, 0, :], half_max[:, :, :, :].rearrange("p q j h -> p (q j) h"),
                                       AX.X, ALU.min))
                part = [max_parts[:, :, :, i].rearrange("p q j -> p (q j)") for i in range(MAXR)]
                after(dve, t.misc_done, rows_before(b, hg))
                link(dve.tensor_copy(part[0], negmax[:, 0, :]))
                link(dve.tensor_tensor(negmax[:, 1, :], negmax[:, 0, :], part[0], ALU.subtract))
                link(dve.tensor_copy(part[1], negmax[:, 1, :]))
                link(dve.tensor_tensor(negmax[:, 0, :], negmax[:, 1, :], part[1], ALU.subtract))
                link(dve.tensor_copy(part[2], negmax[:, 0, :]))
                dve.sem_inc(parts_ready, 1)

            def rows_before(b, hg):
                if isinstance(b, int) and b == 0 and hg == 0:
                    return 0
                if isinstance(b, int) and b == 0 and hg == 1:
                    return 2
                if hg >= 2:
                    rb, rhg = b, hg - 2
                else:
                    rb, rhg = b - 1, hg + 2
                return [n for step, n in plan(rb)[rhg, ROWS_AT[1]] if step == ("rows", 1)][0]

            for half in range(HALVES):
                maxes(0, 0, half)
            split_max(0, 0)
            for half in range(AHEAD):
                maxes(0, 1, half)

            def body(b, par, used):
                steps = plan(b)
                for hg in range(HG):
                    for kt in range(KT):
                        for nb, nhg, half in halves_at(b, hg, kt):
                            maxes(nb, nhg, half)
                            if half == HALVES - 1:
                                split_max(nb, nhg)
                        for step, n in steps[hg, kt]:
                            if step[0] != "rows":
                                t.dve(dve, step, b - 1, 1 - par, n)
                        if (hg, kt) == INVERT_AT and not (isinstance(b, int) and b == 0):
                            t.dve_invert(dve, b - 1)
                        if (hg, kt) == NORMALIZE_AT and not (isinstance(b, int) and b == 0):
                            t.dve_normalize(dve, b - 1)
            over_batches(dve, body)
            t.dve_invert(dve, B - 1)
            for k, step in enumerate(TAIL_STEPS):
                t.dve(dve, step, B - 1, 1, after_last + k + 1)
                if step == ("out", QT - 1):
                    t.dve_normalize(dve, B - 1)


NE, TOPK, HID = 8, 2, 512
HC = HID // P


def gates(nc, g, d, xT_in, gT):
    TT = B * QT
    with ExitStack() as ctx:
        sem, mem = Sems(nc, ctx, "ga"), Mem(nc, ctx, "ga")
        xT = mem.sb("xT", [P, KC, T])
        wg, bg = mem.sb("wg", [P, KC, NE]), mem.sb("bg", [NE, 1])
        lT = mem.sb("lT", [NE, T])
        logit, gate = mem.sb("logit", [P, TT, NE]), mem.sb("gate", [P, TT, NE])
        col, col2 = mem.sb("col", [P, TT]), mem.sb("col2", [P, TT])
        tri = mem.sb("tri", [P, NE, NE])
        more, atleast = mem.sb("more", [P, TT, NE, NE]), mem.sb("atleast", [P, TT, NE, NE])
        acc = mem.ps("acc", [P, 2, 512])
        turned = mem.ps("turned", [P, TT, NE])
        back = mem.ps("back", [P, 2, 512])
        w_loaded, loaded = sem("w_loaded"), sem("loaded", 4)
        product, copied, all_turned = sem("product"), sem("copied"), sem("all_turned")
        chain, shifted, exped, weights_ready, back_turned, back_copied, stored = (
            sem(n) for n in ("chain", "shifted", "exped", "weights_ready", "back_turned", "back_copied", "stored"))
        block = ctx.enter_context(nc.Block())

        @block.sync
        def _(sp):
            sp.dma_start(wg[:, :, :], w_in(d["L0_ffn_Wg"])).then_inc(w_loaded, 16)
            sp.dma_start(bg[:, :], d["L0_ffn_bg"].rearrange("(p a) -> p a", a=1)).then_inc(w_loaded, 16)
            sp.dma_start(tri[:, :, :], d["tri"]).then_inc(w_loaded, 16)
            for k in range(4):
                w = T // 4
                sp.dma_start(xT[:, :, k * w:(k + 1) * w], w_in(xT_in)[:, :, HALO + k * w:HALO + (k + 1) * w])\
                  .then_inc(loaded[k], 16)
            sp.wait_ge(back_copied, B)
            sp.dma_start(gT, lT[:, :]).then_inc(stored, 16)
            sp.wait_ge(stored, 16)

        @block.tensor
        def _(pe):
            pe.wait_ge(w_loaded, 48)
            for b in range(B):
                if b % 2 == 0:
                    pe.wait_ge(loaded[b // 2], 16)
                after(pe, copied, b - 1)
                for c in range(KC):
                    mm = pe.matmul(acc[0:NE, b % 2, :], wg[:, c, :], xT[:, c, b * S:(b + 1) * S],
                                   start=(c == 0), stop=(c == KC - 1))
                mm.then_inc(product, 1)
            for b in range(B):
                pe.wait_ge(copied, b + 1)
                for q in range(QT):
                    at = b * QT + q
                    mm = pe.transpose(turned[:, at, :], lT[:, at * P:(at + 1) * P], g.ident[0:NE, 0:NE])
            mm.then_inc(all_turned, 1)
            pe.wait_ge(weights_ready, 1)
            for b in range(B):
                after(pe, back_copied, b - 1)
                for q in range(QT):
                    mm = pe.transpose(back[0:NE, b % 2, q * P:(q + 1) * P], gate[:, b * QT + q, :], g.ident[:, :])
                mm.then_inc(back_turned, 1)

        @block.scalar
        def _(act):
            act.wait_ge(w_loaded, 48)
            for b in range(B):
                act.wait_ge(product, b + 1)
                act.activation(lT[:, b * S:(b + 1) * S], acc[0:NE, b % 2, :], ACT.Identity, bias=bg[:, :])\
                   .then_inc(copied, 1)
            act.wait_ge(shifted, 1)
            act.activation(gate[:, :, :], logit[:, :, :], ACT.Exp).then_inc(exped, 1)
            for b in range(B):
                act.wait_ge(back_turned, b + 1)
                act.activation(lT[:, b * S:(b + 1) * S], back[0:NE, b % 2, :], ACT.Copy).then_inc(back_copied, 1)

        @block.vector
        def _(dve):
            n = [0]

            def link(ins):
                n[0] += 1
                ins.then_inc(chain, 1)
                dve.wait_ge(chain, n[0])

            def spread(ap, axis, shape):
                return ap.rearrange("p t (a e) -> p t a e" if axis == 2 else "p t (e a) -> p t e a", a=1)\
                         .to_broadcast(shape)
            dve.wait_ge(all_turned, 1)
            link(dve.tensor_reduce(col[:, :], turned[:, :, :], AX.X, ALU.max))
            wide = [P, TT, NE]
            dve.tensor_tensor(logit[:, :, :], turned[:, :, :],
                              col[:, :].rearrange("p (t a) -> p t a", a=1).to_broadcast(wide), ALU.subtract)\
               .then_inc(shifted, 1)
            dve.wait_ge(exped, 1)
            link(dve.tensor_reduce(col2[:, :], gate[:, :, :], AX.X, ALU.add))
            link(dve.reciprocal(col[:, :], col2[:, :]))
            link(dve.tensor_tensor(gate[:, :, :], gate[:, :, :],
                                   col[:, :].rearrange("p (t a) -> p t a", a=1).to_broadcast(wide), ALU.mult))
            pairs = [P, TT, NE, NE]
            mine, other = spread(gate[:, :, :], 3, pairs), spread(gate[:, :, :], 2, pairs)
            link(dve.tensor_tensor(more[:, :, :, :], other, mine, ALU.is_gt))
            link(dve.tensor_tensor(atleast[:, :, :, :], other, mine, ALU.is_ge))
            link(dve.tensor_tensor(atleast[:, :, :, :], atleast[:, :, :, :], more[:, :, :, :], ALU.subtract))
            later = tri[:, :, :].rearrange("p (a e) f -> p a e f", a=1).to_broadcast(pairs)
            link(dve.tensor_tensor(atleast[:, :, :, :], atleast[:, :, :, :], later, ALU.mult))
            link(dve.tensor_tensor(atleast[:, :, :, :], atleast[:, :, :, :], more[:, :, :, :], ALU.add))
            link(dve.tensor_reduce(logit[:, :, :], atleast[:, :, :, :], AX.X, ALU.add))
            dve.scalar_tensor_tensor(out=gate[:, :, :], in0=logit[:, :, :], scalar=float(TOPK), in1=gate[:, :, :],
                                     op0=ALU.is_lt, op1=ALU.mult).then_inc(weights_ready, 1)


def experts(nc, g, d, xT_in, gT, xT_out):
    STEPS = NE * HC
    at_step = {}
    for q in range(QT):
        at_step[2 + 2 * q] = [("out", q)]
        at_step[16 + 2 * q] = [("turn", q)]
    NORMALIZE_AT = 12
    with ExitStack() as ctx:
        sem, mem = Sems(nc, ctx, "ex"), Mem(nc, ctx, "ex")
        mixT = mem.sb("mixT", [P, KC, S])
        wf = mem.sb("wf", [P, KC, D])
        t = Tail(nc, ctx, g, sem, mem, d, "L0_ffn_bf", xT_out,
                 terms=lambda par, k: [(mixT[:, c, k * P:(k + 1) * P], wf[:, c, :]) for c in range(KC)])
        w1, w3 = mem.sb("w1", [P, NE, KC, HID]), mem.sb("w3", [P, NE, KC, HID])
        w2 = mem.sb("w2", [P, NE, HC, D])
        b1, b3 = mem.sb("b1", [P, NE, HC]), mem.sb("b3", [P, NE, HC])
        b2 = mem.sb("b2", [NE, D])
        wide_gate = mem.sb("wide_gate", [P, 2, S])
        xT = mem.sb("xT", [P, 2, KC, S])
        gate = mem.sb("gate", [NE, 2, S])
        h1 = mem.sb("h1", [P, 2, S])
        u = mem.sb("u", [P, 2, S])
        hid = mem.sb("hid", [P, 2, S])
        p1 = [mem.ps(f"p1_{k}", [P, 512]) for k in range(2)]
        p3 = [mem.ps(f"p3_{k}", [P, 512]) for k in range(2)]
        pm = [mem.ps(f"pm{k}", [P, 512]) for k in range(KC)]
        w_loaded, x_loaded = sem("w_loaded", NE), sem("x_loaded", 2)
        s_loaded, gate_loaded = sem("s_loaded"), sem("gate_loaded", 2)
        p1_done, p3_done, h1_ready, u_ready, silu_ready, hid_ready, mixed, batch_mixed, mix_copied = (
            sem(n) for n in ("p1_done", "p3_done", "h1_ready", "u_ready", "silu_ready", "hid_ready", "mixed",
                             "batch_mixed", "mix_copied"))
        block = ctx.enter_context(nc.Block())

        def is_first(b):
            return isinstance(b, int) and b == 0

        def plan(b):
            n, k, out = (b - 1) * len(PLAIN_STEPS), 0, []
            for s in range(STEPS):
                row = []
                for step in ([] if is_first(b) else at_step.get(s, [])):
                    k += 1
                    row.append((step, n + k))
                out.append(row)
            return out
        after_last = (B - 1) * len(PLAIN_STEPS)

        @block.sync
        def _(sp):
            sp.dma_start(xT[:, 0, :, :], w_in(xT_in)[:, :, HALO:HALO + S]).then_inc(x_loaded[0], 16)
            sp.dma_start(gate[:, 0, :], gT[:, 0:S]).then_inc(x_loaded[0], 16)
            sp.dma_start(b1[:, :, :], d["L0_ffn_b1"].rearrange("e (c p) -> p e c", p=P), allow_slow_non_contiguous=True).then_inc(s_loaded, 16)
            sp.dma_start(b3[:, :, :], d["L0_ffn_b3"].rearrange("e (c p) -> p e c", p=P), allow_slow_non_contiguous=True).then_inc(s_loaded, 16)
            sp.dma_start(b2[:, :], d["L0_ffn_b2"]).then_inc(s_loaded, 16)
            sp.dma_start(wf[:, :, :], w_in(d["L0_ffn_Wf"])).then_inc(s_loaded, 16)
            t.load(sp)

            def load_gate(b, e):
                after(sp, hid_ready, b * STEPS + (e - 1) * HC)
                sp.dma_start(wide_gate[:, e % 2, :], gT[e:e + 1, bass.ds(b * S, S)].to_broadcast([P, S]))\
                  .then_inc(gate_loaded[e % 2], 16)
            for e in range(2):
                load_gate(0, e)
            for e in range(NE):
                sp.dma_start(w1[:, e, :, :], w_in(d["L0_ffn_W1"][e])).then_inc(w_loaded[e], 16)
                sp.dma_start(w3[:, e, :, :], w_in(d["L0_ffn_W3"][e])).then_inc(w_loaded[e], 16)
                sp.dma_start(w2[:, e, :, :], w_in(d["L0_ffn_W2"][e])).then_inc(w_loaded[e], 16)

            def body(b, par, used):
                if not is_first(b):
                    load_gate(b, 0)
                    load_gate(b, 1)
                load_next(b, par)
                for e in range(2, NE):
                    load_gate(b, e)

            def load_next(b, par):
                if isinstance(b, int) and b == B - 1:
                    return
                after(sp, batch_mixed, b)
                sp.dma_start(xT[:, 1 - par, :, :], w_in(xT_in)[:, :, bass.ds(b * S + (HALO + S), S)]).then_inc(x_loaded[1 - par], 16)
                sp.dma_start(gate[:, 1 - par, :], gT[:, bass.ds(b * S + S, S)]).then_inc(x_loaded[1 - par], 16)
            over_batches(sp, body)

        @block.tensor
        def _(pe):
            pe.wait_ge(s_loaded, 64)
            t.wait_loaded(pe)

            def mix(b, s):
                e, hc = s // HC, s % HC
                pe.wait_ge(hid_ready, b * STEPS + s + 1)
                if s == 0:
                    after(pe, mix_copied, b)
                for oc in range(KC):
                    mm = pe.matmul(pm[oc][:, :], w2[:, e, hc, oc * P:(oc + 1) * P], hid[:, s % 2, :],
                                   start=(s == 0), stop=False)
                mm.then_inc(mixed, 1)

            def body(b, par, used):
                pe.wait_ge(x_loaded[par], used * 32 + 32)
                for s, steps in enumerate(plan(b)):
                    e, hc = s // HC, s % HC
                    if is_first(b) and hc == 0:
                        pe.wait_ge(w_loaded[e], 48)
                    for w, p, free, done in ((w1, p1, h1_ready, p1_done), (w3, p3, u_ready, p3_done)):
                        after(pe, free, b * STEPS + s - 1)
                        for c in range(KC):
                            mm = pe.matmul(p[s % 2][:, :], w[:, e, c, hc * P:(hc + 1) * P], xT[:, par, c, :],
                                           start=(c == 0), stop=(c == KC - 1))
                        mm.then_inc(done, 1)
                    if s >= 1:
                        mix(b, s - 1)
                    for step, n in steps:
                        t.pe(pe, step, b - 1, 1 - par, n)
                mix(b, STEPS - 1)
                for oc in range(KC):
                    mm = pe.matmul(pm[oc][:, :], b2[:, oc * P:(oc + 1) * P], gate[:, par, :], start=False, stop=True)
                mm.then_inc(batch_mixed, 1)
            over_batches(pe, body)
            for k, step in enumerate(PLAIN_STEPS):
                if k == 0:
                    pe.wait_ge(mix_copied, B)
                t.pe(pe, step, B - 1, 1, after_last + k + 1)

        @block.scalar
        def _(act):
            act.wait_ge(s_loaded, 64)

            def body(b, par, used):
                for s, steps in enumerate(plan(b)):
                    e, hc = s // HC, s % HC
                    n = b * STEPS + s
                    act.wait_ge(p1_done, n + 1)
                    after(act, u_ready, n - 1)
                    act.activation(h1[:, s % 2, :], p1[s % 2][:, :], ACT.Identity, bias=b1[:, e, hc:hc + 1])\
                       .then_inc(h1_ready, 1)
                    act.wait_ge(u_ready, n + 1)
                    act.activation(u[:, s % 2, :], u[:, s % 2, :], ACT.Silu).then_inc(silu_ready, 1)
                    for step, k in steps:
                        t.act(act, step, b - 1, k)
                act.wait_ge(batch_mixed, b + 1)
                for oc in range(KC):
                    ins = act.activation(mixT[:, oc, :], pm[oc][:, :], ACT.Copy)
                ins.then_inc(mix_copied, 1)
            over_batches(act, body)
            for k, step in enumerate(PLAIN_STEPS):
                t.act(act, step, B - 1, after_last + k + 1)

        @block.vector
        def _(dve):
            dve.wait_ge(s_loaded, 64)
            t.wait_loaded(dve)

            def body(b, par, used):
                for s, steps in enumerate(plan(b)):
                    e, hc = s // HC, s % HC
                    n = b * STEPS + s
                    dve.wait_ge(p3_done, n + 1)
                    dve.wait_ge(h1_ready, n + 1)
                    after(dve, hid_ready, n - 1)
                    dve.scalar_tensor_tensor(out=u[:, s % 2, :], in0=p3[s % 2][:, :], scalar=b3[:, e, hc:hc + 1],
                                             in1=h1[:, s % 2, :], op0=ALU.add, op1=ALU.mult).then_inc(u_ready, 1)
                    if hc == 0:
                        dve.wait_ge(gate_loaded[e % 2], (b * (NE // 2) + e // 2) * 16 + 16)
                    dve.wait_ge(silu_ready, n + 1)
                    after(dve, mixed, n - 1)
                    dve.tensor_tensor(hid[:, s % 2, :], u[:, s % 2, :], wide_gate[:, e % 2, :], ALU.mult).then_inc(hid_ready, 1)
                    for step, k in steps:
                        t.dve(dve, step, b - 1, 1 - par, k)
                    if s == NORMALIZE_AT and not is_first(b):
                        t.dve_normalize(dve, b - 1)
            over_batches(dve, body)
            for k, step in enumerate(PLAIN_STEPS):
                t.dve(dve, step, B - 1, 1, after_last + k + 1)
                if step == ("out", QT - 1):
                    t.dve_normalize(dve, B - 1)

        @block.gpsimd
        def _(pool):
            t.begin(pool)
            with pool.Fori(0, B) as b:
                t.pool(pool, b, b * len(PLAIN_STEPS) + len(PLAIN_STEPS))
            t.finish(pool)


NQ = D // 4
BQ = QT * NQ


def quat_combine(dve, chain, out, M, conj, last):
    plus, minus = (ALU.subtract, ALU.add) if conj else (ALU.add, ALU.subtract)
    dve.tensor_tensor(out[:, :, 1:3], M[:, 0, :, 1:3], M[:, 1, :, 0:4:3], plus)
    chain.link(dve.tensor_tensor(out[:, :, 0:4:3], M[:, 0, :, 0:4:3], M[:, 1, :, 1:3], minus))
    dve.tensor_tensor(out[:, :, 0:2], out[:, :, 0:2], M[:, 2, :, 2:4], minus)
    chain.link(dve.tensor_tensor(out[:, :, 2:4], out[:, :, 2:4], M[:, 2, :, 0:2], plus))
    for c, op in ((0, minus), (1, plus), (2, minus)):
        dve.tensor_tensor(out[:, :, c], out[:, :, c], M[:, 3, :, 3 - c], op)
    dve.tensor_tensor(out[:, :, 3], out[:, :, 3], M[:, 3, :, 0], plus).then_inc(last, 1)


def bind(nc, d, xT_in, khat, bound):
    with ExitStack() as ctx:
        sem, mem = Sems(nc, ctx, "qb"), Mem(nc, ctx, "qb")
        w, bias = mem.sb("w", [P, KC, 2, D]), mem.sb("bias", [P, 2, D])
        xT = mem.sb("xT", [P, 2, KC, S])
        kv = mem.sb("kv", [P, 2, QT, 2, D])
        sq, ss, nrm, inv = mem.sb("sq", [P, BQ, 4]), mem.sb("ss", [P, BQ]), mem.sb("nrm", [P, BQ]), mem.sb("inv", [P, BQ])
        M = mem.sb("M", [P, 4, BQ, 4])
        acc = mem.ps("acc", [P, QT, 2, D])
        w_loaded, x_loaded = sem("w_loaded"), sem("x_loaded", 2)
        kv_done, kv_ready, sq_ready, ss_ready, nrm_ready, inv_ready, kh_ready, pool_products, own, bound_ready = (
            sem(n) for n in ("kv_done", "kv_ready", "sq_ready", "ss_ready", "nrm_ready", "inv_ready", "kh_ready",
                             "pool_products", "own", "bound_ready"))
        block = ctx.enter_context(nc.Block())

        def of(tensor, b):
            return tensor[:, bass.ds(b * BQ, BQ), :]

        def keys(par):
            return kv[:, par, :, 0, :].rearrange("p t (n c) -> p t n c", c=4)

        def values(par):
            return kv[:, par, :, 1, :].rearrange("p t (n c) -> p t n c", c=4)

        @block.sync
        def _(sp):
            sp.dma_start(w[:, :, 0, :], w_in(d["L1_attn_WkT"])).then_inc(w_loaded, 16)
            sp.dma_start(w[:, :, 1, :], w_in(d["L1_attn_WvT"])).then_inc(w_loaded, 16)
            for k, n in enumerate(("bk", "bv")):
                sp.dma_start(bias[:, k, :], d["L1_attn_" + n].rearrange("(a n) -> a n", a=1).to_broadcast([P, D]))\
                  .then_inc(w_loaded, 16)

            def body(b, par, used):
                after(sp, kv_done, (b - 1) * QT + 1)
                sp.dma_start(xT[:, par, :, :], w_in(xT_in)[:, :, bass.ds(b * S + HALO, S)]).then_inc(x_loaded[par], 16)
            over_batches(sp, body)

        @block.tensor
        def _(pe):
            pe.wait_ge(w_loaded, 64)

            def body(b, par, used):
                pe.wait_ge(x_loaded[par], used * 16 + 16)
                for q in range(QT):
                    after(pe, kv_ready, (b - 1) * QT + q + 1)
                    for c in range(KC):
                        mm = pe.matmul(acc[:, q, :, :], xT[:, par, c, q * P:(q + 1) * P], w[:, c, :, :],
                                       start=(c == 0), stop=(c == KC - 1))
                    mm.then_inc(kv_done, 1)
            over_batches(pe, body)

        @block.scalar
        def _(act):
            def body(b, par, used):
                act.wait_ge(kv_ready, b * QT + QT)
                after(act, ss_ready, b)
                act.activation(sq[:, :, :].rearrange("p (t n) c -> p t n c", t=QT), keys(par), ACT.Square)\
                   .then_inc(sq_ready, 1)
                act.wait_ge(ss_ready, b + 1)
                after(act, inv_ready, b)
                act.activation(nrm[:, :], ss[:, :], ACT.Sqrt).then_inc(nrm_ready, 1)
            over_batches(act, body)

        @block.vector
        def _(dve):
            chain = Chain(dve, own, 3)
            dve.wait_ge(w_loaded, 64)

            def products(b, par):
                dve.wait_ge(kh_ready, b + 1)
                for c in (0, 1):
                    ins = dve.tensor_tensor(M[:, c, :, :].rearrange("p (t n) c -> p t n c", t=QT), values(par),
                                            of(khat, b)[:, :, c:c + 1].rearrange("p (t n) c -> p t n c", t=QT)
                                            .to_broadcast([P, QT, NQ, 4]), ALU.mult)
                chain.link(ins)
                dve.wait_ge(pool_products, b + 2)
                quat_combine(dve, chain, of(bound, b), M, False, bound_ready)
                dve.wait_ge(bound_ready, b + 1)

            def body(b, par, used):
                for q in range(QT):
                    dve.wait_ge(kv_done, b * QT + q + 1)
                    after(dve, pool_products, b)
                    dve.tensor_tensor(kv[:, par, q, :, :], acc[:, q, :, :], bias[:, :, :], ALU.add).then_inc(kv_ready, 1)
                dve.wait_ge(sq_ready, b + 1)
                after(dve, nrm_ready, b)
                dve.tensor_reduce(ss[:, :], sq[:, :, :], AX.X, ALU.add).then_inc(ss_ready, 1)
                if not (isinstance(b, int) and b == 0):
                    chain.start(b - 1)
                    products(b - 1, 1 - par)
                    chain.end()
                dve.wait_ge(nrm_ready, b + 1)
                after(dve, kh_ready, b)
                dve.tensor_scalar(inv[:, :], nrm[:, :], 1e-12, None, ALU.max).then_inc(maxed, 1)
                dve.wait_ge(maxed, b + 1)
                dve.reciprocal(inv[:, :], inv[:, :]).then_inc(inv_ready, 1)
            maxed = sem("maxed")
            over_batches(dve, body)
            chain.start(B - 1)
            products(B - 1, 1)

        @block.gpsimd
        def _(pool):
            pool.sem_inc(pool_products, 1)

            def body(b, par, used):
                pool.wait_ge(inv_ready, b + 1)
                pool.tensor_tensor(of(khat, b).rearrange("p (t n) c -> p t n c", t=QT), keys(par),
                                   inv[:, :].rearrange("p (t n a) -> p t n a", t=QT, a=1).to_broadcast([P, QT, NQ, 4]),
                                   ALU.mult).then_inc(kh_ready, 1)
                pool.wait_ge(kh_ready, b + 1)
                after(pool, bound_ready, b)
                for c in (2, 3):
                    ins = pool.tensor_tensor(M[:, c, :, :].rearrange("p (t n) c -> p t n c", t=QT), values(par),
                                             of(khat, b)[:, :, c:c + 1].rearrange("p (t n) c -> p t n c", t=QT)
                                             .to_broadcast([P, QT, NQ, 4]), ALU.mult)
                ins.then_inc(pool_products, 1)
            over_batches(pool, body)


def retrieve(nc, g, d, khat, bound, xT_out):
    with ExitStack() as ctx:
        sem, mem = Sems(nc, ctx, "qr"), Mem(nc, ctx, "qr")
        nT = mem.sb("nT", [P, KC, S])
        wo = mem.sb("wo", [P, KC, D])
        t = Tail(nc, ctx, g, sem, mem, d, True, xT_out, factor=2.0,
                 terms=lambda par, k: [(nT[:, c, k * P:(k + 1) * P], wo[:, c, :]) for c in range(KC)])
        ln_g, ln_b = mem.sb("ln_g", [P, KC]), mem.sb("ln_b", [P, KC])
        ln_b_cols, bo = mem.sb("ln_b_cols", [P, KC, P]), mem.sb("bo_row", [P, D])
        upper, ones, root = mem.sb("upper", [P, P]), mem.sb("ones", [P, P]), mem.sb("root", [P, QT])
        memory = mem.sb("memory", [P, 2, BQ, 4])
        M = mem.sb("M", [P, 4, BQ, 4])
        ret = mem.sb("ret", [P, BQ, 4])
        scaled, normed = mem.sb("scaled", [P, QT, D]), mem.sb("normed", [P, QT, D])
        st, mv = mem.sb("st", [P, QT, 6]), mem.sb("mv1", [P, QT, 2])
        veps, rstd = mem.sb("veps1", [P, QT]), mem.sb("rstd1", [P, QT])
        sums, pn = mem.ps("sums", [P, QT, D]), mem.ps("pn", [P, KC, S])
        c_loaded, row_ready, const_ready = sem("c_loaded"), sem("row_ready"), sem("const_ready")
        summed, mem_copied, pool_products, own, ret_ready, scaled_ready, var_ready, rstd_ready, normed_ready, turned, nT_ready = (
            sem(n) for n in ("summed", "mem_copied", "pool_products", "own", "ret_ready", "scaled_ready", "var1_ready",
                             "rstd1_ready", "normed_ready", "turned", "nT_ready"))
        block = ctx.enter_context(nc.Block())

        def of(tensor, b):
            return tensor[:, bass.ds(b * BQ, BQ), :]

        def is_first(b):
            return isinstance(b, int) and b == 0

        def number(b, i):
            return (b - 1) * len(PLAIN_STEPS) + i + 1

        @block.sync
        def _(sp):
            sp.dma_start(wo[:, :, :], w_in(d["L1_attn_WoT"])).then_inc(c_loaded, 16)
            sp.dma_start(ln_g[:, :], d["L1_attn_ln_g"].rearrange("(c p) -> p c", p=P), allow_slow_non_contiguous=True).then_inc(c_loaded, 16)
            sp.dma_start(ln_b[:, :], d["L1_attn_ln_b"].rearrange("(c p) -> p c", p=P), allow_slow_non_contiguous=True).then_inc(c_loaded, 16)
            sp.dma_start(bo[:, :], d["L1_attn_bo"].rearrange("(a n) -> a n", a=1).to_broadcast([P, D])).then_inc(c_loaded, 16)
            sp.dma_start(upper[:, :], d["upper"]).then_inc(c_loaded, 16)
            sp.dma_start(root[:, :], d["root"]).then_inc(c_loaded, 16)
            sp.wait_ge(c_loaded, 96)
            with sp.Fori(0, B) as b:
                t.pool_store(sp, b, number(b + 1, 2 * QT - 1))

        def running_sum(pe, b):
            after(pe, mem_copied, b)
            for q in range(QT):
                for k in range(q + 1):
                    mm = pe.matmul(sums[:, q, :], (upper if k == q else ones)[:, :],
                                   bound[:, bass.ds(b * BQ + k * NQ, NQ), :].rearrange("p n c -> p (n c)"),
                                   start=(k == 0), stop=(k == q))
            mm.then_inc(summed, 1)

        def more(b):
            return not (isinstance(b, int) and b == B - 1)

        @block.tensor
        def _(pe):
            pe.wait_ge(const_ready, 1)
            for c in range(KC):
                mm = pe.matmul(pn[:, 0, 0:D], ln_b_cols[:, c, :], wo[:, c, :], start=(c == 0), stop=(c == KC - 1))
            mm.then_inc(row_ready, 1)
            pe.wait_ge(const_ready, 2)
            running_sum(pe, 0)

            def turn_normed(b):
                pe.wait_ge(normed_ready, b * QT + QT)
                for q in range(QT):
                    for c in range(KC):
                        mm = pe.transpose(pn[:, c, q * P:(q + 1) * P], normed[:, q, c * P:(c + 1) * P], g.ident[:, :])
                mm.then_inc(turned, 1)

            def body(b, par, used):
                if not is_first(b):
                    turn_normed(b - 1)
                if more(b):
                    running_sum(pe, b + 1)
                if not is_first(b):
                    pe.wait_ge(nT_ready, b)
                    for i, step in enumerate(PLAIN_STEPS):
                        t.pe(pe, step, b - 1, 0, number(b, i))
            over_batches(pe, body)
            turn_normed(B - 1)
            pe.wait_ge(nT_ready, B)
            for i, step in enumerate(PLAIN_STEPS):
                t.pe(pe, step, B - 1, 0, number(B, i))

        @block.scalar
        def _(act):
            def copy_memory(b, par):
                act.wait_ge(summed, b + 1)
                after(act, pool_products, b - 1)
                after(act, ret_ready, b - 1)
                act.activation(memory[:, par, :, :], sums[:, :, :].rearrange("p t (n c) -> p (t n) c", c=4), ACT.Copy)\
                   .then_inc(mem_copied, 1)
            act.wait_ge(c_loaded, 96)
            copy_memory(0, 0)

            def copy_normed(b):
                act.wait_ge(turned, b + 1)
                act.activation(nT[:, :, :], pn[:, :, :], ACT.Copy).then_inc(nT_ready, 1)

            def body(b, par, used):
                if not is_first(b):
                    copy_normed(b - 1)
                if more(b):
                    copy_memory(b + 1, 1 - par)
                act.wait_ge(ret_ready, b + 1)
                after(act, normed_ready, b * QT)
                for q in range(QT):
                    act.activation(scaled[:, q, :], ret[:, q * NQ:(q + 1) * NQ, :].rearrange("p n c -> p (n c)"),
                                   ACT.Copy, scale=root[:, q:q + 1]).then_inc(scaled_ready, 1)
                if not is_first(b):
                    for i in range(QT, 2 * QT):
                        t.act(act, PLAIN_STEPS[i], b - 1, number(b, i))
            over_batches(act, body)
            copy_normed(B - 1)
            for i in range(QT, 2 * QT):
                t.act(act, PLAIN_STEPS[i], B - 1, number(B, i))

        @block.vector
        def _(dve):
            made = sem("made")
            dve.wait_ge(c_loaded, 96)
            dve.memset(ones[:, :], 1.0).then_inc(made, 1)
            dve.wait_ge(made, 1)
            for c in range(KC):
                dve.tensor_scalar(ln_b_cols[:, c, :], ones[:, :], ln_b[:, c:c + 1], None, ALU.mult).then_inc(made, 1)
            dve.wait_ge(made, 1 + KC)
            dve.sem_inc(const_ready, 1)
            dve.wait_ge(row_ready, 1)
            dve.tensor_tensor(t.bo[:, :], pn[:, 0, 0:D], bo[:, :], ALU.add).then_inc(made, 1)
            for c in range(KC):
                dve.tensor_scalar(wo[:, c, :], wo[:, c, :], ln_g[:, c:c + 1], None, ALU.mult).then_inc(made, 1)
            dve.wait_ge(made, 2 + 2 * KC)
            dve.sem_inc(const_ready, 1)
            chain = Chain(dve, own, 3 + 2 * QT)

            def body(b, par, used):
                chain.start(b)
                dve.wait_ge(mem_copied, b + 1)
                for c in (0, 1):
                    ins = dve.tensor_tensor(M[:, c, :, :], memory[:, par, :, :],
                                            of(khat, b)[:, :, c:c + 1].to_broadcast([P, BQ, 4]), ALU.mult)
                chain.link(ins)
                if not is_first(b):
                    normalize(b - 1)
                dve.wait_ge(pool_products, b + 1)
                after(dve, scaled_ready, b * QT)
                quat_combine(dve, chain, ret, M, True, ret_ready)
                if not is_first(b):
                    for i in range(QT):
                        t.dve(dve, PLAIN_STEPS[i], b - 1, 0, number(b, i))
                for q in range(QT):
                    dve.wait_ge(scaled_ready, b * QT + q + 1)
                    chain.link(dve.bn_stats(st[:, q, :], scaled[:, q, :]))
                    dve.sem_inc(t.passed, 1)
                    chain.link(dve.bn_aggr(mv[:, q, :], st[:, q, :]))
                chain.end()
                dve.tensor_scalar(veps[:, :], mv[:, :, 1], EPS, None, ALU.add).then_inc(var_ready, 1)
                if not is_first(b):
                    t.dve_normalize(dve, b - 1)

            def normalize(b):
                dve.wait_ge(rstd_ready, b + 1)
                for q in range(QT):
                    dve.tensor_scalar(normed[:, q, :], scaled[:, q, :], mv[:, q, 0:1], rstd[:, q:q + 1],
                                      ALU.subtract, ALU.mult).then_inc(normed_ready, 1)
                dve.wait_ge(normed_ready, b * QT + QT)
            over_batches(dve, body)
            normalize(B - 1)
            for i, step in enumerate(PLAIN_STEPS[:QT]):
                t.dve(dve, step, B - 1, 0, number(B, i))
            t.dve_normalize(dve, B - 1)

        @block.gpsimd
        def _(pool):
            t.begin(pool)
            def body(b, par, used):
                pool.wait_ge(mem_copied, b + 1)
                after(pool, ret_ready, b)
                for c in (2, 3):
                    ins = pool.tensor_tensor(M[:, c, :, :], memory[:, par, :, :],
                                             of(khat, b)[:, :, c:c + 1].to_broadcast([P, BQ, 4]), ALU.mult)
                ins.then_inc(pool_products, 1)
                if not is_first(b):
                    t.pool_keep(pool, b - 1)
                pool.wait_ge(var_ready, b + 1)
                after(pool, normed_ready, b * QT)
                pool.tensor_tensor(rstd[:, :], veps[:, :], g.halfneg[:, :], ALU.pow).then_inc(rstd_ready, 1)
            over_batches(pool, body)
            t.pool_keep(pool, B - 1)
            t.finish(pool)


def context_attention(nc, g, d, xT_in, xT_out):
    GROUPS = [range(k, min(k + 4, KT)) for k in range(0, KT, 4)]
    slots = [[("ct", -1, 2), ("q", 1, 0)],
             [("ct", -1, 3), ("q", 1, 1)],
             [("ct", 0, 0)] + [("out", -1, q) for q in range(QT)],
             [("ct", 0, 1)] + [("turn", -1, q) for q in range(QT)]]
    EPILOGUE = [("ct", -1, 2), ("ct", -1, 3)] + \
               [("out", -1, q) for q in range(QT)] + [("turn", -1, q) for q in range(QT)]
    per_batch = sum(len(s) for s in slots)
    AHEAD = KC
    in_first = sum(rel >= 0 for s in slots for _, rel, _ in s)

    def is_first(b):
        return isinstance(b, int) and b == 0

    def plan(b):
        first, last = is_first(b), isinstance(b, int) and b == B - 1
        n = AHEAD if first else AHEAD + in_first + (b - 1) * per_batch
        out, i = [], 0
        for slot in slots:
            row = []
            for step in slot:
                if not (first and step[1] < 0) and not (last and step[1] > 0):
                    i += 1
                    row.append((step, n + i))
            out.append(row)
        return out

    after_last = AHEAD + in_first + (B - 2) * per_batch + per_batch - AHEAD
    with ExitStack() as ctx:
        sem, mem = Sems(nc, ctx, "cx"), Mem(nc, ctx, "cx")
        mixT = mem.sb("mixT", [P, 2, KC, S])
        wqk, wvo = mem.sb("wqk", [P, KC, D]), mem.sb("wvo", [P, KC, D])
        t = Tail(nc, ctx, g, sem, mem, d, "L1_xattn_bo", xT_out,
                 terms=lambda par, k: [(mixT[:, par, c, k * P:(k + 1) * P], wvo[:, c, :]) for c in range(KC)])
        wq, wk, wv, wo = (mem.sb(n, [P, KC, D]) for n in ("wq", "wk", "wv", "wo"))
        bq, bv, bqk = mem.sb("bq", [P, KC]), mem.sb("bv", [P, KC]), mem.sb("bqk", [P, KC])
        bv_cols = mem.sb("bv_cols", [P, KC, P])
        xT, cT = mem.sb("xT", [P, 2, KC, S]), mem.sb("cT", [P, 2, KC, C])
        cn = mem.sb("cn", [P, 2, KT, D])
        qk = mem.sb("qk", [P, 2, KC, S])
        probs, pT = mem.sb("probs", [P, 2, C]), mem.sb("pT", [P, KT, P])
        negmax, den, inv = mem.sb("negmax", [P, 2]), mem.sb("den", [P, 2]), mem.sb("inv", [P, 2])
        mixed = mem.sb("mixed", [P, 2, D])
        pS = mem.ps("pS", [P, 2048])
        pt = [mem.ps(f"pt{k}", [P, 512]) for k in range(2)]
        pO = mem.ps("pO", [P, 512])
        c_loaded, w_ready = sem("wc_loaded"), sem("w_ready")
        cols_ready, folded = sem("cols_ready"), sem("folded")
        x_loaded, k_loaded = sem("x_loaded", 2), sem("k_loaded", 2)
        scored, max_ready, exped, inv_ready, turned, copied_even, copied_odd, summed, mixed_ready = (
            sem(n) for n in ("scored", "max_ready", "exped", "inv_ready", "turned", "copied_even", "copied_odd",
                             "summed", "mixed_ready"))
        block = ctx.enter_context(nc.Block())
        NG = len(GROUPS)

        @block.sync
        def _(sp):
            for w, n in ((wq, "Wq"), (wk, "Wk"), (wv, "Wv"), (wo, "WoT")):
                sp.dma_start(w[:, :, :], w_in(d["L1_xattn_" + n])).then_inc(c_loaded, 16)
            for v, n in ((bq, "bq"), (bv, "bv")):
                sp.dma_start(v[:, :], d["L1_xattn_" + n].rearrange("(c p) -> p c", p=P), allow_slow_non_contiguous=True).then_inc(c_loaded, 16)
            t.load(sp)

            def load_x(b, par):
                sp.dma_start(xT[:, par, :, :], w_in(xT_in)[:, :, bass.ds(b * S + HALO, S)]).then_inc(x_loaded[par], 16)

            def load(b, par):
                sp.dma_start(cT[:, par, :, :], w_in(d["cT"])[:, :, bass.ds(b * C, C)]).then_inc(k_loaded[par], 16)
                full = (KT - 1) * P
                rows = d["ctx"]
                sp.dma_start(cn[:, par, 0:KT - 1, :], rows[bass.ds(b * C, full), :].rearrange("(t p) n -> p t n", p=P))\
                  .then_inc(k_loaded[par], 16)
                sp.dma_start(cn[0:KLAST, par, KT - 1, :], rows[bass.ds(b * C + full, KLAST), :]).then_inc(k_loaded[par], 16)
            load_x(0, 0)
            load(0, 0)

            def body(b, par, used):
                if not (isinstance(b, int) and b == B - 1):
                    after(sp, summed, (b - 1) * QT + 1)
                    load_x(b + 1, 1 - par)
                    after(sp, summed, b * QT)
                    load(b + 1, 1 - par)
            over_batches(sp, body)

        def misc_pe(pe, step, b, par, n):
            what, rel, k = step
            own = par if rel == 0 else 1 - par
            if what in ("out", "turn"):
                return t.pe(pe, (what, k), b + rel, own, n)
            t.wait_freed(pe, n - 1)
            if what == "q":
                if k == 0:
                    pe.wait_ge(x_loaded[own], x_count(b, par) * 16)
                for c in range(KC):
                    mm = pe.matmul(t.misc[:, :], wqk[:, c, k * P:(k + 1) * P], xT[:, own, c, :], start=(c == 0), stop=(c == KC - 1))
            else:
                pe.wait_ge(mixed_ready, (b + rel) * QT + k + 1)
                for c in range(KC):
                    mm = pe.transpose(t.misc[:, c * P:(c + 1) * P], mixed[:, k % 2, c * P:(c + 1) * P], g.ident[:, :])
            mm.then_inc(t.misc_done, 1)

        used_of = {}

        def x_count(b, par):
            return used_of["used"] + 1 + par

        def misc_act(act, step, b, par, n):
            what, rel, k = step
            if what in ("out", "turn"):
                return t.act(act, (what, k), b + rel, n)
            own = par if rel == 0 else 1 - par
            act.wait_ge(t.misc_done, n)
            if what == "q":
                ins = act.activation(qk[:, own, k, :], t.misc[:, :], ACT.Identity, bias=bqk[:, k:k + 1])
            else:
                ins = act.activation(mixT[:, own, :, k * P:(k + 1) * P], t.misc[:, 0:D].rearrange("p (c t) -> p c t", c=KC), ACT.Copy)
            ins.then_inc(t.freed, 1)

        def scores(pe, b, par, q):
            after(pe, exped, b * QT + q)
            if q == 0:
                pe.wait_ge(k_loaded[par], used_of["used"] * 48 + 48)
                if is_first(b):
                    t.wait_freed(pe, AHEAD)
            for at in range(0, C, 512):
                w = min(512, C - at)
                for c in range(KC):
                    mm = pe.matmul(pS[:, at:at + w], qk[:, par, c, q * P:(q + 1) * P], cT[:, par, c, at:at + w],
                                   start=(c == 0), stop=(c == KC - 1))
            mm.then_inc(scored, 1)

        def turn(pe, b, q, gi):
            unit = b * QT + q
            if gi == 0:
                pe.wait_ge(exped, unit + 1)
            after(pe, copied_odd if gi % 2 else copied_even, unit * 2 + gi // 2)
            for i, kt in enumerate(GROUPS[gi]):
                w = P if kt < KT - 1 else KLAST
                mm = pe.transpose(pt[gi % 2][0:w, i * P:(i + 1) * P], probs[:, q % 2, kt * P:kt * P + w], g.ident[:, :])
            mm.then_inc(turned, 1)

        def sum_up(pe, b, par, q):
            unit = b * QT + q
            after(pe, mixed_ready, unit)
            for gi, tiles in enumerate(GROUPS):
                pe.wait_ge(copied_odd if gi % 2 else copied_even, unit * 2 + gi // 2 + 1)
                for kt in tiles:
                    m = P if kt < KT - 1 else KLAST
                    mm = pe.matmul(pO[:, 0:D], pT[0:m, kt, :], cn[0:m, par, kt, :], start=(kt == 0), stop=(kt == KT - 1))
            mm.then_inc(summed, 1)

        def before(b, par, q):
            return (b, par, q - 1) if q else (b - 1, 1 - par, QT - 1)

        @block.tensor
        def _(pe):
            pe.wait_ge(cols_ready, 1)
            for e in range(KC):
                flags = dict(start=(e == 0), stop=(e == KC - 1))
                pe.matmul(pS[:, 1536:1536 + D], bv_cols[:, e, :], wo[:, e, :], **flags)
            for c in range(KC):
                rows = slice(c * P, (c + 1) * P)
                for to, left, right in ((0, wq, wk), (512, wv, wo)):
                    for e in range(KC):
                        pe.matmul(pS[:, to + c * D:to + (c + 1) * D], left[:, e, rows], right[:, e, :],
                                  start=(e == 0), stop=(e == KC - 1))
                for e in range(KC):
                    mm = pe.matmul(pS[:, 1024 + c:1025 + c], wk[:, e, rows], bq[:, e:e + 1],
                                   start=(e == 0), stop=(e == KC - 1))
            mm.then_inc(folded, 1)
            pe.wait_ge(w_ready, 1)
            used_of["used"] = 0
            pe.wait_ge(x_loaded[0], 16)
            for k in range(KC):
                t.wait_freed(pe, k)
                for c in range(KC):
                    mm = pe.matmul(t.misc[:, :], wqk[:, c, k * P:(k + 1) * P], xT[:, 0, c, :], start=(c == 0), stop=(c == KC - 1))
                mm.then_inc(t.misc_done, 1)

            def finish_unit(b, par, q, steps, run):
                todo = list(steps)

                def one():
                    if todo:
                        step, n = todo.pop(0)
                        misc_pe(pe, step, run[0], run[1], n)
                one()
                turn(pe, b, q, 0)
                turn(pe, b, q, 1)
                one()
                turn(pe, b, q, 2)
                turn(pe, b, q, 3)
                one()
                sum_up(pe, b, par, q)
                while todo:
                    one()

            def body(b, par, used):
                used_of["used"] = used
                for q, steps in enumerate(plan(b)):
                    scores(pe, b, par, q)
                    if is_first(b) and q == 0:
                        for step, n in steps:
                            misc_pe(pe, step, b, par, n)
                    else:
                        finish_unit(*before(b, par, q), steps, (b, par))
            over_batches(pe, body)
            finish_unit(B - 1, 1, QT - 1, [], None)
            for k, step in enumerate(EPILOGUE):
                misc_pe(pe, step, B, 0, after_last + k + 1)

        @block.scalar
        def _(act):
            act.wait_ge(w_ready, 1)
            for k in range(KC):
                misc_act(act, ("q", 0, k), 0, 0, k + 1)

            def copy(b, q, gi):
                unit = b * QT + q
                act.wait_ge(turned, unit * NG + gi + 1)
                tiles = GROUPS[gi]
                act.activation(pT[:, tiles[0]:tiles[-1] + 1, :], pt[gi % 2][:, 0:len(tiles) * P]
                               .rearrange("p (t n) -> p t n", n=P), ACT.Copy).then_inc(copied_even, 1)

            def exp(b, q):
                unit = b * QT + q
                act.wait_ge(max_ready, unit + 1)
                after(act, turned, (unit - 1) * NG)
                act.activation(probs[:, q % 2, :], pS[:, 0:C], ACT.Exp, bias=negmax[:, q % 2:q % 2 + 1],
                               accum_out=den[:, q % 2:q % 2 + 1]).then_inc(exped, 1)

            def mix(b, q):
                unit = b * QT + q
                act.wait_ge(summed, unit + 1)
                act.wait_ge(inv_ready, unit + 1)
                act.activation(mixed[:, q % 2, :], pO[:, 0:D], ACT.Copy, scale=inv[:, q % 2:q % 2 + 1])\
                   .then_inc(mixed_ready, 1)

            def finish_unit(b, q, steps, run, scores_of=None):
                todo = list(steps)

                def one():
                    if todo:
                        step, n = todo.pop(0)
                        misc_act(act, step, run[0], run[1], n)
                one()
                copy(b, q, 0)
                one()
                copy(b, q, 2)
                if scores_of:
                    exp(*scores_of)
                one()
                mix(b, q)
                while todo:
                    one()

            def body(b, par, used):
                for q, steps in enumerate(plan(b)):
                    if is_first(b) and q == 0:
                        exp(b, q)
                        for step, n in steps:
                            misc_act(act, step, b, par, n)
                    else:
                        pb, _, pq = before(b, par, q)
                        finish_unit(pb, pq, steps, (b, par), (b, q))
            over_batches(act, body)
            finish_unit(B - 1, QT - 1, [], None)
            for k, step in enumerate(EPILOGUE):
                misc_act(act, step, B, 0, after_last + k + 1)

        @block.vector
        def _(dve):
            dve.wait_ge(c_loaded, 96)
            t.wait_loaded(dve)
            made = sem("made")
            dve.memset(bv_cols[:, :, :], 1.0).then_inc(made, 1)
            dve.wait_ge(made, 1)
            for c in range(KC):
                dve.tensor_scalar(bv_cols[:, c, :], bv_cols[:, c, :], bv[:, c:c + 1], None, ALU.mult).then_inc(made, 1)
            dve.wait_ge(made, 1 + KC)
            dve.sem_inc(cols_ready, 1)
            dve.wait_ge(folded, 1)
            dve.tensor_scalar(wqk[:, :, :].rearrange("p c n -> p (c n)"), pS[:, 0:KC * D], D ** -0.5, None, ALU.mult).then_inc(made, 1)
            dve.tensor_scalar(bqk[:, :], pS[:, 1024:1024 + KC], D ** -0.5, None, ALU.mult).then_inc(made, 1)
            dve.tensor_copy(wvo[:, :, :].rearrange("p c n -> p (c n)"), pS[:, 512:512 + KC * D]).then_inc(made, 1)
            dve.tensor_tensor(t.bo[:, :], t.bo[:, :], pS[:, 1536:1536 + D], ALU.add).then_inc(made, 1)
            dve.wait_ge(made, 5 + KC)
            dve.sem_inc(w_ready, 1)

            def maximum(b, q):
                unit = b * QT + q
                dve.wait_ge(scored, unit + 1)
                after(dve, exped, unit - 1)
                dve.tensor_reduce(negmax[:, q % 2:q % 2 + 1], pS[:, 0:C], AX.X, ALU.max, negate=True).then_inc(max_ready, 1)

            def inverse(b, q):
                unit = b * QT + q
                dve.wait_ge(exped, unit + 1)
                after(dve, mixed_ready, unit - 1)
                dve.reciprocal(inv[:, q % 2:q % 2 + 1], den[:, q % 2:q % 2 + 1]).then_inc(inv_ready, 1)

            def copy(b, q, gi):
                unit = b * QT + q
                dve.wait_ge(turned, unit * NG + gi + 1)
                tiles = GROUPS[gi]
                m = KLAST if tiles[-1] == KT - 1 else P
                assert m == P or len(tiles) == 1
                dve.tensor_copy(pT[0:m, tiles[0]:tiles[-1] + 1, :], pt[gi % 2][0:m, 0:len(tiles) * P]
                                .rearrange("p (t n) -> p t n", n=P)).then_inc(copied_odd, 1)

            def misc_dve(step, b, n):
                what, rel, k = step
                if what in ("out", "turn"):
                    t.dve(dve, (what, k), b + rel, 0, n)

            def finish_unit(b, q, steps, run, scores_of=None, normalize=None):
                inverse(b, q)
                if scores_of:
                    maximum(*scores_of)
                if normalize is not None:
                    t.dve_normalize(dve, normalize)
                todo = list(steps)

                def one():
                    if todo:
                        step, n = todo.pop(0)
                        misc_dve(step, run, n)
                one()
                copy(b, q, 1)
                one()
                copy(b, q, 3)
                while todo:
                    one()

            def body(b, par, used):
                for q, steps in enumerate(plan(b)):
                    if is_first(b) and q == 0:
                        maximum(b, q)
                        for step, n in steps:
                            misc_dve(step, b, n)
                    else:
                        pb, _, pq = before(b, par, q)
                        finish_unit(pb, pq, steps, b, (b, q), b - 1 if q == QT - 1 and not is_first(b) else None)
            over_batches(dve, body)
            finish_unit(B - 1, QT - 1, [], None)
            for k, step in enumerate(EPILOGUE):
                misc_dve(step, B, after_last + k + 1)
                if step == ("out", -1, QT - 1):
                    t.dve_normalize(dve, B - 1)

        @block.gpsimd
        def _(pool):
            t.begin(pool)
            with pool.Fori(0, B - 1) as b:
                t.pool(pool, b, AHEAD + in_first + b * per_batch + per_batch)
            t.pool(pool, B - 1, after_last + len(EPILOGUE))
            t.finish(pool)


INNER = 704
IT = -(-INNER // P)
ILAST = INNER - (IT - 1) * P
QMAX = 127.0
ROUND = 1.5 * 2.0 ** 23


def quantize_shifted(dve, link, src, tmp, inv):
    link(dve.tensor_scalar(tmp, src, inv, -QMAX - 1, ALU.mult, ALU.max))
    return dve.tensor_scalar(tmp, tmp, QMAX, ROUND, ALU.min, ALU.add)


def quantize(dve, link, out, src, tmp, inv):
    link(quantize_shifted(dve, link, src, tmp, inv))
    return dve.tensor_scalar(out, tmp, ROUND, None, ALU.subtract)


def quantized_ffn(nc, g, d, xT_in, out):
    with ExitStack() as outer:
        keep = Mem(nc, outer, "fk")
        wgu = keep.sb("wgu", [P, KC, 2, INNER], BF16)
        wd = keep.sb("wd", [P, IT, D], BF16)
        col = keep.sb("col", [P, 2, IT])
        down_row = keep.sb("down_row", [P, D])
        hid = keep.sb("hid", [P, IT, T])
        peak = keep.sb("peak", [P, IT, B])
        inv_x, inv_h = keep.sb("inv_x", [P, 1]), keep.sb("inv_h", [P, 1])
        sig = keep.sb("sig", [P, 2])

        with ExitStack() as ctx:
            sem, mem = Sems(nc, ctx, "fw"), Mem(nc, ctx, "fw")
            raw = mem.sb("raw", [P, 2, IT, D])
            raw_d = mem.sb("raw_d", [P, KC, INNER])
            tmp, tmp_d = mem.sb("tmp", [P, 2, IT, D]), mem.sb("tmp_d", [P, KC, INNER])
            qw, qd = mem.sb("qw", [P, 2, IT, D], BF16), mem.sb("qd", [P, KC, INNER], BF16)
            scale, inv = mem.sb("scale", [P, 2 * IT + KC]), mem.sb("inv", [P, 2 * IT + KC])
            diag, ones = mem.sb("diag", [P, KC, P]), mem.sb("ones", [P, P])
            clip, xmax = mem.sb("clip", [P, 2]), mem.sb("xmax", [P, 1])
            xall, sx = mem.sb("xall", [P, 1]), mem.sb("sx", [P, 1])
            bank = [mem.ps(f"bank{k}", [P, 1024], BF16) for k in range(2)]
            row = mem.ps("row", [P, 512])
            loaded, chain, x_peak, x_all = sem("loaded"), sem("chain"), sem("x_peak"), sem("x_all")
            quantized, diag_ready, turned, emptied, row_done, sig_ready = (
                sem(n) for n in ("quantized", "diag_ready", "turned", "emptied", "row_done", "sig_ready"))
            block = ctx.enter_context(nc.Block())
            squares = [(qw[:, s, it, c * P:(c + 1) * P], P, wgu[:, c, s, it * P:it * P + P], P)
                       if it < IT - 1 else
                       (qw[0:ILAST, s, it, c * P:(c + 1) * P], ILAST, wgu[:, c, s, it * P:it * P + ILAST], P)
                       for s in range(2) for it in range(IT) for c in range(KC)]
            squares += [(qd[:, c, it * P:min((it + 1) * P, INNER)], P, wd[0:min(P, INNER - it * P), it, c * P:(c + 1) * P],
                         min(P, INNER - it * P)) for it in range(IT) for c in range(KC)]

            @block.sync
            def _(sp):
                full = (IT - 1) * P
                for s, n in enumerate(("gate", "up")):
                    w = d["L1_ffn_w_" + n]
                    sp.dma_start(raw[:, s, 0:IT - 1, :], w[0:full, :].rearrange("(t p) n -> p t n", p=P)).then_inc(loaded, 16)
                    sp.dma_start(raw[0:ILAST, s, IT - 1, :], w[full:INNER, :]).then_inc(loaded, 16)
                sp.dma_start(raw_d[:, :, :], d["L1_ffn_w_down"].rearrange("(c p) n -> p c n", p=P)).then_inc(loaded, 16)
                for k, n in enumerate(("clip_x", "clip_down")):
                    sp.dma_start(clip[:, k:k + 1], d["L1_ffn_" + n].rearrange("(a n) -> a n", a=1).to_broadcast([P, 1]),
                                 allow_slow_non_contiguous=True).then_inc(loaded, 16)

            @block.gpsimd
            def _(pool):
                pool.wait_ge(x_peak, 1)
                pool.partition_all_reduce(xall[:, :], xmax[:, :], P, bass.bass_isa.ReduceOp.max).then_inc(x_all, 1)

            @block.scalar
            def _(act):
                act.wait_ge(loaded, 112)
                act.activation(sig[:, :], clip[:, :], ACT.Sigmoid).then_inc(sig_ready, 1)

            @block.vector
            def _(dve):
                n = [0]

                def link(ins):
                    n[0] += 1
                    ins.then_inc(chain, 1)
                    dve.wait_ge(chain, n[0])
                dve.tensor_reduce(xmax[:, :], g.x[:, :, :].rearrange("p t n -> p (t n)"), AX.X, ALU.max,
                                  apply_absolute_value=True).then_inc(x_peak, 1)
                link(dve.memset(raw[ILAST:P, :, IT - 1, :], 0.0))
                link(dve.memset(ones[:, :], 1.0))
                dve.wait_ge(loaded, 112)
                link(dve.tensor_reduce(scale[:, 0:2 * IT].rearrange("p (s t) -> p s t", s=2), raw[:, :, :, :], AX.X,
                                       ALU.max, apply_absolute_value=True))
                link(dve.tensor_reduce(scale[:, 2 * IT:], raw_d[:, :, :], AX.X, ALU.max, apply_absolute_value=True))
                link(dve.memset(scale[ILAST:P, IT - 1:2 * IT:IT], 1.0))
                link(dve.tensor_scalar(scale[:, :], scale[:, :], 1 / QMAX, None, ALU.mult))
                link(dve.reciprocal(inv[:, :], scale[:, :]))
                for s in range(2):
                    for it in range(IT):
                        k = s * IT + it
                        link(quantize(dve, link, qw[:, s, it, :], raw[:, s, it, :], tmp[:, s, it, :], inv[:, k:k + 1]))
                for c in range(KC):
                    k = 2 * IT + c
                    link(quantize(dve, link, qd[:, c, :], raw_d[:, c, :], tmp_d[:, c, :], inv[:, k:k + 1]))
                    link(dve.tensor_scalar(diag[:, c, :], g.ident[:, :], scale[:, k:k + 1], None, ALU.mult))
                dve.sem_inc(quantized, 1)
                for i, (_, _, to, m) in enumerate(squares):
                    if i % 8 == 0:
                        dve.wait_ge(turned, min(i + 8, len(squares)))
                    w = to.shape[-1]
                    ins = dve.tensor_copy(to, bank[i // 8 % 2][0:m, i % 8 * P:i % 8 * P + w])
                    ins.then_inc(emptied, 1)
                dve.wait_ge(row_done, 1)
                link(dve.tensor_copy(down_row[:, :], row[:, 0:D]))
                dve.wait_ge(x_all, 1)
                dve.wait_ge(sig_ready, 1)
                link(dve.scalar_tensor_tensor(out=sx[:, :], in0=xall[:, :], scalar=sig[:, 0:1], in1=ones[:, 0:1],
                                              op0=ALU.mult, op1=ALU.mult))
                link(dve.tensor_scalar(sx[:, :], sx[:, :], 1 / QMAX, None, ALU.mult))
                link(dve.reciprocal(inv_x[:, :], sx[:, :]))
                link(dve.tensor_scalar(col[:, :, :], scale[:, 0:2 * IT].rearrange("p (s t) -> p s t", s=2), sx[:, 0:1],
                                       None, ALU.mult))

            @block.tensor
            def _(pe):
                pe.wait_ge(quantized, 1)
                for i, (src, m, to, _) in enumerate(squares):
                    if i >= 16:
                        pe.wait_ge(emptied, (i // 8 - 1) * 8)
                    w = src.shape[-1]
                    pe.transpose(bank[i // 8 % 2][0:w, i % 8 * P:i % 8 * P + m], src, g.identb[0:m, 0:m]).then_inc(turned, 1)
                for c in range(KC):
                    mm = pe.matmul(row[:, c * P:(c + 1) * P], ones[:, :], diag[:, c, :], start=True, stop=True)
                mm.then_inc(row_done, 1)

        with ExitStack() as ctx:
            sem, mem = Sems(nc, ctx, "fu"), Mem(nc, ctx, "fu")
            xT, xs, xq = mem.sb("xT", [P, 2, KC, S]), mem.sb("xs", [P, KC, S]), mem.sb("xq", [P, 2, KC, S], BF16)
            sg = mem.sb("sg", [P, 2, S])
            pg = [mem.ps(f"pg{k}", [P, 512]) for k in range(2)]
            pu = [mem.ps(f"pu{k}", [P, 512]) for k in range(2)]
            x_loaded, own = sem("x_loaded", 2), sem("own")
            xq_ready, gate_done, up_done, silu_ready, hid_ready, peaked = (
                sem(n) for n in ("xq_ready", "gate_done", "up_done", "silu_ready", "hid_ready", "peaked"))
            block = ctx.enter_context(nc.Block())

            @block.sync
            def _(sp):
                def body(b, par, used):
                    after(sp, xq_ready, b)
                    sp.dma_start(xT[:, par, :, :], w_in(xT_in)[:, :, bass.ds(b * S + HALO, S)]).then_inc(x_loaded[par], 16)
                over_batches(sp, body)

            @block.tensor
            def _(pe):
                def body(b, par, used):
                    pe.wait_ge(xq_ready, b + 1)
                    for it in range(IT):
                        n = b * IT + it
                        m = P if it < IT - 1 else ILAST
                        for s, bank, free, done in ((0, pg, silu_ready, gate_done), (1, pu, hid_ready, up_done)):
                            after(pe, free, n - 1)
                            for c in range(KC):
                                mm = pe.matmul(bank[it % 2][0:m, :], wgu[:, c, s, it * P:it * P + m], xq[:, par, c, :],
                                               start=(c == 0), stop=(c == KC - 1))
                            mm.then_inc(done, 1)
                over_batches(pe, body)

            @block.scalar
            def _(act):
                def body(b, par, used):
                    for it in range(IT):
                        n = b * IT + it
                        m = P if it < IT - 1 else ILAST
                        act.wait_ge(gate_done, n + 1)
                        after(act, hid_ready, n - 1)
                        act.activation(sg[0:m, it % 2, :], pg[it % 2][0:m, :], ACT.Silu, scale=col[0:m, 0, it:it + 1])\
                           .then_inc(silu_ready, 1)
                over_batches(act, body)

            @block.vector
            def _(dve):
                dve.memset(peak[:, :, :], 0.0).then_inc(peaked, 1)
                chain = Chain(dve, own, 2)

                def quantize_x(b, par, used):
                    chain.start(b)
                    dve.wait_ge(x_loaded[par], used * 16 + 16)
                    after(dve, up_done, (b - 1) * IT)
                    after(dve, xq_ready, b)
                    quantize(dve, chain.link, xq[:, par, :, :], xT[:, par, :, :], xs[:, :, :], inv_x[:, 0:1])\
                        .then_inc(xq_ready, 1)
                    chain.end()
                quantize_x(0, 0, 0)
                dve.wait_ge(peaked, 1)

                def body(b, par, used):
                    for it in range(IT):
                        n = b * IT + it
                        m = P if it < IT - 1 else ILAST
                        dve.wait_ge(up_done, n + 1)
                        dve.wait_ge(silu_ready, n + 1)
                        to = hid[0:m, it, bass.ds(b * S, S)]
                        dve.scalar_tensor_tensor(out=to, in0=pu[it % 2][0:m, :], scalar=col[0:m, 1, it:it + 1],
                                                 in1=sg[0:m, it % 2, :], op0=ALU.mult, op1=ALU.mult).then_inc(hid_ready, 1)
                        if it == 2 and not (isinstance(b, int) and b == B - 1):
                            quantize_x(b + 1, 1 - par, used + par)
                        dve.wait_ge(hid_ready, n + 1)
                        dve.tensor_reduce(peak[0:m, it, bass.ds(b, 1)], to, AX.X, ALU.max,
                                          apply_absolute_value=True).then_inc(peaked, 1)
                over_batches(dve, body)

        with ExitStack() as ctx:
            sem, mem = Sems(nc, ctx, "fd"), Mem(nc, ctx, "fd")
            hq, hs = mem.sb("hq", [P, 2, IT, S], BF16), mem.sb("hs", [P, IT, S])

            def out_terms(par, k):
                return [(hq[0:P if it < IT - 1 else ILAST, par, it, k * P:(k + 1) * P],
                         wd[0:P if it < IT - 1 else ILAST, it, :]) for it in range(IT)]
            t = Tail(nc, ctx, g, sem, mem, d, None, None, terms=out_terms, row=down_row[:, :], final=out)
            hmax, hall, sh = mem.sb("hmax", [P, 1]), mem.sb("hall", [P, 1]), mem.sb("sh", [P, 1])
            h_peak, h_all, own, hq_ready, first = sem("h_peak"), sem("h_all"), sem("own"), sem("hq_ready"), sem("first")
            minus_round, hs_ready = mem.sb("minus_round", [P, 1]), sem("hs_ready")
            block = ctx.enter_context(nc.Block())

            def is_first(b):
                return isinstance(b, int) and b == 0

            @block.tensor
            def _(pe):
                def body(b, par, used):
                    if not is_first(b):
                        pe.wait_ge(hq_ready, b * IT)
                        for q in range(QT):
                            t.pe(pe, ("out", q), b - 1, 1 - par, (b - 1) * QT + q + 1)
                over_batches(pe, body)
                pe.wait_ge(hq_ready, B * IT)
                for q in range(QT):
                    t.pe(pe, ("out", q), B - 1, 1, (B - 1) * QT + q + 1)

            @block.gpsimd
            def _(pool):
                t.begin(pool)
                pool.wait_ge(h_peak, 1)
                pool.partition_all_reduce(hall[:, :], hmax[:, :], P, bass.bass_isa.ReduceOp.max).then_inc(h_all, 1)
                with pool.Fori(0, B) as b:
                    t.pool(pool, b, 0)
                t.finish(pool)

            @block.scalar
            def _(act):
                def body(b, par, used):
                    t.wait_freed(act, 0 if is_first(b) else (b - 1) * QT)
                    for it in range(IT):
                        m = P if it < IT - 1 else ILAST
                        act.wait_ge(hs_ready, b * IT + it + 1)
                        act.activation(hq[0:m, par, it, :], hs[0:m, it, :], ACT.Identity, bias=minus_round[0:m, :])\
                           .then_inc(hq_ready, 1)
                over_batches(act, body)

            @block.vector
            def _(dve):
                n = [0]

                def link(ins):
                    n[0] += 1
                    ins.then_inc(first, 1)
                    dve.wait_ge(first, n[0])
                dve.tensor_reduce(hmax[:, :], peak[:, :, :].rearrange("p a b -> p (a b)"), AX.X, ALU.max).then_inc(h_peak, 1)
                dve.wait_ge(h_all, 1)
                link(dve.tensor_tensor(sh[:, :], hall[:, :], sig[:, 1:2], ALU.mult))
                link(dve.tensor_scalar(sh[:, :], sh[:, :], 1 / QMAX, None, ALU.mult))
                link(dve.reciprocal(inv_h[:, :], sh[:, :]))
                link(dve.tensor_scalar(down_row[:, :], down_row[:, :], sh[:, 0:1], None, ALU.mult))
                link(dve.memset(minus_round[:, :], -ROUND))
                chain = Chain(dve, own, IT)

                def body(b, par, used):
                    chain.start(b)
                    for it in range(IT):
                        m = P if it < IT - 1 else ILAST
                        after(dve, hq_ready, (b - 1) * IT + it + 1)
                        quantize_shifted(dve, chain.link, hid[0:m, it, bass.ds(b * S, S)], hs[0:m, it, :],
                                         inv_h[0:m, 0:1]).then_inc(hs_ready, 1)
                    chain.end()
                    if not is_first(b):
                        for q in range(QT):
                            t.dve(dve, ("out", q), b - 1, 0, (b - 1) * QT + q + 1)
                        t.dve_normalize(dve, b - 1)
                over_batches(dve, body)
                for q in range(QT):
                    t.dve(dve, ("out", q), B - 1, 0, (B - 1) * QT + q + 1)
                t.dve_normalize(dve, B - 1)


def decoder(nc, d, out):
    with ExitStack() as ctx:
        g = Bag()
        g.x = ctx.enter_context(nc.sbuf_tensor("x_tokens", [P, B * QT, D], F32))
        g.ident = ctx.enter_context(nc.sbuf_tensor("ident", [P, P], F32))
        g.identb = ctx.enter_context(nc.sbuf_tensor("identb", [P, P], BF16))
        g.halfneg = ctx.enter_context(nc.sbuf_tensor("minus_half", [P, QT], F32))
        def scratch(name, shape, dt=F32):
            return nc.dram_tensor(name, shape, dt, kind="Internal").ap()
        q_parts, k_parts = (scratch(n, [3, D, PADT], BF16) for n in ("q_parts", "k_parts"))
        qx_parts, kx_parts = scratch("qx_parts", [3, D, T], BF16), scratch("kx_parts", [3, D, CTX], BF16)
        vx = scratch("vx", [CTX, D])
        gT = scratch("gT", [NE, T])
        xT = [scratch(f"xT{k}", [D, PADT]) for k in range(5)]
        load_all(nc, g, d)
        project_split(nc, "p0", d["xT"], PADT // 10, 10,
                      [(d["L0_attn_WqT"], None, DK ** -0.5, q_parts), (d["L0_attn_WkT"], None, 1.0, k_parts)])
        window_attention(nc, g, d, q_parts, k_parts, xT[0])
        project_split(nc, "p1", xT[0][:, HALO:HALO + T], S, T // S,
                      [(d["L0_xattn_WqT"], d["L0_xattn_bq"], DK ** -0.5, qx_parts)])
        project_split(nc, "p2", d["cT"], CCH, CTX // CCH, [(d["L0_xattn_WkT"], d["L0_xattn_bk"], 1.0, kx_parts)])
        project_v(nc, d, vx)
        cross_attention(nc, g, d, qx_parts, kx_parts, vx, xT[1])
        gates(nc, g, d, xT[1], gT)
        experts(nc, g, d, xT[1], gT, xT[2])
        with ExitStack() as held:
            khat = held.enter_context(nc.sbuf_tensor("khat", [P, B * BQ, 4], F32))
            bound = held.enter_context(nc.sbuf_tensor("bound", [P, B * BQ, 4], F32))
            bind(nc, d, xT[2], khat, bound)
            retrieve(nc, g, d, khat, bound, xT[3])
        context_attention(nc, g, d, xT[3], xT[4])
        quantized_ffn(nc, g, d, xT[4], out)


class Bag:
    pass


def layout(inputs):
    f = np.float32
    a = {k: np.ascontiguousarray(v) for k, v in inputs.items()}
    o = {"x": a["x"]}
    xT = np.zeros((D, PADT), f)
    xT[:, HALO:HALO + T] = a["x"].reshape(T, D).T
    o["xT"] = xT
    cT = np.zeros((D, CTX), f)
    cT[:, :B * C] = a["ctx_1024"].reshape(B * C, D).T
    o["cT"] = cT
    for n in ("L0_xattn_bq", "L0_xattn_bk", "L0_xattn_bv", "L0_xattn_bo"):
        o[n] = a[n]
    for n in ("L0_attn_Wq", "L0_attn_Wk", "L0_attn_Wv", "L0_xattn_Wq", "L0_xattn_Wk", "L0_xattn_Wv"):
        o[n + "T"] = np.ascontiguousarray(a[n].T)
    for n in ("L0_attn", "L0_xattn"):
        w = np.zeros((H, 2 * DK, D), f)
        w[:, :DK] = a[n + "_Wo"].T.reshape(H, DK, D)
        o[n + "_WoP"] = w.reshape(2 * D, D)
    o["ident"] = np.eye(P, dtype=f)
    r, j = np.arange(P)[:, None], np.arange(WIN)[None]
    mask = np.zeros((P, 3, WIN), f)
    for e in range(3):
        seen = (j >= r) & (j <= r + 2 * HALO)
        if e == 0:
            seen &= j >= HALO
        if e == 2:
            seen &= j < P + HALO
        mask[:, e] = np.where(seen, 0, NEG)
    o["mask"] = mask
    q, k = np.arange(S) + HALO, np.arange(BW)
    o["pos_q"] = np.stack([q * 0] * MAXR + [q // P * P] * 3 + [q % P] * 3 + [q * 0 + 1] * 6).astype(f)
    o["pos_k"] = np.stack([k * 0 + 1] * (MAXR + 6) + [-(k // P * P)] * 3 + [-(k % P)] * 3).astype(f)
    pick = np.zeros((POSR, 2, 4), f)
    pick[:MAXR, :, 0] = 1
    for i in range(POSR - MAXR):
        pick[MAXR + i, 0 if i >= 6 else 1, 1 + i % 3] = 1
        pick[MAXR + i, 1 if i >= 6 else 0, 0] = 1
    o["pick"] = pick
    o["slopes"] = np.repeat(a["L0_attn_slopes"][None], POSR, 0)
    for n in ("W1", "W2", "W3", "b1", "b2", "b3", "Wg", "bg", "Wf", "bf"):
        o["L0_ffn_" + n] = a["L0_ffn_" + n]
    e = np.arange(NE)
    o["tri"] = np.repeat((e[None, None, :] > e[None, :, None]).astype(f), P, 0)
    for n in ("bk", "bv", "ln_g", "ln_b", "bo"):
        o["L1_attn_" + n] = a["L1_attn_" + n]
    for n in ("bq", "bv", "bo", "Wq", "Wk", "Wv"):
        o["L1_xattn_" + n] = a["L1_xattn_" + n]
    for n in ("L1_attn_Wk", "L1_attn_Wv", "L1_attn_Wo", "L1_xattn_Wo"):
        o[n + "T"] = np.ascontiguousarray(a[n].T)
    for n in ("clip_x", "clip_down", "w_gate", "w_up", "w_down"):
        o["L1_ffn_" + n] = a["L1_ffn_" + n]
    o["ctx"] = a["ctx_1024"].reshape(B * C, D)
    i = np.arange(P)
    o["upper"] = (i[:, None] <= i[None, :]).astype(f)
    o["root"] = (1 / np.sqrt(np.arange(1, S + 1, dtype=f))).reshape(QT, P).T.copy()
    return o


def kernel(**inputs):
    import concourse.bacc as bacc
    from concourse.bass_utils import run_bass_kernel_spmd

    nc = bacc.Bacc("TRN2", target_bir_lowering=False, num_devices=1)
    arrays = {"in_" + name: np.ascontiguousarray(a) for name, a in layout(inputs).items()}
    d = {name[3:]: nc.dram_tensor(name, a.shape, mybir.dt.from_np(a.dtype), kind="ExternalInput").ap()
         for name, a in arrays.items()}
    out = nc.dram_tensor("out", (B, S, D), F32, kind="ExternalOutput").ap()
    decoder(nc, d, out)
    return run_bass_kernel_spmd(nc, [arrays], core_ids=[0]).results[0]["out"]
```
